# Optimizing a Trainium2 kernel written in Bass

```python
import numpy as np
import jax
import jax.numpy as jnp

def _softmax(x, axis=-1):
    return jax.nn.softmax(x, axis=axis)

def _gelu(x):
    return jax.nn.gelu(x, approximate=True)

def _silu(x):
    return jax.nn.silu(x)

def _sigmoid(x):
    return jax.nn.sigmoid(x)

def _layernorm(x, axis=-1, eps=1e-05):
    m = jnp.mean(x, axis=axis, keepdims=True)
    v = jnp.var(x, axis=axis, keepdims=True)
    return (x - m) / jnp.sqrt(v + eps)

def _scatter_add(tgt, idx, src, axis=0):
    return tgt.at[idx].add(src)

def _segment_sum(src, seg, n):
    return jax.ops.segment_sum(src, seg, n)
kernel_name = 'mk_gnn_resnorm_d4_gnn_r16_9cfaff'

def setup_inputs(seed: int=0):
    np.random.seed(seed)
    _w = jnp.asarray

    def _rec_inputs():
        import jax
        import jax.numpy as jnp
        _gk = jax.random.key(seed)
        x = -0.0002117 + 1 * jax.random.normal(jax.random.fold_in(_gk, 1), (3125, 256), jnp.float32)
        _s = jax.random.randint(jax.random.fold_in(_gk, 2), (50000,), 0, 3125, jnp.int32)
        _d = jax.random.randint(jax.random.fold_in(_gk, 3), (50000,), 0, 3125, jnp.int32)
        _loop = jnp.arange(3125, dtype=jnp.int32)
        src = jnp.concatenate([_s, _d, _loop])
        dst = jnp.concatenate([_d, _s, _loop])
        _o = jnp.argsort(dst, stable=True)
        src = src[_o]
        dst = dst[_o]
        edge_attr_2 = jax.random.uniform(jax.random.fold_in(_gk, 12), (103125, 2), jnp.float32, 0.0, 1)
        edge_type_16 = jax.random.randint(jax.random.fold_in(_gk, 14), (103125,), 0, 16, jnp.int32)
        return (x, src, dst, edge_attr_2, edge_type_16)
    x, src, dst, edge_attr_2, edge_type_16 = _rec_inputs()

    def _L0_gnn_setup():
        import jax, jax.numpy as jnp
        import numpy as np
        N_NODES = 6250
        N_EDGES = 100000
        IN_FEATS = 256
        OUT_FEATS = 64
        NUM_HEADS = 4
        key = jax.random.key(seed)
        k_h, k_adj, k_dir, k_wf, k_wr, k_af = jax.random.split(key, 6)
        h = jax.random.normal(k_h, (N_NODES, IN_FEATS), dtype=jnp.float32)
        adj = jax.random.randint(k_adj, (2, N_EDGES), 0, N_NODES, dtype=jnp.int64)
        bit = jax.random.randint(k_dir, (N_EDGES,), 0, 2).astype(jnp.float32)
        direction = jnp.stack([bit, 1.0 - bit], axis=1)
        s_w = float(np.sqrt(6.0 / (IN_FEATS + OUT_FEATS)))
        s_a = float(np.sqrt(6.0 / (NUM_HEADS + OUT_FEATS)))
        W_forward = jax.random.uniform(k_wf, (OUT_FEATS, IN_FEATS), jnp.float32, -s_w, s_w)
        W_reverse = jax.random.uniform(k_wr, (OUT_FEATS, IN_FEATS), jnp.float32, -s_w, s_w)
        attn_forward = jax.random.uniform(k_af, (1, NUM_HEADS, OUT_FEATS), jnp.float32, -s_a, s_a)
        return {'h': h, 'adj': adj, 'direction': direction, 'W_forward': W_forward, 'W_reverse': W_reverse, 'attn_forward': attn_forward}
    _L0_gnn_all = _L0_gnn_setup()
    _L0_gnn_in = {k: v for k, v in _L0_gnn_all.items() if k in ('W_forward', 'W_reverse', 'attn_forward')}
    del _L0_gnn_all

    def _L1_gnn_setup():
        import jax, jax.numpy as jnp
        import numpy as np
        N = 6250
        E = 100000
        IN_FEATS = 256
        OUT_FEATS = 256
        MAXK = 32

        def _maxk(x, k):
            _, idx = jax.lax.top_k(x, k)
            rows = jnp.arange(x.shape[0])[:, None]
            mask = jnp.zeros_like(x).at[rows, idx].set(1.0)
            return x * mask
        key = jax.random.key(seed)
        k1, k2, k3, k4, k5 = jax.random.split(key, 5)
        feat = jax.random.normal(k1, (N, IN_FEATS), dtype=jnp.float32)
        W_self = jax.random.normal(k2, (IN_FEATS, OUT_FEATS), dtype=jnp.float32) * (1.0 / np.sqrt(IN_FEATS))
        W_neigh = jax.random.normal(k3, (IN_FEATS, OUT_FEATS), dtype=jnp.float32) * (1.0 / np.sqrt(IN_FEATS))
        src = jax.random.randint(k4, (E,), 0, N, dtype=jnp.int64)
        dst = jax.random.randint(k5, (E,), 0, N, dtype=jnp.int64)
        return {'feat': feat, 'W_self': W_self, 'W_neigh': W_neigh, 'src': src, 'dst': dst}
    _L1_gnn_all = _L1_gnn_setup()
    _L1_gnn_in = {k: v for k, v in _L1_gnn_all.items() if k in ('W_self', 'W_neigh')}
    del _L1_gnn_all

    def _L2_gnn_setup():
        import jax, jax.numpy as jnp
        import numpy as np
        from jax.ops import segment_sum
        N_NODES = 625
        N_EDGES = 10000
        IN_FEAT = 256
        OUT_FEAT = 256
        NUM_RELS = 16

        def _inv_degree(idx, n):
            deg = segment_sum(jnp.ones(idx.shape[0], dtype=jnp.float32), idx, num_segments=n)
            return jnp.where(deg > 0, 1.0 / deg, 0.0)

        def _typed_pass(feat, W, bias, src_idx, dst_idx, etypes, norm_per_edge, n):
            proj = jnp.einsum('ni,rio->rno', feat, W)
            m = proj[etypes, src_idx] + bias
            m = m * norm_per_edge[:, None]
            return segment_sum(m, dst_idx, num_segments=n)
        key = jax.random.key(seed)
        ks = jax.random.split(key, 8)
        feat = jax.random.normal(ks[0], (N_NODES, IN_FEAT), dtype=jnp.float32)
        Wf = jax.random.normal(ks[1], (NUM_RELS, IN_FEAT, OUT_FEAT), dtype=jnp.float32)
        Wb = jax.random.normal(ks[2], (NUM_RELS, IN_FEAT, OUT_FEAT), dtype=jnp.float32)
        loop_weight = jax.random.normal(ks[3], (IN_FEAT, OUT_FEAT), dtype=jnp.float32)
        forward_bias = jnp.zeros((OUT_FEAT,), dtype=jnp.float32)
        backward_bias = jnp.zeros((OUT_FEAT,), dtype=jnp.float32)
        self_bias = jnp.zeros((OUT_FEAT,), dtype=jnp.float32)
        src = jax.random.randint(ks[4], (N_EDGES,), 0, N_NODES, dtype=jnp.int32)
        dst = jax.random.randint(ks[5], (N_EDGES,), 0, N_NODES, dtype=jnp.int32)
        etypes = jax.random.randint(ks[6], (N_EDGES,), 0, NUM_RELS, dtype=jnp.int32)
        return {'feat': feat, 'Wf': Wf, 'Wb': Wb, 'loop_weight': loop_weight, 'forward_bias': forward_bias, 'backward_bias': backward_bias, 'self_bias': self_bias, 'src': src, 'dst': dst, 'etypes': etypes, 'use_dis_weight': 0, 'drop_out': 0}
    _L2_gnn_all = _L2_gnn_setup()
    _L2_gnn_in = {k: v for k, v in _L2_gnn_all.items() if k in ('Wf', 'Wb', 'loop_weight', 'forward_bias', 'backward_bias', 'self_bias')}
    del _L2_gnn_all

    def _L3_gnn_setup():
        import jax, jax.numpy as jnp
        import numpy as np
        HEAD = 8
        D = 128
        GIN = 256
        GOUT = 256
        N = 3125
        E = 50000

        def gt_layer(edge_index, embeds, qT, kT, vT, ln_s, ln_b):
            rows, cols = (edge_index[0], edge_index[1])
            n, d = embeds.shape
            hd = d // HEAD
            rowE = embeds[rows]
            colE = embeds[cols]
            q = (rowE @ qT).reshape(-1, HEAD, hd)
            k = (colE @ kT).reshape(-1, HEAD, hd)
            v = (colE @ vT).reshape(-1, HEAD, hd)
            att = jnp.clip(jnp.einsum('ehd,ehd->eh', q, k), -10.0, 10.0)
            expAtt = jnp.exp(att)
            attNorm = jax.ops.segment_sum(expAtt, rows, num_segments=n)[rows]
            att = expAtt / (attNorm + 1e-08)
            res = (att[..., None] * v).reshape(-1, d)
            agg = jax.ops.segment_sum(res, rows, num_segments=n)
            out = agg + embeds
            mu = jnp.mean(out, axis=-1, keepdims=True)
            var = jnp.mean((out - mu) ** 2, axis=-1, keepdims=True)
            return (out - mu) / jnp.sqrt(var + 1e-06) * ln_s + ln_b
        key = jax.random.key(seed)
        ks = jax.random.split(key, 16)

        def xavier(k, shape):
            lim = np.sqrt(6.0 / (shape[0] + shape[1]))
            return jax.random.uniform(k, shape, jnp.float32, -lim, lim)
        inp = {'x': jax.random.normal(ks[0], (N, GIN), jnp.float32), 'edge_index': jax.random.randint(ks[1], (2, E), 0, N, jnp.int64), 'W_P_w': xavier(ks[2], (GIN, D)), 'W_P_b': jnp.zeros((D,), jnp.float32), 'W_pos': jax.random.uniform(ks[3], (1, D), jnp.float32, -0.02, 0.02), 'q1': xavier(ks[4], (D, D)), 'k1': xavier(ks[5], (D, D)), 'v1': xavier(ks[6], (D, D)), 'ln1_s': jnp.ones((D,), jnp.float32), 'ln1_b': jnp.zeros((D,), jnp.float32), 'q2': xavier(ks[7], (D, D)), 'k2': xavier(ks[8], (D, D)), 'v2': xavier(ks[9], (D, D)), 'ln2_s': jnp.ones((D,), jnp.float32), 'ln2_b': jnp.zeros((D,), jnp.float32), 'inv_w': xavier(ks[10], (D, GOUT)), 'inv_b': jnp.zeros((GOUT,), jnp.float32)}
        return inp
    _L3_gnn_all = _L3_gnn_setup()
    _L3_gnn_in = {k: v for k, v in _L3_gnn_all.items() if k in ('W_P_w', 'W_P_b', 'W_pos', 'q1', 'k1', 'v1', 'ln1_s', 'ln1_b', 'q2', 'k2', 'v2', 'ln2_s', 'ln2_b', 'inv_w', 'inv_b')}
    del _L3_gnn_all
    return {'x': x, 'src': src, 'dst': dst, 'edge_attr_2': edge_attr_2, 'edge_type_16': edge_type_16, 'L0_gnn_W_forward': _L0_gnn_in['W_forward'], 'L0_gnn_W_reverse': _L0_gnn_in['W_reverse'], 'L0_gnn_attn_forward': _L0_gnn_in['attn_forward'], 'L1_gnn_W_self': _L1_gnn_in['W_self'], 'L1_gnn_W_neigh': _L1_gnn_in['W_neigh'], 'L2_gnn_Wf': _L2_gnn_in['Wf'], 'L2_gnn_Wb': _L2_gnn_in['Wb'], 'L2_gnn_loop_weight': _L2_gnn_in['loop_weight'], 'L2_gnn_forward_bias': _L2_gnn_in['forward_bias'], 'L2_gnn_backward_bias': _L2_gnn_in['backward_bias'], 'L2_gnn_self_bias': _L2_gnn_in['self_bias'], 'L3_gnn_W_P_w': _L3_gnn_in['W_P_w'], 'L3_gnn_W_P_b': _L3_gnn_in['W_P_b'], 'L3_gnn_W_pos': _L3_gnn_in['W_pos'], 'L3_gnn_q1': _L3_gnn_in['q1'], 'L3_gnn_k1': _L3_gnn_in['k1'], 'L3_gnn_v1': _L3_gnn_in['v1'], 'L3_gnn_ln1_s': _L3_gnn_in['ln1_s'], 'L3_gnn_ln1_b': _L3_gnn_in['ln1_b'], 'L3_gnn_q2': _L3_gnn_in['q2'], 'L3_gnn_k2': _L3_gnn_in['k2'], 'L3_gnn_v2': _L3_gnn_in['v2'], 'L3_gnn_ln2_s': _L3_gnn_in['ln2_s'], 'L3_gnn_ln2_b': _L3_gnn_in['ln2_b'], 'L3_gnn_inv_w': _L3_gnn_in['inv_w'], 'L3_gnn_inv_b': _L3_gnn_in['inv_b']}

def reference(x, src, dst, edge_attr_2, edge_type_16, L0_gnn_W_forward, L0_gnn_W_reverse, L0_gnn_attn_forward, L1_gnn_W_self, L1_gnn_W_neigh, L2_gnn_Wf, L2_gnn_Wb, L2_gnn_loop_weight, L2_gnn_forward_bias, L2_gnn_backward_bias, L2_gnn_self_bias, L3_gnn_W_P_w, L3_gnn_W_P_b, L3_gnn_W_pos, L3_gnn_q1, L3_gnn_k1, L3_gnn_v1, L3_gnn_ln1_s, L3_gnn_ln1_b, L3_gnn_q2, L3_gnn_k2, L3_gnn_v2, L3_gnn_ln2_s, L3_gnn_ln2_b, L3_gnn_inv_w, L3_gnn_inv_b):
    import jax
    import jax.numpy as jnp

    def _L0_gnn_ref(h, adj, direction, W_forward, W_reverse, attn_forward):
        import jax, jax.numpy as jnp
        import numpy as np
        N_NODES = 6250
        N_EDGES = 100000
        IN_FEATS = 256
        OUT_FEATS = 64
        NUM_HEADS = 4
        N = h.shape[0]
        H = attn_forward.shape[1]
        h_fwd = h @ W_forward.T
        h_rev = h @ W_reverse.T
        src, dst = (adj[0], adj[1])
        messages = h_fwd[src] * direction[:, 0:1] + h_rev[src] * direction[:, 1:2]
        scores = jnp.einsum('ef,hf->eh', messages, attn_forward[0])
        scores = jax.nn.leaky_relu(scores, negative_slope=0.2)
        exp_scores = jnp.exp(scores - scores.max(axis=0, keepdims=True))
        sum_exp = jax.ops.segment_sum(exp_scores, dst, num_segments=N)
        norm = exp_scores / (sum_exp[dst] + 1e-10)
        outs = [jax.ops.segment_sum(messages * norm[:, hd:hd + 1], dst, num_segments=N) for hd in range(H)]
        out = jnp.stack(outs, axis=1)
        return out.reshape(N, -1)

    def _L1_gnn_ref(feat, W_self, W_neigh, src, dst):
        import jax, jax.numpy as jnp
        import numpy as np
        N = 6250
        E = 100000
        IN_FEATS = 256
        OUT_FEATS = 256
        MAXK = 32

        def _maxk(x, k):
            _, idx = jax.lax.top_k(x, k)
            rows = jnp.arange(x.shape[0])[:, None]
            mask = jnp.zeros_like(x).at[rows, idx].set(1.0)
            return x * mask
        n = feat.shape[0]
        h_self = feat @ W_self
        h_neigh = feat @ W_neigh
        h_sparse = _maxk(h_neigh, MAXK)
        msg = h_sparse[src]
        summed = jax.ops.segment_sum(msg, dst, num_segments=n)
        deg = jax.ops.segment_sum(jnp.ones((src.shape[0],), dtype=feat.dtype), dst, num_segments=n)
        neigh = summed / jnp.maximum(deg, 1.0)[:, None]
        return h_self + neigh

    def _L2_gnn_ref(feat, Wf, Wb, loop_weight, forward_bias, backward_bias, self_bias, src, dst, etypes, use_dis_weight, drop_out):
        import jax, jax.numpy as jnp
        import numpy as np
        from jax.ops import segment_sum
        N_NODES = 625
        N_EDGES = 10000
        IN_FEAT = 256
        OUT_FEAT = 256
        NUM_RELS = 16

        def _inv_degree(idx, n):
            deg = segment_sum(jnp.ones(idx.shape[0], dtype=jnp.float32), idx, num_segments=n)
            return jnp.where(deg > 0, 1.0 / deg, 0.0)

        def _typed_pass(feat, W, bias, src_idx, dst_idx, etypes, norm_per_edge, n):
            proj = jnp.einsum('ni,rio->rno', feat, W)
            m = proj[etypes, src_idx] + bias
            m = m * norm_per_edge[:, None]
            return segment_sum(m, dst_idx, num_segments=n)
        n = feat.shape[0]
        norm_f = _inv_degree(dst, n)[dst]
        m_forward = _typed_pass(feat, Wf, forward_bias, src, dst, etypes, norm_f, n)
        norm_b = _inv_degree(src, n)[src]
        m_backward = _typed_pass(feat, Wb, backward_bias, dst, src, etypes, norm_b, n)
        s = feat @ loop_weight
        s = s + s + self_bias
        return s + m_forward + m_backward

    def _L3_gnn_ref(x, edge_index, W_P_w, W_P_b, W_pos, q1, k1, v1, ln1_s, ln1_b, q2, k2, v2, ln2_s, ln2_b, inv_w, inv_b):
        import jax, jax.numpy as jnp
        import numpy as np
        HEAD = 8
        D = 128
        GIN = 256
        GOUT = 256
        N = 3125
        E = 50000

        def gt_layer(edge_index, embeds, qT, kT, vT, ln_s, ln_b):
            rows, cols = (edge_index[0], edge_index[1])
            n, d = embeds.shape
            hd = d // HEAD
            rowE = embeds[rows]
            colE = embeds[cols]
            q = (rowE @ qT).reshape(-1, HEAD, hd)
            k = (colE @ kT).reshape(-1, HEAD, hd)
            v = (colE @ vT).reshape(-1, HEAD, hd)
            att = jnp.clip(jnp.einsum('ehd,ehd->eh', q, k), -10.0, 10.0)
            expAtt = jnp.exp(att)
            attNorm = jax.ops.segment_sum(expAtt, rows, num_segments=n)[rows]
            att = expAtt / (attNorm + 1e-08)
            res = (att[..., None] * v).reshape(-1, d)
            agg = jax.ops.segment_sum(res, rows, num_segments=n)
            out = agg + embeds
            mu = jnp.mean(out, axis=-1, keepdims=True)
            var = jnp.mean((out - mu) ** 2, axis=-1, keepdims=True)
            return (out - mu) / jnp.sqrt(var + 1e-06) * ln_s + ln_b
        z = x @ W_P_w + W_P_b
        embeds = z + W_pos
        embeds = gt_layer(edge_index, embeds, q1, k1, v1, ln1_s, ln1_b)
        embeds = gt_layer(edge_index, embeds, q2, k2, v2, ln2_s, ln2_b)
        return embeds @ inv_w + inv_b
    edge_index = jnp.stack([src, dst])
    x = _layernorm(x + _L0_gnn_ref(x, edge_index, edge_attr_2, L0_gnn_W_forward, L0_gnn_W_reverse, L0_gnn_attn_forward), axis=-1)
    x = _layernorm(x + _L1_gnn_ref(x, L1_gnn_W_self, L1_gnn_W_neigh, src, dst), axis=-1)
    x = _layernorm(x + _L2_gnn_ref(x, L2_gnn_Wf, L2_gnn_Wb, L2_gnn_loop_weight, L2_gnn_forward_bias, L2_gnn_backward_bias, L2_gnn_self_bias, src, dst, edge_type_16, 0, 0), axis=-1)
    x = _layernorm(x + _L3_gnn_ref(x, edge_index, L3_gnn_W_P_w, L3_gnn_W_P_b, L3_gnn_W_pos, L3_gnn_q1, L3_gnn_k1, L3_gnn_v1, L3_gnn_ln1_s, L3_gnn_ln1_b, L3_gnn_q2, L3_gnn_k2, L3_gnn_v2, L3_gnn_ln2_s, L3_gnn_ln2_b, L3_gnn_inv_w, L3_gnn_inv_b), axis=-1)
    return x

_drawn_inputs = setup_inputs


def setup_inputs(seed=0):
    import zlib

    import numpy as np

    out = dict(_drawn_inputs(seed))
    spreads = {'L2_gnn_forward_bias': (0.0, 0.8),
     'L2_gnn_backward_bias': (0.0, 0.8),
     'L2_gnn_self_bias': (0.0, 0.8),
     'L3_gnn_W_P_b': (0.0, 0.1),
     'L3_gnn_ln1_s': (1.0, 0.2),
     'L3_gnn_ln1_b': (0.0, 0.1),
     'L3_gnn_ln2_s': (1.0, 0.2),
     'L3_gnn_ln2_b': (0.0, 0.1),
     'L3_gnn_inv_b': (0.0, 0.1)}
    factors = {'L3_gnn_W_pos': 3.162}
    for name, (base, spread) in spreads.items():
        noise = np.random.default_rng([zlib.crc32(name.encode()), seed]).standard_normal(out[name].shape)
        drawn = base * np.exp(spread * noise) if base else spread * noise
        out[name] = jnp.asarray(drawn.astype(out[name].dtype))
    for name, factor in factors.items():
        out[name] = (out[name] * factor).astype(out[name].dtype)
    return out
```

```python
from contextlib import ExitStack

import concourse.bass as bass
from concourse import mybir


def gnn_program(nc, x, src, dst, etype, attr, wf, wr, wft, wrt, attnt, w_self, w_neigh, rel_f, rel_b, loop_w,
                bias_f, bias_b, bias_self, wp, wp_b, w_pos, q1, k1, v1, ln1_s, ln1_b, q2, k2, v2, ln2_s, ln2_b,
                inv_w, inv_b, out, layers=4):
    f32, i32 = mybir.dt.float32, mybir.dt.int32
    ALU, ACT, AX = mybir.AluOpType, mybir.ActivationFunctionType, mybir.AxisListType
    P = 128
    N, C = 3125, 256
    NP = x.shape[0]
    NB = NP // P
    EP = src.shape[0]
    EC = EP // P
    BINS = NB + 1
    G = 4
    R = 4
    T = -(-(EC + NB) // (G * R)) * G * R
    NG = T // G
    TP = T + 1
    HEADS, F0 = 4, 64
    ROW0 = F0 + HEADS
    MAXK = 32
    RELS = rel_f.shape[0]
    D, H3 = 128, 8
    HD = D // H3
    W3 = D + H3
    SC_EDGES = 13
    KD, KS = 5, 3
    LOWEST = -3.4028234663852886e38

    ctx = ExitStack()
    with ctx:
        def sb(name, shape, dt=f32):
            return ctx.enter_context(nc.sbuf_tensor(name, shape, dt))

        def dram(name, shape):
            return nc.dram_tensor(name, shape, f32).ap()

        sems = {}

        def sem(name):
            if name not in sems:
                sems[name] = ctx.enter_context(nc.semaphore(name))
            return sems[name]

        def after(eng, name, value):
            if not (isinstance(value, int) and value <= 0):
                eng.wait_ge(sem(name), value)

        def groups(eng, body, first=0):
            for n in range(R):
                body(n, n % R)
            with eng.Fori(R, NG - 2 * R + 1, R) as n0:
                for h in range(R):
                    body(n0 + h, h)
            for n in range(NG - R, NG):
                body(n, n % R)

        x_sb = sb("x_sb", [P, NB * C])
        slots_d = sb("slots_d", [P, TP * KD])
        slots_s = sb("slots_s", [P, TP * KS])
        block_d = sb("block_d", [1, T], i32)
        block_s = sb("block_s", [1, T], i32)
        gidx = sb("gidx", [P, R, G], i32)
        rows = sb("rows", [P, R * G, 264])
        onehot = sb("onehot", [P, R, G, P])
        msg = sb("msg", [P, R * G * 264])
        acc = sb("acc", [P, 6600])
        big1 = sb("big1", [P, NB * C])
        big2 = sb("big2", [P, NB * C])
        wring = sb("wring", [P, 2, 2, 512])
        xs = sb("xs", [P, 5, 256])
        xts = sb("xts", [P, 5, 256])
        bias = sb("bias", [P, 2, 256])
        iota_i = sb("iota_i", [P, P], i32)
        iota = sb("iota", [P, P])
        ident = sb("ident", [P, P])
        ones = sb("ones", [P, P])
        tri = sb("tri", [P, P])
        cnt = sb("cnt", [P, 32])
        base = sb("base", [P, 32])
        tiles_i = sb("tiles_i", [P, 32], i32)
        tiles_f = sb("tiles_f", [P, 32])
        incl = sb("incl", [P, 32])
        tend = sb("tend", [P, 4])
        tend_i = sb("tend_i", [P, 1], i32)
        stage = sb("stage", [P, 2, SC_EDGES * KD])
        stage_row = sb("stage_row", [P, 2, SC_EDGES], i32)
        small = sb("small", [P, 3 * 104])
        top8 = sb("top8", [P, 4, 8])
        att = sb("att", [P, 3, G * H3])
        wa = sb("wa", [P, 64])
        ps = ctx.enter_context(nc.psum_tensor("ps", [P, 8, 512], f32))

        slots_d_dram = dram("slots_d_dram", [P * TP, KD])
        slots_s_dram = dram("slots_s_dram", [P * TP, KS])
        table0 = dram("table0", [NP, 2 * ROW0])
        mslots = dram("mslots", [P, T * ROW0])
        table1 = dram("table1", [NP, C])
        table2f = dram("table2f", [RELS * NP, C])
        table2b = dram("table2b", [RELS * NP, C])
        table3 = [dram("table3a", [NP, 2 * D]), dram("table3b", [NP, 2 * D])]

        x3 = x_sb[:, :].rearrange("p (b c) -> p b c", c=C)
        sd3 = slots_d[:, :].rearrange("p (t w) -> p t w", w=KD)
        ss3 = slots_s[:, :].rearrange("p (t w) -> p t w", w=KS)
        key_i = acc[:, 0:EC].bitcast(i32)
        kb_i = acc[:, EC:2 * EC].bitcast(i32)
        kbf = acc[:, 2 * EC:3 * EC]
        mask = acc[:, 3 * EC:4 * EC]
        scan = acc[:, 4 * EC:5 * EC]
        prod = acc[:, 5 * EC:6 * EC]
        rank = acc[:, 6 * EC:7 * EC]
        other_i = acc[:, 3 * EC:4 * EC].bitcast(i32)
        etype_i = acc[:, 4 * EC:5 * EC].bitcast(i32)
        pos_i = acc[:, 3 * EC:4 * EC].bitcast(i32)
        posc_i = acc[:, 4 * EC:5 * EC].bitcast(i32)
        attr_sb = rows[:, :, :].rearrange("p a b -> p (a b)")[:, 0:2 * EC]
        rec_d = big2[:, 0:EC * KD]
        row_d = big2[:, EC * KD:EC * (KD + 1)].bitcast(i32)
        rec_s = big1[:, 0:EC * KS]
        row_s = big1[:, EC * KS:EC * (KS + 1)].bitcast(i32)
        iota_t_i = msg[0:32, 0:T].bitcast(i32)
        iota_t = msg[0:32, T:2 * T]
        tile_ge = msg[0:32, 2 * T:3 * T]
        scores = big2[:, 0:T * HEADS]
        sc3 = scores.rearrange("p (t h) -> p t h", h=HEADS)
        pen = big2[:, T * HEADS:T * (HEADS + 1)]
        msgA = msg[:, :].rearrange("p (r g w) -> p r g w", r=R, g=G)
        ms0 = msg[:, 0:R * G * ROW0].rearrange("p (r g w) -> p r g w", r=R, g=G)
        lin0 = msg[:, R * G * ROW0:2 * R * G * ROW0].rearrange("p (r g w) -> p r g w", r=R, g=G)
        res3 = msg[:, 0:R * G * W3].rearrange("p (r g w) -> p r g w", r=R, g=G)
        oneT = msg[:, R * G * W3:R * G * (W3 + P)].rearrange("p (r g w) -> p r g w", r=R, g=G)
        qk3 = big1[:, 0:R * G * D].rearrange("p (r g w) -> p r g w", r=R, g=G)
        rows4 = rows[:, :, :].rearrange("p (r g) w -> p r g w", g=G)
        emb = big2[:, 0:NB * D]
        q_sb = acc[:, NB * W3:NB * (W3 + D)]
        tab = big2[:, NB * D:NB * D + 5 * 512]
        tab0 = rows[:, :, :].rearrange("p a b -> p (a b)")[:, 2 * EC:2 * EC + 5 * 2 * ROW0]
        xt_all = big1[:, :].rearrange("p (k n) -> p k n", k=2)
        projtab = big2[:, 0:2 * 5 * 512].rearrange("p (s j w) -> p s j w", s=2, j=5)

        def bc(ap, shape):
            return ap.to_broadcast(shape)

        GATHERS = ["e0", "e1", "e2f", "e2b", "e3a", "e3b"]
        SUMS = ["e0b", "e1", "e2f", "e2b", "e3a", "e3b"]
        gathers0 = {s: NG * n for n, s in enumerate(GATHERS)}
        groups0 = {s: NG * n for n, s in enumerate(SUMS)}
        tiles0 = {s: T * n for n, s in enumerate(SUMS)}

        def gathered(s, n, h):
            return 16 * (NG // R) * GATHERS.index(s) + (16 // R) * (n - h) + 16

        def stage_index(act, s, slots, words, word):
            def body(n, h):
                after(act, "tile_sum", tiles0[s] + G * (n - R + 1))
                src_ap = slots[:, bass.ds(n * (G * words), G * words)].rearrange("p (t w) -> p t w", w=words)
                nc.scalar.activation(gidx[:, h, :], src_ap[:, :, word], ACT.Copy).then_inc(sem("row_numbers"), 1)
            return body

        def gather_loop(pool, s, table, width):
            def body(n, h):
                after(pool, "row_numbers", gathers0[s] + n + 1)
                pool.nop(nofuse=True)
                for k in range(G):
                    j = h * G + k
                    nc.gpsimd.indirect_dma_start(
                        out=rows[:, j, 0:width], out_offset=None, in_=table[:, :],
                        in_offset=bass.IndirectOffsetOnAxis(ap=gidx[:, h, k:k + 1], axis=0),
                    ).then_inc(sem(f"rows_ready{j}"), 16)
            groups(pool, body)

        def one_hot(dve, s, slots, words, n, h):
            loc = slots[:, bass.ds(n * (G * words), G * words)].rearrange("p (t w) -> p t w", w=words)[:, :, 2:3]
            nc.vector.tensor_tensor(onehot[:, h, :, :], bc(iota[:, :].unsqueeze(1), [P, G, P]),
                                    bc(loc, [P, G, P]), ALU.is_equal).then_inc(sem("tile_onehot"), 1)

        def tile_blocks(block, n, engine):
            _, numbers = nc.values_load_multi_w_load_instructions(
                block[0:1, bass.ds(n * G, G)], engines=(engine,), min_val=0, max_val=NB - 1,
                skip_runtime_bounds_check_because="a count of blocks, cut off at NB - 1 when it was made")
            return numbers

        def add_tiles(dve, s, block, n, bank0, width):
            of_tile = tile_blocks(block, n, mybir.EngineType.DVE)
            for k in range(G):
                b = of_tile[k]
                after(dve, "tile_sum", tiles0[s] + n * G + k + 1)
                after(dve, "tile_added", tiles0[s] + n * G + k)
                nc.vector.tensor_tensor(acc[:, bass.ds(b * width, width)], acc[:, bass.ds(b * width, width)],
                                        ps[:, bank0 + k, 0:width], ALU.add).then_inc(sem("tile_added"), 1)

        def sum_tile(pe, s, n, h, k, bank0, width, rhs):
            after(pe, "tile_added", tiles0[s] + n * G + k - G + 1)
            nc.tensor.matmul(ps[:, bank0 + k, 0:width], onehot[:, h, k, :], rhs,
                             start=True, stop=True).then_inc(sem("tile_sum"), 1)

        def sum_act(act, s, slots, words, word):
            groups(act, stage_index(act, s, slots, words, word))

        def sum_pe(pe, s, width):
            def body(n, h):
                after(pe, "tile_onehot", groups0[s] + n + 1)
                for k in range(G):
                    after(pe, f"rows_ready{h * G + k}", gathered(s, n, h))
                    sum_tile(pe, s, n, h, k, 0, width, rows[:, h * G + k, 0:width])
            groups(pe, body)

        def sum_dve(dve, s, slots, words, block, width):
            def body(n, h):
                after(dve, "tile_sum", tiles0[s] + G * (n - R + 1))
                one_hot(dve, s, slots, words, n, h)
                if not isinstance(n, int) or n > 0:
                    add_tiles(dve, s, block, n - 1, 0, width)
            groups(dve, body)
            add_tiles(dve, s, block, NG - 1, 0, width)

        DENSE = {"d0": (x_sb, 256, 2 * ROW0), "d1": (x_sb, 256, 512), "d2": (x_sb, 256, 256),
                 "d3": (x_sb, 256, D), "da": (emb, D, 3 * D), "db": (emb, D, 3 * D), "d4": (emb, D, C)}

        first = {s: NB * n for n, s in enumerate(DENSE)}

        def blocks(eng, body):
            body(0)
            with eng.Fori(1, NB // 5) as it:
                body(it)

        def dense_act(act, s):
            src_sb, width, _ = DENSE[s]

            def body(it):
                for j in range(5):
                    after(act, "block_tr", first[s] + 5 * it + j - 4)
                    nc.scalar.activation(xs[:, j, 0:width], src_sb[:, bass.ds((5 * it + j) * width, width)],
                                         ACT.Copy).then_inc(sem("block_xs"), 1)
                for j in range(5):
                    after(act, "block_out", first[s] + 5 * it + j - 4)
                    if s == "d2":
                        after(act, "d2_xt_all", 5 * it + j - 4)
                    after(act, "block_tr", first[s] + 5 * it + j + 1)
                    nc.scalar.activation(xts[:, j, 0:width], ps[:, j % 2, 0:width], ACT.Copy)\
                        .then_inc(sem("block_xt"), 1)
            blocks(act, body)

        def dense_pe(pe, s, weights):
            _, width, wide = DENSE[s]
            kin = width // P

            def product(it, j):
                after(pe, "block_xt", first[s] + 5 * it + j + 1)
                after(pe, "block_ev", first[s] + 5 * it + j - 4)
                for k in range(kin):
                    last = nc.tensor.matmul(ps[:, 2 + j, 0:wide], xts[:, j, k * P:(k + 1) * P],
                                            weights[:, k, 0:wide], start=(k == 0), stop=(k == kin - 1))
                last.then_inc(sem("block_out"), 1)

            def body(it):
                for j in range(5):
                    after(pe, "block_xs", first[s] + 5 * it + j + 1)
                    after(pe, "block_xt", first[s] + 5 * it + j - (1 if j else 0))
                    for k in range(kin):
                        last = nc.tensor.transpose(ps[:, j % 2, k * P:(k + 1) * P], xs[:, j, k * P:(k + 1) * P],
                                                   ident[:, :])
                    last.then_inc(sem("block_tr"), 1)
                    if j:
                        product(it, j - 1)
                product(it, 4)
            blocks(pe, body)

        def table_store(sp, s, table, width, tab=tab):
            def body(it):
                after(sp, "block_ev", first[s] + 5 * it + 5)
                sp.dma_start(table[bass.ds(it * (5 * P), 5 * P), :].rearrange("(j p) w -> p j w", p=P),
                             tab[:, 0:5 * width].rearrange("p (j w) -> p j w", w=width))\
                    .then_inc(sem(s + "_stored"), 16)
            blocks(sp, body)

        TABLE_STORED = 16 * (NB // 5)

        ORDERS = {"gd": (dst, src, slots_d, KD, rec_d, row_d, block_d), "gs": (src, dst, slots_s, KS, rec_s, row_s, block_s)}

        def sort_dve(dve, o, link):
            _, _, slots, words, rec, rowno, block = ORDERS[o]
            r3 = rec.rearrange("p (f w) -> p f w", w=words)
            dve.wait_ge(sem(o + "_loaded"), 16 * (4 if o == "gd" else 3))
            link(nc.vector.tensor_scalar(kb_i, key_i, 7, None, ALU.logical_shift_right))
            link(nc.vector.tensor_scalar(key_i, key_i, P - 1, None, ALU.bitwise_and))
            nc.vector.tensor_copy(r3[:, :, 2], key_i)
            nc.vector.tensor_copy(r3[:, :, 0], other_i)
            if o == "gd":
                nc.vector.tensor_copy(r3[:, :, 3:5], attr_sb.rearrange("p (f w) -> p f w", w=2))
            nc.vector.scalar_tensor_tensor(r3[:, :, 1], etype_i, float(NP), other_i, ALU.mult, ALU.add)
            link(nc.vector.memset(rank, 0.0))
            link(nc.vector.tensor_copy(kbf, kb_i))
            steps = o + "_rank"
            with dve.Fori(0, BINS) as b:
                this = iota[:, bass.ds(b, 1)]
                nc.vector.tensor_scalar(mask, kbf, this, None, ALU.is_equal).then_inc(sem(steps), 1)
                dve.wait_ge(sem(steps), b * 5 + 1)
                nc.vector.tensor_tensor_scan(scan, mask, mask, 0.0, ALU.add, ALU.max).then_inc(sem(steps), 1)
                dve.wait_ge(sem(steps), b * 5 + 2)
                nc.vector.tensor_copy(cnt[:, bass.ds(b, 1)], scan[:, EC - 1:EC]).then_inc(sem(steps), 1)
                nc.vector.tensor_tensor(prod, mask, scan, ALU.mult).then_inc(sem(steps), 1)
                dve.wait_ge(sem(steps), b * 5 + 4)
                nc.vector.tensor_tensor(rank, rank, prod, ALU.add).then_inc(sem(steps), 1)
                dve.wait_ge(sem(steps), b * 5 + 5)
            nc.vector.tensor_copy(incl[:, 0:1], cnt[:, 0:1]).then_inc(sem(o + "_counted"), 1)
            dve.wait_ge(sem(o + "_totals"), 1)
            for tot, width, ti, tf in ((ps[:, 0, 0:BINS], BINS, tiles_i, tiles_f), (ps[0:BINS, 2, 0:1], 1, tend_i, tend)):
                p = tot.shape[0]
                link(nc.vector.tensor_scalar(tf[0:p, 0:width], tot, float(P - 1), None, ALU.add))
                link(nc.vector.tensor_copy(ti[0:p, 0:width], tf[0:p, 0:width]))
                link(nc.vector.tensor_scalar(ti[0:p, 0:width], ti[0:p, 0:width], 7, None, ALU.logical_shift_right))
                link(nc.vector.tensor_copy(tf[0:p, 0:width], ti[0:p, 0:width]))
            nc.vector.tensor_copy(incl[0:1, 31:32], tend[0:1, 0:1]).then_inc(sem(o + "_tiles"), 1)
            link(nc.vector.tensor_tensor_scan(incl[:, 0:NB], tiles_f[:, 0:NB], tiles_f[:, 0:NB], 0.0, ALU.add, ALU.max))
            link(nc.vector.tensor_tensor(base[:, 0:NB], incl[:, 0:NB], tiles_f[:, 0:NB], ALU.subtract))
            nc.vector.memset(base[:, NB:BINS], float(T))
            link(nc.vector.tensor_scalar(base[:, 0:NB], base[:, 0:NB], float(P), -1.0, ALU.mult, ALU.add))
            link(nc.vector.memset(base[:, NB:BINS], float(T * P - 1)))
            link(nc.vector.tensor_tensor(base[:, 0:BINS], base[:, 0:BINS], ps[:, 1, 0:BINS], ALU.add))
            steps2 = o + "_pos"
            with dve.Fori(0, BINS) as b:
                nc.vector.tensor_scalar(prod, kbf, iota[:, bass.ds(b, 1)], base[:, bass.ds(b, 1)],
                                        ALU.is_equal, ALU.mult).then_inc(sem(steps2), 1)
                dve.wait_ge(sem(steps2), b * 2 + 1)
                nc.vector.tensor_tensor(rank, rank, prod, ALU.add).then_inc(sem(steps2), 1)
                dve.wait_ge(sem(steps2), b * 2 + 2)
            link(nc.vector.tensor_copy(pos_i, rank))
            link(nc.vector.tensor_scalar(posc_i, pos_i, 7, None, ALU.logical_shift_right))
            link(nc.vector.tensor_scalar(pos_i, pos_i, P - 1, None, ALU.bitwise_and))
            nc.vector.scalar_tensor_tensor(rowno, pos_i, float(TP), posc_i, ALU.mult, ALU.add)\
                .then_inc(sem(o + "_rows"), 1)
            dve.wait_ge(sem(o + "_tends"), 1)
            link(nc.vector.tensor_tensor(tend[0:NB, 1:2], tend[0:NB, 0:1], ps[0:NB, 3, 0:1], ALU.add))
            nc.vector.tensor_scalar(tile_ge[0:NB, :], iota_t[0:NB, :], tend[0:NB, 1:2], None, ALU.is_ge)\
                .then_inc(sem(o + "_ge"), 1)
            dve.wait_ge(sem(o + "_blocks"), 1)
            nc.vector.tensor_scalar(block[0:1, 0:T // 2], ps[0:1, 4, 0:T // 2], float(NB - 1), None, ALU.min)
            link(nc.vector.tensor_scalar(block[0:1, T // 2:T], ps[0:1, 5, 0:T // 2], float(NB - 1), None, ALU.min))

        def sort_pe(pe, o):
            pe.wait_ge(sem(o + "_counted"), 1)
            nc.tensor.matmul(ps[:, 0, 0:BINS], ones[:, :], cnt[:, 0:BINS], start=True, stop=True)
            nc.tensor.matmul(ps[:, 1, 0:BINS], tri[:, :], cnt[:, 0:BINS], start=True, stop=True)
            nc.tensor.matmul(ps[0:BINS, 2, 0:1], cnt[:, 0:BINS], ones[:, 0:1], start=True, stop=True)\
                .then_inc(sem(o + "_totals"), 1)
            pe.wait_ge(sem(o + "_tiles"), 1)
            nc.tensor.matmul(ps[0:NB, 3, 0:1], tri[0:NB, 0:NB], tend[0:NB, 0:1], start=True, stop=True)\
                .then_inc(sem(o + "_tends"), 1)
            pe.wait_ge(sem(o + "_ge"), 1)
            for half in range(2):
                last = nc.tensor.matmul(ps[0:1, 4 + half, 0:T // 2], ones[0:NB, 0:1],
                                        tile_ge[0:NB, half * (T // 2):(half + 1) * (T // 2)], start=True, stop=True)
            last.then_inc(sem(o + "_blocks"), 1)

        NS = EC // SC_EDGES

        def scatter(pool, o, dram_slots):
            _, _, _, words, rec, rowno, _ = ORDERS[o]
            pool.wait_ge(sem(o + "_rows"), 1)
            pool.wait_ge(sem(o + "_filled"), 16)

            def body(n, h):
                after(pool, f"{o}_placed{h}", SC_EDGES * 8 * (n - h))
                nc.gpsimd.tensor_copy(stage[:, h, 0:SC_EDGES * words],
                                      rec[:, bass.ds(n * (SC_EDGES * words), SC_EDGES * words)])\
                    .then_inc(sem(o + "_staged"), 1)
                nc.gpsimd.tensor_copy(stage_row[:, h, :], rowno[:, bass.ds(n * SC_EDGES, SC_EDGES)])\
                    .then_inc(sem(o + "_staged"), 1)
                pool.wait_ge(sem(o + "_staged"), 2 * n + 2)
                pool.nop(nofuse=True)
                for k in range(SC_EDGES):
                    nc.gpsimd.indirect_dma_start(
                        out=dram_slots[:, :], out_offset=bass.IndirectOffsetOnAxis(ap=stage_row[:, h, k:k + 1], axis=0),
                        in_=stage[:, h, k * words:(k + 1) * words], in_offset=None,
                    ).then_inc(sem(f"{o}_placed{h}"), 16)
            body(0, 0)
            body(1, 1)
            with pool.Fori(2, NS - 1, 2) as n0:
                body(n0, 0)
                body(n0 + 1, 1)

        def slots_load(sp, o, dram_slots):
            _, _, slots, words, _, _, _ = ORDERS[o]
            for h in range(2):
                sp.wait_ge(sem(f"{o}_placed{h}"), SC_EDGES * 8 * NS)
            sp.dma_start(slots[:, :], dram_slots.rearrange("(p t) w -> p (t w)", p=P)).then_inc(sem(o + "_slots"), 16)

        def norm_act(act, s):
            act.wait_ge(sem(s + "_var"), 1)
            nc.scalar.activation(small[:, 32:32 + NB], small[:, 0:NB], ACT.Sqrt).then_inc(sem(s + "_std"), 1)

        def norm_dve(dve, s, y, width, eps, link, scratch=big1):
            sq = scratch[:, 0:NB * width].rearrange("p (b c) -> p b c", c=width)
            m = small[:, 64:64 + NB]
            link(nc.vector.tensor_reduce(m, y, AX.X, ALU.add))
            link(nc.vector.tensor_scalar(m, m, 1.0 / width, None, ALU.mult))
            link(nc.vector.tensor_tensor(y, y, bc(m.unsqueeze(2), [P, NB, width]), ALU.subtract))
            link(nc.vector.tensor_tensor(sq, y, y, ALU.mult))
            link(nc.vector.tensor_reduce(m, sq, AX.X, ALU.add))
            nc.vector.tensor_scalar(small[:, 0:NB], m, 1.0 / width, eps, ALU.mult, ALU.add).then_inc(sem(s + "_var"), 1)
            dve.wait_ge(sem(s + "_std"), 1)
            link(nc.vector.reciprocal(small[:, 96:96 + NB], small[:, 32:32 + NB]))
            link(nc.vector.tensor_tensor(y, y, bc(small[:, 96:96 + NB].unsqueeze(2), [P, NB, width]), ALU.mult))

        ATTENTIONS = ["e3a", "e3b"]

        def att_groups(eng, step):
            for n in range(R):
                step(n, n, NG - n)
            with eng.Fori(R, NG - 2 * R + 1, R) as n0:
                for h in range(R):
                    step(n0 + h, h, NG)
            for n in range(NG - R, NG):
                step(n, n % R, NG - n)

        def att_act(act, s):
            start = NG * ATTENTIONS.index(s)

            def index(n, h):
                after(act, "att_res", start + n - R + 1)
                of = slots_s[:, bass.ds(n * (G * KS), G * KS)].rearrange("p (t w) -> p t w", w=KS)
                nc.scalar.activation(gidx[:, h, :], of[:, :, 0], ACT.Copy).then_inc(sem("row_numbers"), 1)

            def transposed(n, h):
                after(act, "att_tr", start + n + 1)
                nc.scalar.activation(oneT[:, h, :, :], ps[:, h % 2, :].rearrange("p (g e) -> p g e", g=G), ACT.Copy)\
                    .then_inc(sem("att_oneT"), 1)

            def exponents(n, h):
                after(act, "att_att", start + n + 1)
                after(act, "tile_sum", tiles0[s] + G * (n - R + 1))
                nc.scalar.activation(res3[:, h, :, D:W3], att[:, 1 + h % 2, :].rearrange("p (g a) -> p g a", a=H3),
                                     ACT.Exp).then_inc(sem("att_p"), 1)

            def step(n, h, left):
                if left > 3:
                    index(n + 3, (h + 3) % R)
                exponents(n, h)
                if left > 2:
                    transposed(n + 2, (h + 2) % R)
            for n in range(3):
                index(n, n)
            transposed(0, 0)
            transposed(1, 1)
            att_groups(act, step)

        def att_pe(pe, s):
            start = NG * ATTENTIONS.index(s)

            def transposes(n, h):
                after(pe, "tile_onehot", groups0[s] + n + 1)
                after(pe, "att_oneT", start + n - 1)
                for k in range(G):
                    last = nc.tensor.transpose(ps[:, h % 2, k * P:(k + 1) * P], onehot[:, h, k, :], ident[:, :])
                last.then_inc(sem("att_tr"), 1)

            def queries(n, h):
                after(pe, "att_oneT", start + n + 1)
                after(pe, "att_qk", start + n - 1)
                of_tile = tile_blocks(block_s, n, mybir.EngineType.PE)
                for k in range(G):
                    b = of_tile[k]
                    last = nc.tensor.matmul(ps[:, 2 + h % 2, k * D:(k + 1) * D], oneT[:, h, k, :],
                                            q_sb[:, bass.ds(b * D, D)], start=True, stop=True)
                last.then_inc(sem("att_q"), 1)

            def sums(n, h):
                after(pe, "att_res", start + n + 1)
                for k in range(G):
                    sum_tile(pe, s, n, h, k, 4, W3, res3[:, h, k, :])

            def step(n, h, left):
                if not isinstance(n, int) or n > 1:
                    sums(n - 2, (h - 2) % R)
                if left > 1:
                    queries(n + 1, (h + 1) % R)
                if left > 2:
                    transposes(n + 2, (h + 2) % R)
            transposes(0, 0)
            transposes(1, 1)
            queries(0, 0)
            att_groups(pe, step)
            sums(NG - 2, (NG - 2) % R)
            sums(NG - 1, (NG - 1) % R)

        def att_dve(dve, s):
            start = NG * ATTENTIONS.index(s)

            def scores3(n, h):
                after(dve, "att_q", start + n + 1)
                for k in range(G):
                    after(dve, f"rows_ready{h * G + k}", gathered(s, n, h))
                nc.vector.tensor_tensor(qk3[:, h, :, :], ps[:, 2 + h % 2, :].rearrange("p (g d) -> p g d", d=D),
                                        rows4[:, h, :, 0:D], ALU.mult).then_inc(sem("att_qk"), 1)
                dve.wait_ge(sem("att_qk"), start + n + 1)
                nc.vector.tensor_reduce(att[:, 0, :], qk3[:, h, :, :].rearrange("p g (a d) -> p (g a) d", d=HD),
                                        AX.X, ALU.add).then_inc(sem("att_red"), 1)
                dve.wait_ge(sem("att_red"), start + n + 1)
                after(dve, "att_p", start + n - 1)
                nc.vector.tensor_scalar(att[:, 1 + h % 2, :], att[:, 0, :], 10.0, -10.0, ALU.min, ALU.max)\
                    .then_inc(sem("att_att"), 1)

            def weighted(n, h):
                after(dve, "att_p", start + n + 1)
                nc.vector.tensor_tensor(
                    res3[:, h, :, 0:D].rearrange("p g (a d) -> p g a d", d=HD),
                    rows4[:, h, :, D:2 * D].rearrange("p g (a d) -> p g a d", d=HD),
                    bc(res3[:, h, :, D:W3].unsqueeze(3), [P, G, H3, HD]), ALU.mult).then_inc(sem("att_res"), 1)

            def step(n, h, left):
                scores3(n, h)
                if left > 2:
                    after(dve, "tile_sum", tiles0[s] + G * (n - R + 3))
                    one_hot(dve, s, slots_s, KS, n + 2, (h + 2) % R)
                if not isinstance(n, int) or n > 0:
                    weighted(n - 1, (h - 1) % R)
                if not isinstance(n, int) or n > 1:
                    add_tiles(dve, s, block_s, n - 2, 4, W3)
            one_hot(dve, s, slots_s, KS, 0, 0)
            one_hot(dve, s, slots_s, KS, 1, 1)
            att_groups(dve, step)
            weighted(NG - 1, (NG - 1) % R)
            add_tiles(dve, s, block_s, NG - 2, 4, W3)
            add_tiles(dve, s, block_s, NG - 1, 4, W3)

        block_ = ctx.enter_context(nc.Block())

        @block_.sync
        def _(sp):
            def edges(a):
                return a.rearrange("(p f) -> p f", p=P)

            def weight(dst_ap, src_ap, name):
                sp.dma_start(dst_ap, src_ap).then_inc(sem(name), 16)

            weight(key_i, edges(dst), "gd_loaded")
            weight(other_i, edges(src), "gd_loaded")
            weight(etype_i, edges(etype), "gd_loaded")
            weight(attr_sb, attr.rearrange("(p f) w -> p (f w)", p=P), "gd_loaded")
            weight(x3, x.rearrange("(b p) c -> p b c", p=P), "x_loaded")
            for k in range(2):
                weight(wring[:, 0, k, 0:F0], wft[k * P:(k + 1) * P, :], "w0_loaded")
                weight(wring[:, 0, k, ROW0:ROW0 + F0], wrt[k * P:(k + 1) * P, :], "w0_loaded")
            weight(wring[0:F0, 1, 0, 0:C], wf, "w0_loaded")
            weight(wring[0:F0, 1, 0, C:2 * C], wr, "w0_loaded")
            weight(wring[0:F0, 1, 1, 0:HEADS], attnt, "w0_loaded")
            sp.wait_ge(sem("fill"), 2)
            weight(slots_d_dram.rearrange("(p t) w -> p (t w)", p=P), slots_d[:, :], "gd_filled")
            weight(slots_s_dram.rearrange("(p t) w -> p (t w)", p=P), slots_s[:, :], "gs_filled")
            sp.wait_ge(sem("gd_rows"), 1)
            sp.wait_ge(sem("gd_done"), 1)
            weight(key_i, edges(src), "gs_loaded")
            weight(other_i, edges(dst), "gs_loaded")
            weight(etype_i, edges(etype), "gs_loaded")
            table_store(sp, "d0", table0, 2 * ROW0, tab0)
            slots_load(sp, "gd", slots_d_dram)

            def m_store(n, h):
                after(sp, "e0_ms", n + 1)
                sp.dma_start(mslots[:, bass.ds(n * (G * ROW0), G * ROW0)], ms0[:, h, :, :].rearrange("p g w -> p (g w)"))\
                    .then_inc(sem(f"m_stored{h}"), 16)
            groups(sp, m_store)
            for h in range(R):
                sp.wait_ge(sem(f"m_stored{h}"), 16 * (NG // R))

            def m_load(n, h):
                after(sp, "e0b_msg", n - R + 1)
                sp.dma_start(rows4[:, h, :, 0:ROW0],
                             mslots[:, bass.ds(n * (G * ROW0), G * ROW0)].rearrange("p (g w) -> p g w", g=G))\
                    .then_inc(sem(f"m_loaded{h}"), 16)
            groups(sp, m_load)
            slots_load(sp, "gs", slots_s_dram)
            if layers > 1:
                sp.wait_ge(sem("e0_done"), 1)
                for k in range(2):
                    weight(wring[:, 0, k, 0:C], w_self[k * P:(k + 1) * P, :], "w1_loaded")
                    weight(wring[:, 0, k, C:2 * C], w_neigh[k * P:(k + 1) * P, :], "w1_loaded")
                table_store(sp, "d1", table1, C)
            if layers > 2:
                sp.wait_ge(sem("e1_done"), 1)
                for k in range(2):
                    weight(wring[:, 0, k, 0:C], loop_w[k * P:(k + 1) * P, :], "w2_loaded")
                weight(bias[:, 0, :], bias_self.rearrange("(a n) -> a n", a=1).partition_broadcast(P), "w2_loaded")
                for name, rel, b, table in (("pf", rel_f, bias_f, table2f), ("pb", rel_b, bias_b, table2b)):
                    sp.wait_ge(sem("d2_done" if name == "pf" else "pf_done"), 1)
                    weight(bias[:, 1, :], b.rearrange("(a n) -> a n", a=1).partition_broadcast(P), name + "_bias")
                    rk = rel.rearrange("r (k p) c -> r k p c", p=P)

                    def w_load(q, s):
                        for k in range(2):
                            for r in range(2):
                                sp.dma_start(wring[:, s, k, r * C:(r + 1) * C],
                                             rk[bass.ds(q * 2 + r, 1), k, :, :].rearrange("a p c -> p (a c)"))\
                                    .then_inc(sem(f"{name}_w{s}"), 16)

                    w_load(0, 0)
                    w_load(1, 1)

                    def pairs(q, s, more):
                        for g in range(NB // 5):
                            after(sp, name + "_ev", NB * q + 5 * g + 5)
                            for r in range(2):
                                sp.dma_start(table[bass.ds((q * 2 + r) * NP + g * 5 * P, 5 * P), :]
                                             .rearrange("(j p) w -> p j w", p=P),
                                             projtab[:, (s * (NB // 5) + g) % 2, :, r * C:(r + 1) * C])\
                                    .then_inc(sem(f"{name}_stored{(s * (NB // 5) + g) % 2}"), 16)
                        if more:
                            after(sp, name + "_mm", NB * q + NB)
                            w_load(q + 2, s)
                    with sp.Fori(0, RELS // 2 - 3, 2) as q0:
                        pairs(q0, 0, True)
                        pairs(q0 + 1, 1, True)
                    pairs(RELS // 2 - 2, 0, False)
                    pairs(RELS // 2 - 1, 1, False)
            if layers > 3:
                sp.wait_ge(sem("e2_done"), 1)
                for k in range(2):
                    weight(wring[:, 0, k, 0:D], wp[k * P:(k + 1) * P, :], "w3_loaded")
                weight(bias[:, 0, 0:D], wp_b.rearrange("(a n) -> a n", a=1).partition_broadcast(P), "w3_loaded")
                weight(bias[:, 1, 0:D], w_pos.rearrange("(a n) -> a n", a=1).partition_broadcast(P), "w3_loaded")
                for s, e, qkv, table, sc, bi, before in (("da", "e3a", (q1, k1, v1), table3[0], ln1_s, ln1_b, "d3_done"),
                                                         ("db", "e3b", (q2, k2, v2), table3[1], ln2_s, ln2_b, "e3a_done")):
                    sp.wait_ge(sem(before), 1)
                    for i, w in enumerate(qkv):
                        weight(wring[:, 0, 0, i * D:(i + 1) * D], w, s + "_loaded")
                    weight(bias[:, 0, 0:D], sc.rearrange("(a n) -> a n", a=1).partition_broadcast(P), s + "_loaded")
                    weight(bias[:, 1, 0:D], bi.rearrange("(a n) -> a n", a=1).partition_broadcast(P), s + "_loaded")
                    table_store(sp, s, table, 2 * D)
                sp.wait_ge(sem("e3b_done"), 1)
                weight(wring[:, 0, 0, 0:C], inv_w, "w4_loaded")
                weight(bias[:, 0, :], inv_b.rearrange("(a n) -> a n", a=1).partition_broadcast(P), "w4_loaded")
            sp.wait_ge(sem("x_done"), 1)
            full = N // P
            sp.dma_start(out[0:full * P, :].rearrange("(b p) c -> p b c", p=P), x3[:, 0:full, :]).then_inc(sem("out_stored"), 16)
            sp.dma_start(out[full * P:N, :], x_sb[0:N - full * P, full * C:(full + 1) * C]).then_inc(sem("out_stored"), 16)
            sp.wait_ge(sem("out_stored"), 32)

        @block_.gpsimd
        def _(pool):
            pool.iota(iota_i[:, :], [[1, P]], base=0, channel_multiplier=0).then_inc(sem("iota"), 1)
            pool.iota(iota_t_i, [[1, T]], base=0, channel_multiplier=0).then_inc(sem("iota"), 1)
            pool.memset(ident[:, :], 0.0).then_inc(sem("consts"), 1)
            pool.memset(tri[:, :], 1.0).then_inc(sem("consts"), 1)
            pool.memset(ones[:, :], 1.0).then_inc(sem("consts"), 1)
            pool.memset(slots_d[:, :], 0.0).then_inc(sem("consts"), 1)
            pool.memset(slots_s[:, :], 0.0).then_inc(sem("consts"), 1)
            pool.wait_ge(sem("consts"), 5)
            pool.affine_select(out=ident[:, :], in_=ident[:, :], compare_op=ALU.not_equal, fill=1.0, base=0,
                               pattern=[[-1, P]], channel_multiplier=1).then_inc(sem("consts"), 1)
            pool.affine_select(out=tri[:, :], in_=tri[:, :], compare_op=ALU.is_gt, fill=0.0, base=0,
                               pattern=[[1, P]], channel_multiplier=-1).then_inc(sem("consts"), 1)
            pool.memset(sd3[:, :, 2:3], -1.0).then_inc(sem("fill"), 1)
            pool.memset(ss3[:, :, 2:3], -1.0).then_inc(sem("fill"), 1)
            scatter(pool, "gd", slots_d_dram)
            pool.wait_ge(sem("d0_stored"), TABLE_STORED)
            gather_loop(pool, "e0", table0, 2 * ROW0)
            scatter(pool, "gs", slots_s_dram)
            if layers > 1:
                pool.wait_ge(sem("d1_stored"), TABLE_STORED)
                gather_loop(pool, "e1", table1, C)
            if layers > 2:
                for name, e, table in (("pf", "e2f", table2f), ("pb", "e2b", table2b)):
                    for s in range(2):
                        pool.wait_ge(sem(f"{name}_stored{s}"), 32 * (RELS // 2) * (NB // 5) // 2)
                    gather_loop(pool, e, table, C)
            if layers > 3:
                for s, e, table in (("da", "e3a", table3[0]), ("db", "e3b", table3[1])):
                    pool.wait_ge(sem(s + "_stored"), TABLE_STORED)
                    gather_loop(pool, e, table, 2 * D)

        @block_.scalar
        def _(act):
            act.wait_ge(sem("x_loaded"), 16)
            dense_act(act, "d0")
            act.wait_ge(sem("gd_slots"), 16)

            def e0(n, h):
                after(act, "e0_ms", n - R + 1)
                src_ap = slots_d[:, bass.ds(n * (G * KD), G * KD)].rearrange("p (t w) -> p t w", w=KD)
                nc.scalar.activation(gidx[:, h, :], src_ap[:, :, 0], ACT.Copy).then_inc(sem("row_numbers"), 1)

            def e0_scores(n, h):
                after(act, "e0_ms", n + 1)
                nc.scalar.activation(scores[:, bass.ds(n * (G * HEADS), G * HEADS)].rearrange("p (g w) -> p g w", w=HEADS),
                                     ms0[:, h, :, F0:ROW0], ACT.Copy).then_inc(sem("e0_sc"), 1)
            for n in range(R - 1):
                e0(n, n)
            for n in range(R):
                e0(n + 3, (n + 3) % R)
                e0_scores(n, n)
            with act.Fori(R, NG - 2 * R + 1, R) as n0:
                for h in range(R):
                    e0(n0 + h + 3, (h + 3) % R)
                    e0_scores(n0 + h, h)
            for n in range(NG - R, NG):
                if n + 3 < NG:
                    e0(n + 3, (n + 3) % R)
                e0_scores(n, n % R)
            act.wait_ge(sem("e0_shifted"), 1)
            nc.scalar.activation(scores, scores, ACT.Exp).then_inc(sem("e0_p"), 1)
            act.wait_ge(sem("e0_p"), 1)
            for h in range(R):
                act.wait_ge(sem(f"m_stored{h}"), 16 * (NG // R))

            def e0b(n, h):
                after(act, "tile_sum", tiles0["e0b"] + G * (n - R + 1))
                nc.scalar.activation(msgA[:, h, :, HEADS * F0:HEADS * F0 + HEADS],
                                     scores[:, bass.ds(n * (G * HEADS), G * HEADS)].rearrange("p (g w) -> p g w", w=HEADS),
                                     ACT.Copy).then_inc(sem("e0b_p"), 1)
            groups(act, e0b)
            norm_act(act, "n0")
            if layers > 1:
                act.wait_ge(sem("e0_done"), 1)
                dense_act(act, "d1")
                sum_act(act, "e1", slots_d, KD, 0)
                norm_act(act, "n1")
            if layers > 2:
                act.wait_ge(sem("e1_done"), 1)
                dense_act(act, "d2")
                sum_act(act, "e2f", slots_d, KD, 1)
                act.wait_ge(sem("gs_slots"), 16)
                act.wait_ge(sem("e2f_done"), 1)
                sum_act(act, "e2b", slots_s, KS, 1)
                norm_act(act, "n2")
            if layers > 3:
                act.wait_ge(sem("e2_done"), 1)
                dense_act(act, "d3")
                for s, e, nm in (("da", "e3a", "n3a"), ("db", "e3b", "n3b")):
                    act.wait_ge(sem("d3_done" if s == "da" else "e3a_done"), 1)
                    dense_act(act, s)
                    att_act(act, e)
                    norm_act(act, nm)
                act.wait_ge(sem("e3b_done"), 1)
                dense_act(act, "d4")
                norm_act(act, "n4")

        @block_.vector
        def _(dve):
            chain = [0]

            def link(ins):
                chain[0] += 1
                ins.then_inc(sem("vector"), 1)
                dve.wait_ge(sem("vector"), chain[0])

            dve.wait_ge(sem("iota"), 2)
            link(nc.vector.tensor_copy(iota[:, :], iota_i[:, :]))
            link(nc.vector.tensor_copy(iota_t, iota_t_i))
            dve.wait_ge(sem("consts"), 7)
            sort_dve(dve, "gd", link)
            dve.sem_inc(sem("gd_done"), 1)
            dve.wait_ge(sem("w0_scores"), 1)
            for k in range(2):
                link(nc.vector.tensor_copy(wring[:, 0, k, F0:ROW0], ps[:, 6, k * HEADS:(k + 1) * HEADS]))
                link(nc.vector.tensor_copy(wring[:, 0, k, ROW0 + F0:2 * ROW0], ps[:, 6, (2 + k) * HEADS:(3 + k) * HEADS]))
            dve.sem_inc(sem("w0_done"), 1)

            def d0(it):
                for j in range(5):
                    after(dve, "block_out", first["d0"] + 5 * it + j + 1)
                    if j == 0:
                        after(dve, "d0_stored", 16 * it)
                    nc.vector.tensor_copy(tab0[:, j * 2 * ROW0:(j + 1) * 2 * ROW0], ps[:, 2 + j, 0:2 * ROW0])\
                        .then_inc(sem("block_ev"), 1)
            blocks(dve, d0)
            sort_dve(dve, "gs", link)
            dve.wait_ge(sem("gd_slots"), 16)

            def e0(n, h):
                rec = slots_d[:, bass.ds(n * (G * KD), G * KD)].rearrange("p (t w) -> p t w", w=KD)
                for k in range(G):
                    after(dve, f"rows_ready{h * G + k}", gathered("e0", n, h))
                after(dve, "e0_ms", n - R + 1)
                nc.vector.tensor_tensor(lin0[:, h, :, :], rows4[:, h, :, ROW0:2 * ROW0],
                                        bc(rec[:, :, 4:5], [P, G, ROW0]), ALU.mult).then_inc(sem("e0_lin"), 1)
                after(dve, f"m_stored{h}", (16 // R) * (n - h))
                after(dve, "e0_sc", n - R + 1)
                nc.vector.tensor_tensor(ms0[:, h, :, :], rows4[:, h, :, 0:ROW0],
                                        bc(rec[:, :, 3:4], [P, G, ROW0]), ALU.mult).then_inc(sem("e0_lin"), 1)
                dve.wait_ge(sem("e0_lin"), 2 * n + 2)
                nc.vector.tensor_tensor(ms0[:, h, :, :], ms0[:, h, :, :], lin0[:, h, :, :], ALU.add)\
                    .then_inc(sem("e0_ms"), 1)
            groups(dve, e0)
            dve.wait_ge(sem("e0_sc"), NG)
            link(nc.vector.scalar_tensor_tensor(scores, scores, 0.2, scores, ALU.mult, ALU.max))
            link(nc.vector.tensor_scalar(pen, sd3[:, 0:T, 2], 0.0, -1e30, ALU.is_lt, ALU.mult))
            link(nc.vector.tensor_tensor(sc3, sc3, bc(pen.unsqueeze(2), [P, T, HEADS]), ALU.add))
            link(nc.vector.tensor_reduce(small[:, 0:HEADS], scores.rearrange("p (t h) -> p h t", h=HEADS), AX.X, ALU.max))
            link(nc.vector.memset(acc[:, :], 0.0))
            dve.sem_inc(sem("e0_max"), 1)
            dve.wait_ge(sem("e0_maxT"), 1)
            link(nc.vector.tensor_reduce(small[0:HEADS, 8:9], ps[0:HEADS, 6, 0:P], AX.X, ALU.max))
            link(nc.vector.tensor_scalar(small[0:HEADS, 16:16 + HEADS], ident[0:HEADS, 0:HEADS], small[0:HEADS, 8:9], None, ALU.mult))
            dve.sem_inc(sem("e0_diag"), 1)
            dve.wait_ge(sem("e0_maxB"), 1)
            link(nc.vector.tensor_copy(small[:, 24:24 + HEADS], ps[:, 7, 0:HEADS]))
            nc.vector.tensor_tensor(sc3, sc3, bc(small[:, 24:24 + HEADS].unsqueeze(1), [P, T, HEADS]), ALU.subtract)\
                .then_inc(sem("e0_shifted"), 1)
            dve.wait_ge(sem("e0_p"), 1)
            for h in range(R):
                dve.wait_ge(sem(f"m_stored{h}"), 16 * (NG // R))
            W0 = HEADS * F0 + HEADS

            def e0b(n, h):
                after(dve, "tile_sum", tiles0["e0b"] + G * (n - R + 1))
                one_hot(dve, "e0b", slots_d, KD, n, h)
                after(dve, f"m_loaded{h}", (16 // R) * (n - h) + 16)
                p = scores[:, bass.ds(n * (G * HEADS), G * HEADS)].rearrange("p (g a) -> p g a", a=HEADS)
                nc.vector.tensor_tensor(
                    msgA[:, h, :, 0:HEADS * F0].rearrange("p g (a f) -> p g a f", f=F0),
                    bc(rows4[:, h, :, 0:F0].unsqueeze(2), [P, G, HEADS, F0]),
                    bc(p.unsqueeze(3), [P, G, HEADS, F0]), ALU.mult).then_inc(sem("e0b_msg"), 1)
                if not isinstance(n, int) or n > 0:
                    add_tiles(dve, "e0b", block_d, n - 1, 0, W0)
            groups(dve, e0b)
            add_tiles(dve, "e0b", block_d, NG - 1, 0, W0)
            dve.wait_ge(sem("tile_added"), tiles0["e0b"] + T)
            a0 = acc[:, 0:NB * W0].rearrange("p (b w) -> p b w", w=W0)
            den = small[:, 128:128 + NB * HEADS].rearrange("p (b a) -> p b a", a=HEADS)
            link(nc.vector.tensor_scalar(den, a0[:, :, HEADS * F0:W0], 1e-10, None, ALU.add))
            link(nc.vector.reciprocal(den, den))
            o0 = a0[:, :, 0:HEADS * F0]
            link(nc.vector.tensor_tensor(o0.rearrange("p b (a f) -> p b a f", f=F0), o0.rearrange("p b (a f) -> p b a f", f=F0),
                                         bc(den.unsqueeze(3), [P, NB, HEADS, F0]), ALU.mult))
            link(nc.vector.tensor_tensor(x3, x3, o0, ALU.add))
            norm_dve(dve, "n0", x3, C, 1e-5, link, big2)
            dve.sem_inc(sem("e0_done"), 1)
            deg = small[:, 128:128 + NB]

            if layers > 1:
                def d1(it):
                    for j in range(5):
                        i = 5 * it + j
                        hn = ps[:, 2 + j, C:2 * C]
                        x_b = x_sb[:, bass.ds(i * C, C)]
                        work = [msg[:, j * 512:j * 512 + C], msg[:, j * 512 + C:j * 512 + 2 * C]]
                        after(dve, "block_out", first["d1"] + i + 1)
                        nc.vector.tensor_tensor(x_b, x_b, ps[:, 2 + j, 0:C], ALU.add)
                        left = hn
                        for r in range(MAXK // 8):
                            nc.vector.max(top8[:, r, :], left).then_inc(sem("d1_top"), 1)
                            dve.wait_ge(sem("d1_top"), 8 * i + 2 * r + 1)
                            dve.nop(nofuse=True)
                            nc.vector.match_replace(work[r % 2], top8[:, r, :], left, LOWEST).then_inc(sem("d1_top"), 1)
                            dve.wait_ge(sem("d1_top"), 8 * i + 2 * r + 2)
                            dve.nop(nofuse=True)
                            left = work[r % 2]
                        if j == 0:
                            after(dve, "d1_stored", 16 * it)
                        nc.vector.scalar_tensor_tensor(tab[:, j * C:(j + 1) * C], left, LOWEST, hn, ALU.is_equal, ALU.mult)\
                            .then_inc(sem("block_ev"), 1)
                blocks(dve, d1)
                nc.vector.memset(rows[:, :, C:C + 1], 1.0).then_inc(sem("ones_col"), 1)
                link(nc.vector.memset(acc[:, :], 0.0))
                sum_dve(dve, "e1", slots_d, KD, block_d, C + 1)
                dve.wait_ge(sem("tile_added"), tiles0["e1"] + T)
                a1 = acc[:, 0:NB * (C + 1)].rearrange("p (b w) -> p b w", w=C + 1)
                link(nc.vector.tensor_copy(deg.unsqueeze(2), a1[:, :, C:C + 1]))
                link(nc.vector.tensor_scalar(small[:, 160:160 + NB], deg, 1.0, None, ALU.max))
                link(nc.vector.reciprocal(small[:, 160:160 + NB], small[:, 160:160 + NB]))
                link(nc.vector.tensor_tensor(a1[:, :, 0:C], a1[:, :, 0:C], bc(small[:, 160:160 + NB].unsqueeze(2), [P, NB, C]), ALU.mult))
                link(nc.vector.tensor_tensor(x3, x3, a1[:, :, 0:C], ALU.add))
                for h in range(2):
                    dve.wait_ge(sem(f"gs_placed{h}"), SC_EDGES * 8 * NS)
                norm_dve(dve, "n1", x3, C, 1e-5, link)
                dve.sem_inc(sem("e1_done"), 1)

            def mean_add(a, dg):
                link(nc.vector.tensor_scalar(small[:, 160:160 + NB], dg, 1.0, None, ALU.max))
                link(nc.vector.reciprocal(small[:, 160:160 + NB], small[:, 160:160 + NB]))
                link(nc.vector.tensor_tensor(a, a, bc(small[:, 160:160 + NB].unsqueeze(2), [P, NB, C]), ALU.mult))
                link(nc.vector.tensor_tensor(x3, x3, a, ALU.add))

            if layers > 2:
                dve.wait_ge(sem("w2_loaded"), 16 * 3)

                def d2(it):
                    for j in range(5):
                        i = 5 * it + j
                        x_b = x_sb[:, bass.ds(i * C, C)]
                        after(dve, "block_out", first["d2"] + i + 1)
                        nc.vector.tensor_copy(xt_all[:, :, bass.ds(i * P, P)], xts[:, j, :].rearrange("p (k n) -> p k n", k=2))\
                            .then_inc(sem("d2_xt_all"), 1)
                        nc.vector.scalar_tensor_tensor(tab[:, j * C:(j + 1) * C], ps[:, 2 + j, 0:C], 2.0, bias[:, 0, :],
                                                       ALU.mult, ALU.add).then_inc(sem("d2_s"), 1)
                        after(dve, "d2_s", i + 1)
                        nc.vector.tensor_tensor(x_b, x_b, tab[:, j * C:(j + 1) * C], ALU.add).then_inc(sem("block_ev"), 1)
                blocks(dve, d2)
                dve.wait_ge(sem("d2_xt_all"), NB)
                dve.wait_ge(sem("block_ev"), first["d2"] + NB)
                dve.sem_inc(sem("d2_done"), 1)
                for name in ("pf", "pb"):
                    dve.wait_ge(sem(name + "_bias"), 16)

                    def pairs(q, s):
                        for m in range(NB):
                            g = m // 5
                            slot = (s * (NB // 5) + g) % 2
                            after(dve, name + "_mm", NB * q + m + 1)
                            if m % 5 == 0:
                                if isinstance(q, int):
                                    after(dve, f"{name}_stored{slot}", 32 * ((q * (NB // 5) + g) // 2))
                                else:
                                    after(dve, f"{name}_stored{slot}", (q - s) * (16 * (NB // 5)) + 32 * ((s * (NB // 5) + g) // 2))
                            nc.vector.tensor_tensor(
                                projtab[:, slot, m % 5, :].rearrange("p (r c) -> p r c", r=2),
                                ps[:, m % 5, :].rearrange("p (r c) -> p r c", r=2),
                                bc(bias[:, 1, :].unsqueeze(1), [P, 2, C]), ALU.add).then_inc(sem(name + "_ev"), 1)
                    pairs(0, 0)
                    pairs(1, 1)
                    with dve.Fori(2, RELS // 2 - 1, 2) as q0:
                        pairs(q0, 0)
                        pairs(q0 + 1, 1)
                    dve.wait_ge(sem(name + "_ev"), NB * (RELS // 2))
                    for s in range(2):
                        dve.wait_ge(sem(f"{name}_stored{s}"), 32 * (RELS // 2) * (NB // 5) // 2)
                    dve.sem_inc(sem(name + "_done"), 1)
                link(nc.vector.memset(acc[:, :], 0.0))
                sum_dve(dve, "e2f", slots_d, KD, block_d, C)
                dve.wait_ge(sem("tile_added"), tiles0["e2f"] + T)
                mean_add(acc[:, 0:NB * C].rearrange("p (b w) -> p b w", w=C), deg)
                link(nc.vector.memset(acc[:, :], 0.0))
                dve.wait_ge(sem("gs_slots"), 16)
                dve.sem_inc(sem("e2f_done"), 1)
                sum_dve(dve, "e2b", slots_s, KS, block_s, C + 1)
                dve.wait_ge(sem("tile_added"), tiles0["e2b"] + T)
                a2 = acc[:, 0:NB * (C + 1)].rearrange("p (b w) -> p b w", w=C + 1)
                link(nc.vector.tensor_copy(deg.unsqueeze(2), a2[:, :, C:C + 1]))
                mean_add(a2[:, :, 0:C], deg)
                norm_dve(dve, "n2", x3, C, 1e-5, link)
                dve.sem_inc(sem("e2_done"), 1)

            if layers > 3:
                emb3 = emb.rearrange("p (b d) -> p b d", d=D)
                dve.wait_ge(sem("w3_loaded"), 16 * 4)
                link(nc.vector.tensor_tensor(bias[:, 0, 0:D], bias[:, 0, 0:D], bias[:, 1, 0:D], ALU.add))

                def d3(it):
                    for j in range(5):
                        after(dve, "block_out", first["d3"] + 5 * it + j + 1)
                        nc.vector.tensor_tensor(emb[:, bass.ds((5 * it + j) * D, D)], ps[:, 2 + j, 0:D], bias[:, 0, 0:D],
                                                ALU.add).then_inc(sem("block_ev"), 1)
                blocks(dve, d3)
                dve.wait_ge(sem("block_ev"), first["d3"] + NB)
                dve.sem_inc(sem("d3_done"), 1)
                for s, e, nm in (("da", "e3a", "n3a"), ("db", "e3b", "n3b")):
                    dve.wait_ge(sem(s + "_loaded"), 16 * 5)

                    def qkv(it):
                        for j in range(5):
                            after(dve, "block_out", first[s] + 5 * it + j + 1)
                            nc.vector.tensor_copy(q_sb[:, bass.ds((5 * it + j) * D, D)], ps[:, 2 + j, 0:D])\
                                .then_inc(sem(s + "_q"), 1)
                            if j == 0:
                                after(dve, s + "_stored", 16 * it)
                            nc.vector.tensor_copy(tab[:, j * 2 * D:(j + 1) * 2 * D], ps[:, 2 + j, D:3 * D])\
                                .then_inc(sem("block_ev"), 1)
                    blocks(dve, qkv)
                    dve.wait_ge(sem(s + "_q"), NB)
                    link(nc.vector.memset(acc[:, 0:NB * W3], 0.0))
                    att_dve(dve, e)
                    dve.wait_ge(sem("tile_added"), tiles0[e] + T)
                    a3 = acc[:, 0:NB * W3].rearrange("p (b w) -> p b w", w=W3)
                    den3 = small[:, 104:104 + NB * H3].rearrange("p (b a) -> p b a", a=H3)
                    link(nc.vector.tensor_scalar(den3, a3[:, :, D:W3], 1e-8, None, ALU.add))
                    link(nc.vector.reciprocal(den3, den3))
                    agg = a3[:, :, 0:D].rearrange("p b (a d) -> p b a d", d=HD)
                    link(nc.vector.tensor_tensor(agg, agg, bc(den3.unsqueeze(3), [P, NB, H3, HD]), ALU.mult))
                    link(nc.vector.tensor_tensor(emb3, emb3, a3[:, :, 0:D], ALU.add))
                    norm_dve(dve, nm, emb3, D, 1e-6, link)
                    link(nc.vector.tensor_tensor(emb3, emb3, bc(bias[:, 0, 0:D].unsqueeze(1), [P, NB, D]), ALU.mult))
                    link(nc.vector.tensor_tensor(emb3, emb3, bc(bias[:, 1, 0:D].unsqueeze(1), [P, NB, D]), ALU.add))
                    dve.sem_inc(sem(e + "_done"), 1)
                dve.wait_ge(sem("w4_loaded"), 32)

                def d4(it):
                    for j in range(5):
                        i = 5 * it + j
                        x_b = x_sb[:, bass.ds(i * C, C)]
                        after(dve, "block_out", first["d4"] + i + 1)
                        nc.vector.tensor_tensor(tab[:, j * C:(j + 1) * C], ps[:, 2 + j, 0:C], bias[:, 0, :], ALU.add)\
                            .then_inc(sem("d4_s"), 1)
                        after(dve, "d4_s", i + 1)
                        nc.vector.tensor_tensor(x_b, x_b, tab[:, j * C:(j + 1) * C], ALU.add).then_inc(sem("block_ev"), 1)
                blocks(dve, d4)
                dve.wait_ge(sem("block_ev"), first["d4"] + NB)
                norm_dve(dve, "n4", x3, C, 1e-5, link)
            dve.sem_inc(sem("x_done"), 1)

        @block_.tensor
        def _(pe):
            pe.wait_ge(sem("consts"), 7)
            sort_pe(pe, "gd")
            pe.wait_ge(sem("w0_loaded"), 16 * 7)
            for d in range(2):
                for k in range(2):
                    last = nc.tensor.matmul(ps[:, 6, (2 * d + k) * HEADS:(2 * d + k + 1) * HEADS],
                                            wring[0:F0, 1, 0, d * C + k * P:d * C + (k + 1) * P],
                                            wring[0:F0, 1, 1, 0:HEADS], start=True, stop=True)
            last.then_inc(sem("w0_scores"), 1)
            pe.wait_ge(sem("w0_done"), 1)
            dense_pe(pe, "d0", wring[:, 0, :, :])
            sort_pe(pe, "gs")
            pe.wait_ge(sem("e0_max"), 1)
            nc.tensor.transpose(ps[0:HEADS, 6, 0:P], small[:, 0:HEADS], ident[:, :]).then_inc(sem("e0_maxT"), 1)
            pe.wait_ge(sem("e0_diag"), 1)
            nc.tensor.matmul(ps[:, 7, 0:HEADS], ones[0:HEADS, :], small[0:HEADS, 16:16 + HEADS], start=True, stop=True)\
                .then_inc(sem("e0_maxB"), 1)
            W0 = HEADS * F0 + HEADS

            def e0b(n, h):
                after(pe, "tile_onehot", groups0["e0b"] + n + 1)
                after(pe, "e0b_msg", n + 1)
                after(pe, "e0b_p", n + 1)
                for k in range(G):
                    sum_tile(pe, "e0b", n, h, k, 0, W0, msgA[:, h, k, 0:W0])
            groups(pe, e0b)
            if layers > 1:
                pe.wait_ge(sem("w1_loaded"), 16 * 4)
                dense_pe(pe, "d1", wring[:, 0, :, :])
                pe.wait_ge(sem("ones_col"), 1)
                sum_pe(pe, "e1", C + 1)
            if layers > 2:
                pe.wait_ge(sem("w2_loaded"), 16 * 3)
                dense_pe(pe, "d2", wring[:, 0, :, :])
                pe.wait_ge(sem("d2_done"), 1)
                for name in ("pf", "pb"):
                    def pairs(q, s):
                        after(pe, f"{name}_w{s}", 32 * (q - s) + 64)
                        for m in range(NB):
                            after(pe, name + "_ev", NB * q + m - 4)
                            for k in range(2):
                                last = nc.tensor.matmul(ps[:, m % 5, :], xt_all[:, k, m * P:(m + 1) * P],
                                                        wring[:, s, k, :], start=(k == 0), stop=(k == 1))
                            last.then_inc(sem(name + "_mm"), 1)
                    pairs(0, 0)
                    pairs(1, 1)
                    with pe.Fori(2, RELS // 2 - 1, 2) as q0:
                        pairs(q0, 0)
                        pairs(q0 + 1, 1)
                sum_pe(pe, "e2f", C)
                pe.wait_ge(sem("e2f_done"), 1)
                sum_pe(pe, "e2b", C + 1)
            if layers > 3:
                pe.wait_ge(sem("w3_loaded"), 16 * 4)
                dense_pe(pe, "d3", wring[:, 0, :, :])
                for s, e in (("da", "e3a"), ("db", "e3b")):
                    pe.wait_ge(sem(s + "_loaded"), 16 * 5)
                    dense_pe(pe, s, wring[:, 0, :, :])
                    pe.wait_ge(sem(s + "_q"), NB)
                    att_pe(pe, e)
                pe.wait_ge(sem("w4_loaded"), 32)
                dense_pe(pe, "d4", wring[:, 0, :, :])


def kernel(x, src, dst, edge_attr_2, edge_type_16, L0_gnn_W_forward, L0_gnn_W_reverse, L0_gnn_attn_forward,
           L1_gnn_W_self, L1_gnn_W_neigh, L2_gnn_Wf, L2_gnn_Wb, L2_gnn_loop_weight, L2_gnn_forward_bias,
           L2_gnn_backward_bias, L2_gnn_self_bias, L3_gnn_W_P_w, L3_gnn_W_P_b, L3_gnn_W_pos, L3_gnn_q1, L3_gnn_k1,
           L3_gnn_v1, L3_gnn_ln1_s, L3_gnn_ln1_b, L3_gnn_q2, L3_gnn_k2, L3_gnn_v2, L3_gnn_ln2_s, L3_gnn_ln2_b,
           L3_gnn_inv_w, L3_gnn_inv_b):
    import numpy as np
    import concourse.bacc as bacc
    from concourse import mybir
    from concourse.bass_utils import run_bass_kernel_spmd

    arrays = host_arrays(x, src, dst, edge_attr_2, edge_type_16, L0_gnn_W_forward, L0_gnn_W_reverse, L0_gnn_attn_forward,
                         L1_gnn_W_self, L1_gnn_W_neigh, L2_gnn_Wf, L2_gnn_Wb, L2_gnn_loop_weight, L2_gnn_forward_bias,
                         L2_gnn_backward_bias, L2_gnn_self_bias, L3_gnn_W_P_w, L3_gnn_W_P_b, L3_gnn_W_pos, L3_gnn_q1,
                         L3_gnn_k1, L3_gnn_v1, L3_gnn_ln1_s, L3_gnn_ln1_b, L3_gnn_q2, L3_gnn_k2, L3_gnn_v2, L3_gnn_ln2_s,
                         L3_gnn_ln2_b, L3_gnn_inv_w, L3_gnn_inv_b)
    nc = bacc.Bacc("TRN2", target_bir_lowering=False, num_devices=1)
    named = {f"in_{name}": a for name, a in arrays.items()}
    ins = {name: nc.dram_tensor(f"in_{name}", a.shape, mybir.dt.from_np(a.dtype), kind="ExternalInput").ap()
           for name, a in arrays.items()}
    out = nc.dram_tensor("out_0", (3125, 256), mybir.dt.float32, kind="ExternalOutput").ap()
    gnn_program(nc, **ins, out=out)
    r = run_bass_kernel_spmd(nc, [named], core_ids=[0])
    return r.results[0]["out_0"]


def host_arrays(x, src, dst, attr, etype, wf, wr, attn, w_self, w_neigh, rel_f, rel_b, loop_w, bias_f, bias_b, bias_self,
                wp, wp_b, w_pos, q1, k1, v1, ln1_s, ln1_b, q2, k2, v2, ln2_s, ln2_b, inv_w, inv_b):
    import numpy as np

    def tail(a, n, value):
        a = np.asarray(a)
        return np.concatenate([a, np.full((n,) + a.shape[1:], value, a.dtype)])

    nodes, edges = np.asarray(x).shape[0], np.asarray(src).shape[0]
    more_n, more_e = -nodes % 128, -edges % (128 * 26)
    padded = nodes + more_n
    arrays = dict(x=tail(x, more_n, 0), src=tail(src, more_e, padded), dst=tail(dst, more_e, padded),
                  etype=tail(etype, more_e, 0), attr=tail(attr, more_e, 0), wf=wf, wr=wr,
                  wft=np.transpose(np.asarray(wf)), wrt=np.transpose(np.asarray(wr)),
                  attnt=np.transpose(np.asarray(attn)[0]), w_self=w_self, w_neigh=w_neigh, rel_f=rel_f, rel_b=rel_b,
                  loop_w=loop_w, bias_f=bias_f, bias_b=bias_b, bias_self=bias_self, wp=wp, wp_b=wp_b,
                  w_pos=np.asarray(w_pos).reshape(-1), q1=q1, k1=k1, v1=v1, ln1_s=ln1_s, ln1_b=ln1_b, q2=q2, k2=k2, v2=v2,
                  ln2_s=ln2_s, ln2_b=ln2_b, inv_w=inv_w, inv_b=inv_b)
    return {name: np.ascontiguousarray(a) for name, a in arrays.items()}
```

```python
from contextlib import ExitStack

import concourse.bass as bass
from concourse import mybir


def gnn_program(nc, x, src, dst, etype, attr, wf, wr, wft, wrt, attnt, w_self, w_neigh, rel_f, rel_b, loop_w,
                bias_f, bias_b, bias_self, wp, wp_b, w_pos, q1, k1, v1, ln1_s, ln1_b, q2, k2, v2, ln2_s, ln2_b,
                inv_w, inv_b, out, layers=4):
    f32, i32 = mybir.dt.float32, mybir.dt.int32
    ALU, ACT, AX = mybir.AluOpType, mybir.ActivationFunctionType, mybir.AxisListType
    P = 128
    N, C = 3125, 256
    NP = x.shape[0]
    NB = NP // P
    EP = src.shape[0]
    EC = EP // P
    BINS = NB + 1
    G = 4
    R = 4
    T = -(-(EC + NB) // (G * R)) * G * R
    NG = T // G
    TP = T + 1
    HEADS, F0 = 4, 64
    HEADS_DVE = 2
    ROW0 = F0 + HEADS
    MAXK = 32
    RELS = rel_f.shape[0]
    D, H3 = 128, 8
    HD = D // H3
    W3 = D + H3
    SC_EDGES = 13
    KD, KS = 5, 3
    OFF = T * P
    LOWEST = -3.4028234663852886e38

    ctx = ExitStack()
    with ctx:
        def sb(name, shape, dt=f32):
            return ctx.enter_context(nc.sbuf_tensor(name, shape, dt))

        def dram(name, shape):
            return nc.dram_tensor(name, shape, f32).ap()

        sems = {}

        def sem(name):
            if name not in sems:
                sems[name] = ctx.enter_context(nc.semaphore(name))
            return sems[name]

        def after(eng, name, value):
            if not (isinstance(value, int) and value <= 0):
                eng.wait_ge(sem(name), value)

        def groups(eng, body, first=0):
            for n in range(R):
                body(n, n % R)
            with eng.Fori(R, NG - 2 * R + 1, R) as n0:
                for h in range(R):
                    body(n0 + h, h)
            for n in range(NG - R, NG):
                body(n, n % R)

        PAIRS = RELS // 2

        def groups_beside(eng, body, unit):
            assert NG == PAIRS * (NB + 1)
            for n in range(PAIRS):
                body(n, n % R)
            for j in range(PAIRS):
                body(PAIRS + j, j % R)
                unit(0, j)
            with eng.Fori(2, NB + 1) as i:
                for j in range(PAIRS):
                    body(i * PAIRS + j, j % R)
                    unit(i - 1, j)

        x_sb = sb("x_sb", [P, NB * C])
        slots_d = sb("slots_d", [P, TP * KD])
        slots_s = sb("slots_s", [P, TP * KS])
        block_d = sb("block_d", [1, T], i32)
        block_s = sb("block_s", [1, T], i32)
        gidx = sb("gidx", [P, R, G], i32)
        rows = sb("rows", [P, R * G, 264])
        onehot = sb("onehot", [P, R, G, P])
        msg = sb("msg", [P, R * G * 264])
        acc = sb("acc", [P, 6600])
        big1 = sb("big1", [P, NB * C])
        big2 = sb("big2", [P, NB * C])
        wring = sb("wring", [P, 2, 2, 512])
        xs = sb("xs", [P, 5, 256])
        xts = sb("xts", [P, 5, 256])
        bias = sb("bias", [P, 2, 256])
        iota_i = sb("iota_i", [P, P], i32)
        iota = sb("iota", [P, P])
        ident = sb("ident", [P, P])
        ones = sb("ones", [P, P])
        tri = sb("tri", [P, P])
        cnt = sb("cnt", [P, 32])
        base = sb("base", [P, 32])
        tiles_i = sb("tiles_i", [P, 32], i32)
        tiles_f = sb("tiles_f", [P, 32])
        incl = sb("incl", [P, 32])
        tend = sb("tend", [P, 4])
        tend_i = sb("tend_i", [P, 1], i32)
        stage = sb("stage", [P, 2, SC_EDGES * KD])
        stage_row = sb("stage_row", [P, 2, SC_EDGES], i32)
        small = sb("small", [P, 3 * 104])
        top8 = sb("top8", [P, 4, 8])
        unsorted = sb("unsorted", [1, 4], i32)
        in_order = sb("in_order", [1, 4])
        att = sb("att", [P, 3, G * H3])
        wa = sb("wa", [P, 64])
        ps = ctx.enter_context(nc.psum_tensor("ps", [P, 8, 512], f32))

        recs_d = dram("recs_d", [OFF + P * TP, KD])
        slots_s_dram = dram("slots_s_dram", [P * TP, KS])
        table0 = dram("table0", [NP, 2 * ROW0])
        mslots = dram("mslots", [P, T * ROW0])
        table1 = dram("table1", [NP, C])
        table2f = dram("table2f", [RELS * NP, C])
        table2b = dram("table2b", [RELS * NP, C])
        table3 = [dram("table3a", [NP, 2 * D]), dram("table3b", [NP, 2 * D])]

        x3 = x_sb[:, :].rearrange("p (b c) -> p b c", c=C)
        sd3 = slots_d[:, :].rearrange("p (t w) -> p t w", w=KD)
        ss3 = slots_s[:, :].rearrange("p (t w) -> p t w", w=KS)
        key_i = acc[:, 0:EC].bitcast(i32)
        kb_i = acc[:, EC:2 * EC].bitcast(i32)
        kbf = acc[:, 2 * EC:3 * EC]
        mask = acc[:, 3 * EC:4 * EC]
        scan = acc[:, 4 * EC:5 * EC]
        prod = acc[:, 5 * EC:6 * EC]
        rank = acc[:, 6 * EC:7 * EC]
        other_i = acc[:, 3 * EC:4 * EC].bitcast(i32)
        etype_i = acc[:, 4 * EC:5 * EC].bitcast(i32)
        pos_i = acc[:, 3 * EC:4 * EC].bitcast(i32)
        posc_i = acc[:, 4 * EC:5 * EC].bitcast(i32)
        attr_sb = rows[:, :, :].rearrange("p a b -> p (a b)")[:, 0:2 * EC]
        rec_d = big2[:, 0:EC * KD]
        row_d = big2[:, EC * KD:EC * (KD + 1)].bitcast(i32)
        rec_s = big1[:, 0:EC * KS]
        row_s = big1[:, EC * KS:EC * (KS + 1)].bitcast(i32)
        MS0 = 2 * R * G * ROW0
        iota_t_i = msg[0:32, MS0:MS0 + T].bitcast(i32)
        tile_ge = msg[0:32, MS0:MS0 + T]
        iota_t = msg[0:32, MS0 + T:MS0 + 2 * T]
        tile_block = big1[:, EC * (KS + 1):EC * (KS + 1) + T]
        tile_first = big1[0:1, EC * (KS + 1) + T:EC * (KS + 1) + 2 * T].bitcast(i32)
        next_i = small[0:P - 1, 300:301].bitcast(i32)
        next_f = small[0:P - 1, 301:302]
        falls = small[:, 302:304]
        scores = big2[:, 0:T * HEADS]
        sc3 = scores.rearrange("p (t h) -> p t h", h=HEADS)
        pen = big2[:, T * HEADS:T * (HEADS + 1)]
        msgA = msg[:, :].rearrange("p (r g w) -> p r g w", r=R, g=G)
        ms0 = msg[:, 0:R * G * ROW0].rearrange("p (r g w) -> p r g w", r=R, g=G)
        lin0 = msg[:, R * G * ROW0:2 * R * G * ROW0].rearrange("p (r g w) -> p r g w", r=R, g=G)
        res3 = msg[:, 0:R * G * W3].rearrange("p (r g w) -> p r g w", r=R, g=G)
        oneT = msg[:, R * G * W3:R * G * (W3 + P)].rearrange("p (r g w) -> p r g w", r=R, g=G)
        qk3 = big1[:, 0:R * G * D].rearrange("p (r g w) -> p r g w", r=R, g=G)
        rows4 = rows[:, :, :].rearrange("p (r g) w -> p r g w", g=G)
        emb = big2[:, 0:NB * D]
        q_sb = acc[:, NB * W3:NB * (W3 + D)]
        tab = big2[:, NB * D:NB * D + 5 * 512]
        tab0 = rows[:, :, :].rearrange("p a b -> p (a b)")[:, 2 * EC:2 * EC + 5 * 2 * ROW0]
        xt_all = big1[:, :].rearrange("p (k n) -> p k n", k=2)
        rel_res = [big2[:, i * 512:(i + 1) * 512] for i in range(12)] + [msg[:, i * 512:(i + 1) * 512] for i in range(4)]
        pb_ring = msg[:, 4 * 512:8 * 512].rearrange("p (s w) -> p s w", s=4)
        projtab = big2[:, 0:2 * 5 * 512].rearrange("p (s j w) -> p s j w", s=2, j=5)

        def bc(ap, shape):
            return ap.to_broadcast(shape)

        GATHERS = ["e0", "e1", "e2f", "e2b", "e3a", "e3b"]
        SUMS = ["e0b", "e1", "e2f", "e2b", "e3a", "e3b"]
        gathers0 = {s: NG * n for n, s in enumerate(GATHERS)}
        groups0 = {s: NG * n for n, s in enumerate(SUMS)}
        tiles0 = {s: T * n for n, s in enumerate(SUMS)}

        def gathered(s, n, h):
            return 16 * (NG // R) * GATHERS.index(s) + (16 // R) * (n - h) + 16

        def stage_index(act, s, slots, words, word):
            def body(n, h):
                after(act, "tile_sum", tiles0[s] + G * (n - R + 1))
                src_ap = slots[:, bass.ds(n * (G * words), G * words)].rearrange("p (t w) -> p t w", w=words)
                nc.scalar.activation(gidx[:, h, :], src_ap[:, :, word], ACT.Copy).then_inc(sem("row_numbers"), 1)
            return body

        def gather_loop(pool, s, table, width):
            def body(n, h):
                after(pool, "row_numbers", gathers0[s] + n + 1)
                pool.nop(nofuse=True)
                for k in range(G):
                    j = h * G + k
                    nc.gpsimd.indirect_dma_start(
                        out=rows[:, j, 0:width], out_offset=None, in_=table[:, :],
                        in_offset=bass.IndirectOffsetOnAxis(ap=gidx[:, h, k:k + 1], axis=0),
                    ).then_inc(sem(f"rows_ready{j}"), 16)
            groups(pool, body)

        def one_hot(dve, s, slots, words, n, h):
            loc = slots[:, bass.ds(n * (G * words), G * words)].rearrange("p (t w) -> p t w", w=words)[:, :, 2:3]
            nc.vector.tensor_tensor(onehot[:, h, :, :], bc(iota[:, :].unsqueeze(1), [P, G, P]),
                                    bc(loc, [P, G, P]), ALU.is_equal).then_inc(sem("tile_onehot"), 1)

        def tile_blocks(block, n, engine):
            _, numbers = nc.values_load_multi_w_load_instructions(
                block[0:1, bass.ds(n * G, G)], engines=(engine,), min_val=0, max_val=NB - 1,
                skip_runtime_bounds_check_because="a count of blocks, cut off at NB - 1 when it was made")
            return numbers

        def adder(dve, s, block, n, bank, width):
            of_tile = tile_blocks(block, n, mybir.EngineType.DVE)

            def add(k):
                b = of_tile[k]
                after(dve, "tile_sum", tiles0[s] + n * G + k + 1)
                after(dve, "tile_added", tiles0[s] + n * G + k)
                nc.vector.tensor_tensor(acc[:, bass.ds(b * width, width)], acc[:, bass.ds(b * width, width)],
                                        ps[:, bank + k, 0:width], ALU.add).then_inc(sem("tile_added"), 1)
            return add

        def add_tiles(dve, s, block, n, bank, width):
            add = adder(dve, s, block, n, bank, width)
            for k in range(G):
                add(k)

        def sum_tile(pe, s, n, h, k, bank, banks, width, rhs):
            after(pe, "tile_added", tiles0[s] + n * G + k - banks + 1)
            nc.tensor.matmul(ps[:, bank + k, 0:width], onehot[:, h, k, :], rhs,
                             start=True, stop=True).then_inc(sem("tile_sum"), 1)

        def sum_act(act, s, slots, words, word, loop=groups):
            loop(act, stage_index(act, s, slots, words, word))

        def sum_pe(pe, s, width, loop=groups):
            def body(n, h):
                after(pe, "tile_onehot", groups0[s] + n + 1)
                for k in range(G):
                    after(pe, f"rows_ready{h * G + k}", gathered(s, n, h))
                    sum_tile(pe, s, n, h, k, 0, G, width, rows[:, h * G + k, 0:width])
            loop(pe, body)

        def sum_dve(dve, s, slots, words, block, width, loop=groups):
            def body(n, h):
                later = not isinstance(n, int) or n > 0
                if later:
                    add = adder(dve, s, block, n - 1, 0, width)
                    add(0)
                after(dve, "tile_sum", tiles0[s] + G * (n - R + 1))
                one_hot(dve, s, slots, words, n, h)
                if later:
                    for k in range(1, G):
                        add(k)
            loop(dve, body)
            add_tiles(dve, s, block, NG - 1, 0, width)

        DENSE = {"d0": (x_sb, 256, 2 * ROW0), "d1": (x_sb, 256, 512), "d2": (x_sb, 256, 256),
                 "d3": (x_sb, 256, D), "da": (emb, D, 3 * D), "db": (emb, D, 3 * D), "d4": (emb, D, C)}

        first = {s: NB * n for n, s in enumerate(DENSE)}

        def blocks(eng, body):
            body(0)
            with eng.Fori(1, NB // 5) as it:
                body(it)

        def dense_act(act, s):
            src_sb, width, _ = DENSE[s]

            def body(it):
                for j in range(5):
                    after(act, "block_tr", first[s] + 5 * it + j - 4)
                    nc.scalar.activation(xs[:, j, 0:width], src_sb[:, bass.ds((5 * it + j) * width, width)],
                                         ACT.Copy).then_inc(sem("block_xs"), 1)
                for j in range(5):
                    after(act, "block_out", first[s] + 5 * it + j - 4)
                    if s == "d2":
                        after(act, "d2_xt_all", 5 * it + j - 4)
                    after(act, "block_tr", first[s] + 5 * it + j + 1)
                    nc.scalar.activation(xts[:, j, 0:width], ps[:, j % 2, 0:width], ACT.Copy)\
                        .then_inc(sem("block_xt"), 1)
            blocks(act, body)

        def dense_pe(pe, s, weights):
            _, width, wide = DENSE[s]
            kin = width // P

            def product(it, j):
                after(pe, "block_xt", first[s] + 5 * it + j + 1)
                after(pe, "block_ev", first[s] + 5 * it + j - 4)
                for k in range(kin):
                    last = nc.tensor.matmul(ps[:, 2 + j, 0:wide], xts[:, j, k * P:(k + 1) * P],
                                            weights[:, k, 0:wide], start=(k == 0), stop=(k == kin - 1))
                last.then_inc(sem("block_out"), 1)

            def body(it):
                for j in range(5):
                    after(pe, "block_xs", first[s] + 5 * it + j + 1)
                    after(pe, "block_xt", first[s] + 5 * it + j - (1 if j else 0))
                    for k in range(kin):
                        last = nc.tensor.transpose(ps[:, j % 2, k * P:(k + 1) * P], xs[:, j, k * P:(k + 1) * P],
                                                   ident[:, :])
                    last.then_inc(sem("block_tr"), 1)
                    if j:
                        product(it, j - 1)
                product(it, 4)
            blocks(pe, body)

        def table_store(sp, s, table, width, tab=tab):
            def body(it):
                after(sp, "block_ev", first[s] + 5 * it + 5)
                sp.dma_start(table[bass.ds(it * (5 * P), 5 * P), :].rearrange("(j p) w -> p j w", p=P),
                             tab[:, 0:5 * width].rearrange("p (j w) -> p j w", w=width))\
                    .then_inc(sem(s + "_stored"), 16)
            blocks(sp, body)

        TABLE_STORED = 16 * (NB // 5)

        ORDERS = {"gd": (dst, src, slots_d, KD, rec_d, row_d, block_d), "gs": (src, dst, slots_s, KS, rec_s, row_s, block_s)}

        def sort_keys(dve, o, link):
            _, _, slots, words, rec, rowno, block = ORDERS[o]
            r3 = rec.rearrange("p (f w) -> p f w", w=words)
            dve.wait_ge(sem(o + "_loaded"), 16 * (5 if o == "gd" else 3))
            link(nc.vector.tensor_scalar(kb_i, key_i, 7, None, ALU.logical_shift_right))
            if o == "gd":
                link(nc.vector.tensor_scalar(other_i, other_i, float(NP - 1), None, ALU.min))
                nc.vector.tensor_copy(r3[:, :, 3:5], attr_sb.rearrange("p (f w) -> p f w", w=2))
            else:
                link(nc.vector.tensor_scalar(key_i, key_i, P - 1, None, ALU.bitwise_and))
            nc.vector.tensor_copy(r3[:, :, 2], key_i)
            nc.vector.tensor_copy(r3[:, :, 0], other_i)
            nc.vector.scalar_tensor_tensor(r3[:, :, 1], etype_i, float(NP), other_i, ALU.mult, ALU.add)\
                .then_inc(sem(o + "_records"), 1)
            link(nc.vector.memset(rank, 0.0))
            link(nc.vector.tensor_copy(kbf, kb_i))

        def count_bin(dve, o, b):
            nc.vector.tensor_scalar(mask, kbf, iota[:, bass.ds(b, 1)], 0.0, ALU.is_equal, ALU.add,
                                    accum_out=cnt[:, bass.ds(b, 1)]).then_inc(sem(o + "_count"), 1)
            dve.wait_ge(sem(o + "_count"), b + 1)

        def rank_bin(dve, o, b):
            steps = sem(o + "_rank")
            nc.vector.tensor_scalar(mask, kbf, iota[:, bass.ds(b, 1)], None, ALU.is_equal).then_inc(steps, 1)
            dve.wait_ge(steps, b * 4 + 1)
            nc.vector.tensor_tensor_scan(scan, mask, mask, 0.0, ALU.add, ALU.max).then_inc(steps, 1)
            dve.wait_ge(steps, b * 4 + 2)
            nc.vector.scalar_tensor_tensor(prod, scan, base[:, bass.ds(b, 1)], mask, ALU.add, ALU.mult).then_inc(steps, 1)
            dve.wait_ge(steps, b * 4 + 3)
            nc.vector.tensor_tensor(rank, rank, prod, ALU.add).then_inc(steps, 1)
            dve.wait_ge(steps, b * 4 + 4)

        TOTAL, BEFORE, COLUMN, FALLS = 0, 32, 64, 80

        def sort_tiles(dve, o, link):
            _, _, slots, words, rec, rowno, block = ORDERS[o]
            dve.sem_inc(sem(o + "_counted"), 1)
            dve.wait_ge(sem(o + "_totals"), 1)
            for tot, width, ti, tf in ((ps[0:BINS, 0, COLUMN:COLUMN + 1], 1, tend_i, tend),
                                       (ps[:, 0, TOTAL:TOTAL + BINS], BINS, tiles_i, tiles_f)):
                p = tot.shape[0]
                link(nc.vector.tensor_scalar(tf[0:p, 0:width], tot, float(P - 1), None, ALU.add))
                link(nc.vector.tensor_copy(ti[0:p, 0:width], tf[0:p, 0:width]))
                link(nc.vector.tensor_scalar(ti[0:p, 0:width], ti[0:p, 0:width], 7, None, ALU.logical_shift_right))
                link(nc.vector.tensor_copy(tf[0:p, 0:width], ti[0:p, 0:width]))
                if width == 1:
                    link(nc.vector.scalar_tensor_tensor(tend[0:NB, 2:3], tend[0:NB, 0:1], -float(P),
                                                        ps[0:NB, 0, COLUMN:COLUMN + 1], ALU.mult, ALU.add))
                    dve.sem_inc(sem(o + "_tiles"), 1)
            link(nc.vector.tensor_tensor_scan(incl[:, 0:NB], tiles_f[:, 0:NB], tiles_f[:, 0:NB], 0.0, ALU.add, ALU.max))
            link(nc.vector.tensor_tensor(base[:, 0:NB], incl[:, 0:NB], tiles_f[:, 0:NB], ALU.subtract))
            after_tiles = float(OFF) if o == "gd" else 0.0
            link(nc.vector.tensor_scalar(base[:, 0:NB], base[:, 0:NB], float(P), after_tiles - 1.0, ALU.mult, ALU.add))
            link(nc.vector.memset(base[:, NB:BINS], float(T * P) + after_tiles - 1.0))
            link(nc.vector.tensor_tensor(base[:, 0:BINS], base[:, 0:BINS], ps[:, 0, BEFORE:BEFORE + BINS], ALU.add))
            dve.wait_ge(sem(o + "_tends"), 1)
            link(nc.vector.tensor_tensor(tend[0:NB, 1:2], tend[0:NB, 0:1], ps[0:NB, 1, 0:1], ALU.add))
            nc.vector.tensor_scalar(tile_ge[0:NB - 1, :], iota_t[0:NB - 1, :], tend[0:NB - 1, 1:2], None, ALU.is_ge)\
                .then_inc(sem(o + "_ge"), 1)
            dve.wait_ge(sem(o + "_blocks"), 1)
            for half in range(2):
                part = slice(half * (T // 2), (half + 1) * (T // 2))
                link(nc.vector.tensor_copy(block[0:1, part], ps[0:1, 4 + half, 0:T // 2]))
                if o == "gd":
                    link(nc.vector.tensor_copy(tile_block[:, part], ps[:, 4 + half, 0:T // 2]))

        def sort_pe(pe, o):
            pe.wait_ge(sem(o + "_counted"), 1)
            nc.tensor.matmul(ps[:, 0, TOTAL:TOTAL + BINS], ones[:, :], cnt[:, 0:BINS], start=True, stop=True)
            nc.tensor.matmul(ps[:, 0, BEFORE:BEFORE + BINS], tri[:, :], cnt[:, 0:BINS], start=True, stop=True)
            if o == "gd":
                nc.tensor.matmul(ps[0:1, 0, FALLS:FALLS + 1], falls[:, 0:1], ones[:, 0:1], start=True, stop=True)
            nc.tensor.matmul(ps[0:BINS, 0, COLUMN:COLUMN + 1], cnt[:, 0:BINS], ones[:, 0:1], start=True, stop=True)\
                .then_inc(sem(o + "_totals"), 1)
            pe.wait_ge(sem(o + "_tiles"), 1)
            nc.tensor.matmul(ps[0:NB, 1, 0:1], tri[0:NB, 0:NB], tend[0:NB, 0:1], start=True, stop=True)\
                .then_inc(sem(o + "_tends"), 1)
            pe.wait_ge(sem(o + "_ge"), 1)
            for half in range(2):
                ge = tile_ge[0:NB - 1, half * (T // 2):(half + 1) * (T // 2)]
                last = nc.tensor.matmul(ps[:, 4 + half, 0:T // 2], ones[0:NB - 1, :], ge, start=True, stop=True)
                if o == "gd":
                    last = nc.tensor.matmul(ps[0:1, 6 + half, 0:T // 2], tend[0:NB - 1, 2:3], ge, start=True, stop=True)
            last.then_inc(sem(o + "_blocks"), 1)

        NS = EC // SC_EDGES

        def scatter(pool, o, dram_slots):
            _, _, _, words, rec, rowno, _ = ORDERS[o]
            pool.wait_ge(sem(o + "_rows"), 1)
            pool.wait_ge(sem(o + "_filled"), 32 if o == "gd" else 16)

            def body(n, h):
                after(pool, f"{o}_placed{h}", SC_EDGES * 8 * (n - h))
                nc.gpsimd.tensor_copy(stage[:, h, 0:SC_EDGES * words],
                                      rec[:, bass.ds(n * (SC_EDGES * words), SC_EDGES * words)])\
                    .then_inc(sem(o + "_staged"), 1)
                nc.gpsimd.tensor_copy(stage_row[:, h, :], rowno[:, bass.ds(n * SC_EDGES, SC_EDGES)])\
                    .then_inc(sem(o + "_staged"), 1)
                pool.wait_ge(sem(o + "_staged"), 2 * n + 2)
                pool.nop(nofuse=True)
                for k in range(SC_EDGES):
                    nc.gpsimd.indirect_dma_start(
                        out=dram_slots[:, :], out_offset=bass.IndirectOffsetOnAxis(ap=stage_row[:, h, k:k + 1], axis=0),
                        in_=stage[:, h, k * words:(k + 1) * words], in_offset=None,
                    ).then_inc(sem(f"{o}_placed{h}"), 16)
            body(0, 0)
            body(1, 1)
            with pool.Fori(2, NS - 1, 2) as n0:
                body(n0, 0)
                body(n0 + 1, 1)

        def slots_load(sp, o, dram_slots):
            _, _, slots, words, _, _, _ = ORDERS[o]
            for h in range(2):
                sp.wait_ge(sem(f"{o}_placed{h}"), SC_EDGES * 8 * NS)
            sp.dma_start(slots[:, :], dram_slots.rearrange("(p t) w -> p (t w)", p=P)).then_inc(sem(o + "_slots"), 16)

        def norm_act(act, s):
            act.wait_ge(sem(s + "_var"), 1)
            nc.scalar.activation(small[:, 32:32 + NB], small[:, 0:NB], ACT.Sqrt).then_inc(sem(s + "_std"), 1)

        def norm_dve(dve, s, y, width, eps, link, scratch=big1):
            sq = scratch[:, 0:NB * width].rearrange("p (b c) -> p b c", c=width)
            m = small[:, 64:64 + NB]
            link(nc.vector.tensor_reduce(m, y, AX.X, ALU.add))
            link(nc.vector.tensor_scalar(m, m, 1.0 / width, None, ALU.mult))
            link(nc.vector.tensor_tensor(y, y, bc(m.unsqueeze(2), [P, NB, width]), ALU.subtract))
            link(nc.vector.tensor_tensor(sq, y, y, ALU.mult))
            link(nc.vector.tensor_reduce(m, sq, AX.X, ALU.add))
            nc.vector.tensor_scalar(small[:, 0:NB], m, 1.0 / width, eps, ALU.mult, ALU.add).then_inc(sem(s + "_var"), 1)
            dve.wait_ge(sem(s + "_std"), 1)
            link(nc.vector.reciprocal(small[:, 96:96 + NB], small[:, 32:32 + NB]))
            link(nc.vector.tensor_tensor(y, y, bc(small[:, 96:96 + NB].unsqueeze(2), [P, NB, width]), ALU.mult))

        ATTENTIONS = ["e3a", "e3b"]

        def att_groups(eng, step):
            for n in range(R):
                step(n, n, NG - n)
            with eng.Fori(R, NG - 2 * R + 1, R) as n0:
                for h in range(R):
                    step(n0 + h, h, NG)
            for n in range(NG - R, NG):
                step(n, n % R, NG - n)

        def att_act(act, s):
            start = NG * ATTENTIONS.index(s)

            def index(n, h):
                after(act, "att_res", start + n - R + 1)
                of = slots_s[:, bass.ds(n * (G * KS), G * KS)].rearrange("p (t w) -> p t w", w=KS)
                nc.scalar.activation(gidx[:, h, :], of[:, :, 0], ACT.Copy).then_inc(sem("row_numbers"), 1)

            def transposed(n, h):
                after(act, "att_tr", start + n + 1)
                nc.scalar.activation(oneT[:, h, :, :], ps[:, h % 2, :].rearrange("p (g e) -> p g e", g=G), ACT.Copy)\
                    .then_inc(sem("att_oneT"), 1)

            def exponents(n, h):
                after(act, "att_att", start + n + 1)
                after(act, "tile_sum", tiles0[s] + G * (n - R + 1))
                nc.scalar.activation(res3[:, h, :, D:W3], att[:, 1 + h % 2, :].rearrange("p (g a) -> p g a", a=H3),
                                     ACT.Exp).then_inc(sem("att_p"), 1)

            def step(n, h, left):
                if left > 3:
                    index(n + 3, (h + 3) % R)
                exponents(n, h)
                if left > 2:
                    transposed(n + 2, (h + 2) % R)
            for n in range(3):
                index(n, n)
            transposed(0, 0)
            transposed(1, 1)
            att_groups(act, step)

        def att_pe(pe, s):
            start = NG * ATTENTIONS.index(s)

            def transposes(n, h):
                after(pe, "tile_onehot", groups0[s] + n + 1)
                after(pe, "att_oneT", start + n - 1)
                for k in range(G):
                    last = nc.tensor.transpose(ps[:, h % 2, k * P:(k + 1) * P], onehot[:, h, k, :], ident[:, :])
                last.then_inc(sem("att_tr"), 1)

            def queries(n, h):
                after(pe, "att_oneT", start + n + 1)
                after(pe, "att_qk", start + n - 1)
                of_tile = tile_blocks(block_s, n, mybir.EngineType.PE)
                for k in range(G):
                    b = of_tile[k]
                    last = nc.tensor.matmul(ps[:, 2 + h % 2, k * D:(k + 1) * D], oneT[:, h, k, :],
                                            q_sb[:, bass.ds(b * D, D)], start=True, stop=True)
                last.then_inc(sem("att_q"), 1)

            def sums(n, h):
                after(pe, "att_res", start + n + 1)
                for k in range(G):
                    sum_tile(pe, s, n, h, k, 4, G, W3, res3[:, h, k, :])

            def step(n, h, left):
                if not isinstance(n, int) or n > 1:
                    sums(n - 2, (h - 2) % R)
                if left > 1:
                    queries(n + 1, (h + 1) % R)
                if left > 2:
                    transposes(n + 2, (h + 2) % R)
            transposes(0, 0)
            transposes(1, 1)
            queries(0, 0)
            att_groups(pe, step)
            sums(NG - 2, (NG - 2) % R)
            sums(NG - 1, (NG - 1) % R)

        def att_dve(dve, s):
            start = NG * ATTENTIONS.index(s)

            def step(n, h, left):
                older = not isinstance(n, int) or n > 1
                add = adder(dve, s, block_s, n - 2, 4, W3) if older else lambda k: None
                after(dve, "att_q", start + n + 1)
                for k in range(G):
                    after(dve, f"rows_ready{h * G + k}", gathered(s, n, h))
                nc.vector.tensor_tensor(qk3[:, h, :, :], ps[:, 2 + h % 2, :].rearrange("p (g d) -> p g d", d=D),
                                        rows4[:, h, :, 0:D], ALU.mult).then_inc(sem("att_qk"), 1)
                add(0)
                dve.wait_ge(sem("att_qk"), start + n + 1)
                nc.vector.tensor_reduce(att[:, 0, :], qk3[:, h, :, :].rearrange("p g (a d) -> p (g a) d", d=HD),
                                        AX.X, ALU.add).then_inc(sem("att_red"), 1)
                add(1)
                dve.wait_ge(sem("att_red"), start + n + 1)
                after(dve, "att_p", start + n - 1)
                nc.vector.tensor_scalar(att[:, 1 + h % 2, :], att[:, 0, :], 10.0, -10.0, ALU.min, ALU.max)\
                    .then_inc(sem("att_att"), 1)
                if left > 2:
                    after(dve, "tile_sum", tiles0[s] + G * (n - R + 3))
                    one_hot(dve, s, slots_s, KS, n + 2, (h + 2) % R)
                add(2)
                if not isinstance(n, int) or n > 0:
                    weighted(n - 1, (h - 1) % R)
                add(3)

            def weighted(n, h):
                after(dve, "att_p", start + n + 1)
                nc.vector.tensor_tensor(
                    res3[:, h, :, 0:D].rearrange("p g (a d) -> p g a d", d=HD),
                    rows4[:, h, :, D:2 * D].rearrange("p g (a d) -> p g a d", d=HD),
                    bc(res3[:, h, :, D:W3].unsqueeze(3), [P, G, H3, HD]), ALU.mult).then_inc(sem("att_res"), 1)
            one_hot(dve, s, slots_s, KS, 0, 0)
            one_hot(dve, s, slots_s, KS, 1, 1)
            att_groups(dve, step)
            weighted(NG - 1, (NG - 1) % R)
            add_tiles(dve, s, block_s, NG - 2, 4, W3)
            add_tiles(dve, s, block_s, NG - 1, 4, W3)

        block_ = ctx.enter_context(nc.Block())

        @block_.sync
        def _(sp):
            def edges(a):
                return a.rearrange("(p f) -> p f", p=P)

            def weight(dst_ap, src_ap, name):
                sp.dma_start(dst_ap, src_ap).then_inc(sem(name), 16)

            weight(key_i, edges(dst), "gd_loaded")
            with nc.allow_non_contiguous_dma(reason="one word a partition, once"):
                weight(next_i, edges(dst)[1:P, 0:1], "gd_loaded")
            weight(other_i, edges(src), "gd_loaded")
            weight(etype_i, edges(etype), "gd_loaded")
            weight(attr_sb, attr.rearrange("(p f) w -> p (f w)", p=P), "gd_loaded")
            weight(x3, x.rearrange("(b p) c -> p b c", p=P), "x_loaded")
            for k in range(2):
                weight(wring[:, 0, k, 0:F0], wft[k * P:(k + 1) * P, :], "w0_loaded")
                weight(wring[:, 0, k, ROW0:ROW0 + F0], wrt[k * P:(k + 1) * P, :], "w0_loaded")
            weight(wring[0:F0, 1, 0, 0:C], wf, "w0_loaded")
            weight(wring[0:F0, 1, 0, C:2 * C], wr, "w0_loaded")
            weight(wring[0:F0, 1, 1, 0:HEADS], attnt, "w0_loaded")
            sp.wait_ge(sem("fill"), 2)
            weight(recs_d[OFF:OFF + P * TP, :].rearrange("(p t) w -> p (t w)", p=P), slots_d[:, :], "gd_filled")
            weight(recs_d[EP:OFF, :].rearrange("(p t) w -> p (t w)", p=P), slots_d[:, 0:(OFF - EP) // P * KD], "gd_filled")
            weight(slots_s_dram.rearrange("(p t) w -> p (t w)", p=P), slots_s[:, :], "gs_filled")
            sp.wait_ge(sem("gd_records"), 1)
            weight(recs_d[0:EP, :].rearrange("(p f) w -> p (f w)", p=P), rec_d, "gd_recorded")
            sp.wait_ge(sem("gd_done"), 1)
            weight(key_i, edges(src), "gs_loaded")
            weight(other_i, edges(dst), "gs_loaded")
            weight(etype_i, edges(etype), "gs_loaded")
            table_store(sp, "d0", table0, 2 * ROW0, tab0)
            sp.wait_ge(sem("gd_filled"), 32)
            sp.wait_ge(sem("gd_recorded"), 16)
            sp.wait_ge(sem("gd_scattered"), 1)

            def records_load(n, h):
                after(sp, "row_numbers", gathers0["e0"] + n - R + 1)
                _, starts = nc.values_load_multi_w_load_instructions(
                    tile_first[0:1, bass.ds(n * G, G)], engines=(mybir.EngineType.SP,), min_val=0, max_val=OFF + (T - 1) * P,
                    skip_runtime_bounds_check_because="128 * tile, less what blocks before fell short, or OFF more")
                for k in range(G):
                    sp.dma_start(slots_d[:, bass.ds((n * G + k) * KD, KD)], recs_d[bass.ds(starts[k], P), :])\
                        .then_inc(sem(f"records_loaded{h}"), 16)
            groups(sp, records_load)
            for h in range(R):
                sp.wait_ge(sem(f"m_stored{h}"), 16 * (NG // R))

            def m_load(n, h):
                after(sp, "e0b_msg", n - R + 1)
                after(sp, "e0b_p", n - R + 1)
                sp.dma_start(rows4[:, h, :, 0:ROW0],
                             mslots[:, bass.ds(n * (G * ROW0), G * ROW0)].rearrange("p (g w) -> p g w", g=G))\
                    .then_inc(sem(f"m_loaded{h}"), 16)
            groups(sp, m_load)
            if layers > 1:
                sp.wait_ge(sem("e0_done"), 1)
                for k in range(2):
                    weight(wring[:, 0, k, 0:C], w_self[k * P:(k + 1) * P, :], "w1_loaded")
                    weight(wring[:, 0, k, C:2 * C], w_neigh[k * P:(k + 1) * P, :], "w1_loaded")
                table_store(sp, "d1", table1, C)
                slots_load(sp, "gs", slots_s_dram)
            if layers > 2:
                sp.wait_ge(sem("e1_done"), 1)
                for k in range(2):
                    weight(wring[:, 0, k, 0:C], loop_w[k * P:(k + 1) * P, :], "w2_loaded")
                weight(bias[:, 0, :], bias_self.rearrange("(a n) -> a n", a=1).partition_broadcast(P), "w2_loaded")
                sp.wait_ge(sem("d2_done"), 1)
                weight(bias[:, 1, :], bias_f.rearrange("(a n) -> a n", a=1).partition_broadcast(P), "pf_bias")
                rk = rel_f.rearrange("r (k p) c -> r k p c", p=P)

                def w_load(q, s):
                    for k in range(2):
                        for r in range(2):
                            sp.dma_start(wring[:, s, k, r * C:(r + 1) * C],
                                         rk[bass.ds(q * 2 + r, 1), k, :, :].rearrange("a p c -> p (a c)"))\
                                .then_inc(sem(f"pf_w{s}"), 16)

                w_load(0, 0)
                w_load(1, 1)

                def pairs(q, s, more):
                    for g in range(NB // 5):
                        after(sp, "pf_ev", NB * q + 5 * g + 5)
                        for r in range(2):
                            sp.dma_start(table2f[bass.ds((q * 2 + r) * NP + g * 5 * P, 5 * P), :]
                                         .rearrange("(j p) w -> p j w", p=P),
                                         projtab[:, (s * (NB // 5) + g) % 2, :, r * C:(r + 1) * C])\
                                .then_inc(sem(f"pf_stored{(s * (NB // 5) + g) % 2}"), 16)
                    if more:
                        after(sp, "pf_mm", NB * q + NB)
                        w_load(q + 2, s)
                with sp.Fori(0, RELS // 2 - 3, 2) as q0:
                    pairs(q0, 0, True)
                    pairs(q0 + 1, 1, True)
                pairs(RELS // 2 - 2, 0, False)
                pairs(RELS // 2 - 1, 1, False)
                sp.wait_ge(sem("pf_done"), 1)
                weight(bias[:, 1, :], bias_b.rearrange("(a n) -> a n", a=1).partition_broadcast(P), "pb_loaded")
                rk_b = rel_b.rearrange("r (k p) c -> k p r c", p=P)
                for q in range(PAIRS):
                    for k in range(2):
                        weight(rel_res[2 * q + k].rearrange("p (r c) -> p r c", r=2), rk_b[k, :, 2 * q:2 * q + 2, :], "pb_loaded")

                def pb_store(m, q):
                    after(sp, "pb_ev", m * PAIRS + q + 1)
                    sp.dma_start(table2b.rearrange("(r n) c -> n r c", n=NP)[bass.ds(m * P, P), 2 * q:2 * q + 2, :],
                                 pb_ring[:, q % 4, :].rearrange("p (r c) -> p r c", r=2)).then_inc(sem(f"pb_stored{q % 4}"), 16)
                for q in range(PAIRS):
                    pb_store(0, q)
                with sp.Fori(1, NB) as m:
                    for q in range(PAIRS):
                        pb_store(m, q)
            if layers > 3:
                sp.wait_ge(sem("e2_done"), 1)
                for k in range(2):
                    weight(wring[:, 0, k, 0:D], wp[k * P:(k + 1) * P, :], "w3_loaded")
                weight(bias[:, 0, 0:D], wp_b.rearrange("(a n) -> a n", a=1).partition_broadcast(P), "w3_loaded")
                weight(bias[:, 1, 0:D], w_pos.rearrange("(a n) -> a n", a=1).partition_broadcast(P), "w3_loaded")
                for s, e, qkv, table, sc, bi, before in (("da", "e3a", (q1, k1, v1), table3[0], ln1_s, ln1_b, "d3_done"),
                                                         ("db", "e3b", (q2, k2, v2), table3[1], ln2_s, ln2_b, "e3a_done")):
                    sp.wait_ge(sem(before), 1)
                    for i, w in enumerate(qkv):
                        weight(wring[:, 0, 0, i * D:(i + 1) * D], w, s + "_loaded")
                    weight(bias[:, 0, 0:D], sc.rearrange("(a n) -> a n", a=1).partition_broadcast(P), s + "_loaded")
                    weight(bias[:, 1, 0:D], bi.rearrange("(a n) -> a n", a=1).partition_broadcast(P), s + "_loaded")
                    table_store(sp, s, table, 2 * D)
                sp.wait_ge(sem("e3b_done"), 1)
                weight(wring[:, 0, 0, 0:C], inv_w, "w4_loaded")
                weight(bias[:, 0, :], inv_b.rearrange("(a n) -> a n", a=1).partition_broadcast(P), "w4_loaded")
            sp.wait_ge(sem("x_done"), 1)
            full = N // P
            sp.dma_start(out[0:full * P, :].rearrange("(b p) c -> p b c", p=P), x3[:, 0:full, :]).then_inc(sem("out_stored"), 16)
            sp.dma_start(out[full * P:N, :], x_sb[0:N - full * P, full * C:(full + 1) * C]).then_inc(sem("out_stored"), 16)
            sp.wait_ge(sem("out_stored"), 32)

        @block_.gpsimd
        def _(pool):
            pool.iota(iota_i[:, :], [[1, P]], base=0, channel_multiplier=0).then_inc(sem("iota"), 1)
            pool.iota(iota_t_i, [[1, T]], base=0, channel_multiplier=0).then_inc(sem("iota"), 1)
            pool.memset(ident[:, :], 0.0).then_inc(sem("consts"), 1)
            pool.memset(tri[:, :], 1.0).then_inc(sem("consts"), 1)
            pool.memset(ones[:, :], 1.0).then_inc(sem("consts"), 1)
            pool.memset(slots_d[:, :], 0.0).then_inc(sem("consts"), 1)
            pool.memset(slots_s[:, :], 0.0).then_inc(sem("consts"), 1)
            pool.wait_ge(sem("consts"), 5)
            pool.affine_select(out=ident[:, :], in_=ident[:, :], compare_op=ALU.not_equal, fill=1.0, base=0,
                               pattern=[[-1, P]], channel_multiplier=1).then_inc(sem("consts"), 1)
            pool.affine_select(out=tri[:, :], in_=tri[:, :], compare_op=ALU.is_gt, fill=0.0, base=0,
                               pattern=[[1, P]], channel_multiplier=-1).then_inc(sem("consts"), 1)
            pool.memset(sd3[:, :, 2:3], -1.0).then_inc(sem("fill"), 1)
            pool.memset(ss3[:, :, 2:3], -1.0).then_inc(sem("fill"), 1)
            pool.wait_ge(sem("gd_known"), 1)
            scattering = nc.gpsimd.value_load(unsorted[0:1, 0:1])
            with pool.If(scattering != 0):
                scatter(pool, "gd", recs_d)
                for h in range(2):
                    pool.wait_ge(sem(f"gd_placed{h}"), SC_EDGES * 8 * NS)
            pool.sem_inc(sem("gd_scattered"), 1)
            pool.wait_ge(sem("d0_stored"), TABLE_STORED)
            gather_loop(pool, "e0", table0, 2 * ROW0)
            scatter(pool, "gs", slots_s_dram)
            if layers > 1:
                pool.wait_ge(sem("d1_stored"), TABLE_STORED)
                gather_loop(pool, "e1", table1, C)
            if layers > 2:
                for s in range(2):
                    pool.wait_ge(sem(f"pf_stored{s}"), 32 * PAIRS * (NB // 5) // 2)
                gather_loop(pool, "e2f", table2f, C)
                for s in range(4):
                    pool.wait_ge(sem(f"pb_stored{s}"), 16 * PAIRS * NB // 4)
                gather_loop(pool, "e2b", table2b, C)
            if layers > 3:
                for s, e, table in (("da", "e3a", table3[0]), ("db", "e3b", table3[1])):
                    pool.wait_ge(sem(s + "_stored"), TABLE_STORED)
                    gather_loop(pool, e, table, 2 * D)

        @block_.scalar
        def _(act):
            act.wait_ge(sem("x_loaded"), 16)
            dense_act(act, "d0")

            def e0(n, h):
                after(act, "e0_ms", n - R + 1)
                after(act, f"records_loaded{h}", (16 * G // R) * (n - h) + 16 * G)
                src_ap = slots_d[:, bass.ds(n * (G * KD), G * KD)].rearrange("p (t w) -> p t w", w=KD)
                nc.scalar.activation(gidx[:, h, :], src_ap[:, :, 0], ACT.Copy).then_inc(sem("row_numbers"), 1)

            def e0_scores(n, h):
                after(act, "e0_ms", n + 1)
                nc.scalar.activation(scores[:, bass.ds(n * (G * HEADS), G * HEADS)].rearrange("p (g w) -> p g w", w=HEADS),
                                     ms0[:, h, :, F0:ROW0], ACT.Copy).then_inc(sem("e0_sc"), 1)
                act.dma_start(mslots[:, bass.ds(n * (G * ROW0), G * ROW0)], ms0[:, h, :, :].rearrange("p g w -> p (g w)"))\
                    .then_inc(sem(f"m_stored{h}"), 16)
            for n in range(R - 1):
                e0(n, n)
            for n in range(R):
                e0(n + 3, (n + 3) % R)
                e0_scores(n, n)
            with act.Fori(R, NG - 2 * R + 1, R) as n0:
                for h in range(R):
                    e0(n0 + h + 3, (h + 3) % R)
                    e0_scores(n0 + h, h)
            for n in range(NG - R, NG):
                if n + 3 < NG:
                    e0(n + 3, (n + 3) % R)
                e0_scores(n, n % R)
            act.wait_ge(sem("e0_shifted"), 1)
            nc.scalar.activation(scores, scores, ACT.Exp).then_inc(sem("e0_p"), 1)
            act.wait_ge(sem("e0_p"), 1)
            for h in range(R):
                act.wait_ge(sem(f"m_stored{h}"), 16 * (NG // R))

            def e0b(n, h):
                after(act, "tile_sum", tiles0["e0b"] + G * (n - R + 1))
                after(act, f"m_loaded{h}", (16 // R) * (n - h) + 16)
                for k in range(G):
                    for a in range(HEADS_DVE, HEADS):
                        nc.scalar.activation(msgA[:, h, k, a * F0:(a + 1) * F0], rows4[:, h, k, 0:F0], ACT.Copy,
                                             scale=scores[:, bass.ds(n * (G * HEADS) + (k * HEADS + a), 1)])
                nc.scalar.activation(msgA[:, h, :, HEADS * F0:HEADS * F0 + HEADS],
                                     scores[:, bass.ds(n * (G * HEADS), G * HEADS)].rearrange("p (g w) -> p g w", w=HEADS),
                                     ACT.Copy).then_inc(sem("e0b_p"), 1)
            groups(act, e0b)
            norm_act(act, "n0")
            if layers > 1:
                act.wait_ge(sem("e0_done"), 1)
                dense_act(act, "d1")
                sum_act(act, "e1", slots_d, KD, 0)
                norm_act(act, "n1")
            if layers > 2:
                act.wait_ge(sem("e1_done"), 1)
                dense_act(act, "d2")

                def pb_xt(m, q):
                    if q == PAIRS // 2:
                        after(act, "pb_mm", m * PAIRS)
                        nc.scalar.activation(xts[:, 0, :].rearrange("p (k n) -> p k n", k=2), xt_all[:, :, bass.ds(m * P, P)],
                                             ACT.Copy).then_inc(sem("pb_xt"), 1)
                sum_act(act, "e2f", slots_d, KD, 1, lambda eng, body: groups_beside(eng, body, pb_xt))
                act.wait_ge(sem("gs_slots"), 16)
                act.wait_ge(sem("e2f_done"), 1)
                sum_act(act, "e2b", slots_s, KS, 1)
                norm_act(act, "n2")
            if layers > 3:
                act.wait_ge(sem("e2_done"), 1)
                dense_act(act, "d3")
                for s, e, nm in (("da", "e3a", "n3a"), ("db", "e3b", "n3b")):
                    act.wait_ge(sem("d3_done" if s == "da" else "e3a_done"), 1)
                    dense_act(act, s)
                    att_act(act, e)
                    norm_act(act, nm)
                act.wait_ge(sem("e3b_done"), 1)
                dense_act(act, "d4")
                norm_act(act, "n4")

        @block_.vector
        def _(dve):
            chain = [0]

            def link(ins):
                chain[0] += 1
                ins.then_inc(sem("vector"), 1)
                dve.wait_ge(sem("vector"), chain[0])

            dve.wait_ge(sem("iota"), 2)
            link(nc.vector.tensor_copy(iota[:, :], iota_i[:, :]))
            link(nc.vector.tensor_copy(iota_t, iota_t_i))
            dve.wait_ge(sem("consts"), 7)
            sort_keys(dve, "gd", link)
            link(nc.vector.memset(falls[:, :], 0.0))
            link(nc.vector.tensor_scalar(next_i, next_i, 7, None, ALU.logical_shift_right))
            link(nc.vector.tensor_copy(next_f, next_i))
            link(nc.vector.tensor_tensor(falls[0:P - 1, 1:2], kbf[0:P - 1, EC - 1:EC], next_f, ALU.is_gt))
            link(nc.vector.tensor_tensor(prod[:, 0:EC - 1], kbf[:, 0:EC - 1], kbf[:, 1:EC], ALU.is_gt))
            link(nc.vector.tensor_reduce(falls[:, 0:1], prod[:, 0:EC - 1], AX.X, ALU.max))
            link(nc.vector.tensor_tensor(falls[:, 0:1], falls[:, 0:1], falls[:, 1:2], ALU.add))
            with dve.Fori(0, BINS) as b:
                count_bin(dve, "gd", b)
            sort_tiles(dve, "gd", link)
            link(nc.vector.tensor_copy(unsorted[:, 0:1], ps[0:1, 0, FALLS:FALLS + 1]))
            link(nc.vector.tensor_scalar(in_order[:, 0:1], ps[0:1, 0, FALLS:FALLS + 1], 0.0, None, ALU.is_equal))
            first_f = tile_ge[0:1, :]
            for half in range(2):
                link(nc.vector.tensor_scalar(first_f[:, half * (T // 2):(half + 1) * (T // 2)], ps[0:1, 6 + half, 0:T // 2],
                                             float(-OFF), in_order[:, 0:1], ALU.add, ALU.mult))
            link(nc.vector.scalar_tensor_tensor(first_f, iota_t[0:1, :], float(P), first_f, ALU.mult, ALU.add))
            link(nc.vector.tensor_scalar(tile_first, first_f, float(OFF), None, ALU.add))
            dve.sem_inc(sem("gd_known"), 1)
            ranking = nc.vector.value_load(unsorted[0:1, 0:1])
            with dve.If(ranking != 0):
                with dve.Fori(0, BINS) as b:
                    rank_bin(dve, "gd", b)
                nc.vector.tensor_copy(row_d, rank).then_inc(sem("gd_rows"), 1)
                dve.wait_ge(sem("gd_rows"), 1)
            dve.sem_inc(sem("gd_done"), 1)
            dve.wait_ge(sem("w0_scores"), 1)
            for k in range(2):
                link(nc.vector.tensor_copy(wring[:, 0, k, F0:ROW0], ps[:, 2, k * HEADS:(k + 1) * HEADS]))
                link(nc.vector.tensor_copy(wring[:, 0, k, ROW0 + F0:2 * ROW0], ps[:, 2, (2 + k) * HEADS:(3 + k) * HEADS]))
            dve.sem_inc(sem("w0_done"), 1)

            def d0(it):
                for j in range(5):
                    after(dve, "block_out", first["d0"] + 5 * it + j + 1)
                    if j == 0:
                        after(dve, "d0_stored", 16 * it)
                    nc.vector.tensor_copy(tab0[:, j * 2 * ROW0:(j + 1) * 2 * ROW0], ps[:, 2 + j, 0:2 * ROW0])\
                        .then_inc(sem("block_ev"), 1)
            blocks(dve, d0)
            sort_keys(dve, "gs", link)

            def e0(n, h):
                rec = slots_d[:, bass.ds(n * (G * KD), G * KD)].rearrange("p (t w) -> p t w", w=KD)
                for k in range(G):
                    after(dve, f"rows_ready{h * G + k}", gathered("e0", n, h))
                after(dve, "e0_ms", n - R + 1)
                nc.vector.tensor_tensor(lin0[:, h, :, :], rows4[:, h, :, ROW0:2 * ROW0],
                                        bc(rec[:, :, 4:5], [P, G, ROW0]), ALU.mult).then_inc(sem("e0_lin"), 1)
                after(dve, f"m_stored{h}", (16 // R) * (n - h))
                after(dve, "e0_sc", n - R + 1)
                nc.vector.tensor_tensor(ms0[:, h, :, :], rows4[:, h, :, 0:ROW0],
                                        bc(rec[:, :, 3:4], [P, G, ROW0]), ALU.mult).then_inc(sem("e0_lin"), 1)
                dve.wait_ge(sem("e0_lin"), 2 * n + 2)
                nc.vector.tensor_tensor(ms0[:, h, :, :], ms0[:, h, :, :], lin0[:, h, :, :], ALU.add)\
                    .then_inc(sem("e0_ms"), 1)
            for n in range(R):
                e0(n, n)
            with dve.Fori(0, NB) as b:
                for h in range(R):
                    e0(b * R + (R + h), h)
                count_bin(dve, "gs", b)
            count_bin(dve, "gs", NB)
            sort_tiles(dve, "gs", link)
            with dve.Fori(0, NB) as b:
                for h in range(R):
                    e0(b * R + ((NB + 1) * R + h), h)
                rank_bin(dve, "gs", b)
            rank_bin(dve, "gs", NB)
            for n in range((2 * NB + 1) * R, NG):
                e0(n, n % R)
            link(nc.vector.tensor_copy(pos_i, rank))
            link(nc.vector.tensor_scalar(posc_i, pos_i, 7, None, ALU.logical_shift_right))
            link(nc.vector.tensor_scalar(pos_i, pos_i, P - 1, None, ALU.bitwise_and))
            link(nc.vector.scalar_tensor_tensor(row_s, pos_i, float(TP), posc_i, ALU.mult, ALU.add))
            dve.sem_inc(sem("gs_rows"), 1)
            loc = sd3[:, 0:T, 2]
            link(nc.vector.scalar_tensor_tensor(loc, tile_block, -float(P), loc, ALU.mult, ALU.add))
            dve.wait_ge(sem("e0_sc"), NG)
            link(nc.vector.scalar_tensor_tensor(scores, scores, 0.2, scores, ALU.mult, ALU.max))
            link(nc.vector.tensor_scalar(pen, loc, 0.0, -1e30, ALU.is_lt, ALU.mult))
            link(nc.vector.tensor_scalar(tile_block, loc, float(P), -1e30, ALU.is_ge, ALU.mult))
            link(nc.vector.tensor_tensor(pen, pen, tile_block, ALU.add))
            link(nc.vector.tensor_tensor(sc3, sc3, bc(pen.unsqueeze(2), [P, T, HEADS]), ALU.add))
            link(nc.vector.tensor_reduce(small[:, 0:HEADS], scores.rearrange("p (t h) -> p h t", h=HEADS), AX.X, ALU.max))
            link(nc.vector.memset(acc[:, :], 0.0))
            dve.sem_inc(sem("e0_max"), 1)
            dve.wait_ge(sem("e0_maxT"), 1)
            link(nc.vector.tensor_reduce(small[0:HEADS, 8:9], ps[0:HEADS, 6, 0:P], AX.X, ALU.max))
            link(nc.vector.tensor_scalar(small[0:HEADS, 16:16 + HEADS], ident[0:HEADS, 0:HEADS], small[0:HEADS, 8:9], None, ALU.mult))
            dve.sem_inc(sem("e0_diag"), 1)
            dve.wait_ge(sem("e0_maxB"), 1)
            link(nc.vector.tensor_copy(small[:, 24:24 + HEADS], ps[:, 7, 0:HEADS]))
            nc.vector.tensor_tensor(sc3, sc3, bc(small[:, 24:24 + HEADS].unsqueeze(1), [P, T, HEADS]), ALU.subtract)\
                .then_inc(sem("e0_shifted"), 1)
            dve.wait_ge(sem("e0_p"), 1)
            for h in range(R):
                dve.wait_ge(sem(f"m_stored{h}"), 16 * (NG // R))
            W0 = HEADS * F0 + HEADS

            def e0b(n, h):
                older = not isinstance(n, int) or n > 1
                add = adder(dve, "e0b", block_d, n - 2, G * (h % 2), W0) if older else lambda k: None
                add(0)
                after(dve, "tile_sum", tiles0["e0b"] + G * (n - R + 1))
                one_hot(dve, "e0b", slots_d, KD, n, h)
                add(1)
                after(dve, f"m_loaded{h}", (16 // R) * (n - h) + 16)
                p = scores[:, bass.ds(n * (G * HEADS), G * HEADS)].rearrange("p (g a) -> p g a", a=HEADS)[:, :, 0:HEADS_DVE]
                nc.vector.tensor_tensor(
                    msgA[:, h, :, 0:HEADS_DVE * F0].rearrange("p g (a f) -> p g a f", f=F0),
                    bc(rows4[:, h, :, 0:F0].unsqueeze(2), [P, G, HEADS_DVE, F0]),
                    bc(p.unsqueeze(3), [P, G, HEADS_DVE, F0]), ALU.mult).then_inc(sem("e0b_msg"), 1)
                add(2)
                add(3)
            groups(dve, e0b)
            add_tiles(dve, "e0b", block_d, NG - 2, 0, W0)
            add_tiles(dve, "e0b", block_d, NG - 1, G, W0)
            dve.wait_ge(sem("tile_added"), tiles0["e0b"] + T)
            a0 = acc[:, 0:NB * W0].rearrange("p (b w) -> p b w", w=W0)
            den = small[:, 128:128 + NB * HEADS].rearrange("p (b a) -> p b a", a=HEADS)
            link(nc.vector.tensor_scalar(den, a0[:, :, HEADS * F0:W0], 1e-10, None, ALU.add))
            link(nc.vector.reciprocal(den, den))
            o0 = a0[:, :, 0:HEADS * F0]
            link(nc.vector.tensor_tensor(o0.rearrange("p b (a f) -> p b a f", f=F0), o0.rearrange("p b (a f) -> p b a f", f=F0),
                                         bc(den.unsqueeze(3), [P, NB, HEADS, F0]), ALU.mult))
            link(nc.vector.tensor_tensor(x3, x3, o0, ALU.add))
            norm_dve(dve, "n0", x3, C, 1e-5, link, big2)
            dve.sem_inc(sem("e0_done"), 1)
            deg = small[:, 128:128 + NB]

            if layers > 1:
                def d1(it):
                    for j in range(5):
                        i = 5 * it + j
                        hn = ps[:, 2 + j, C:2 * C]
                        x_b = x_sb[:, bass.ds(i * C, C)]
                        work = [msg[:, j * 512:j * 512 + C], msg[:, j * 512 + C:j * 512 + 2 * C]]
                        after(dve, "block_out", first["d1"] + i + 1)
                        nc.vector.tensor_tensor(x_b, x_b, ps[:, 2 + j, 0:C], ALU.add)
                        left = hn
                        for r in range(MAXK // 8):
                            nc.vector.max(top8[:, r, :], left).then_inc(sem("d1_top"), 1)
                            dve.wait_ge(sem("d1_top"), 8 * i + 2 * r + 1)
                            dve.nop(nofuse=True)
                            nc.vector.match_replace(work[r % 2], top8[:, r, :], left, LOWEST).then_inc(sem("d1_top"), 1)
                            dve.wait_ge(sem("d1_top"), 8 * i + 2 * r + 2)
                            dve.nop(nofuse=True)
                            left = work[r % 2]
                        if j == 0:
                            after(dve, "d1_stored", 16 * it)
                        nc.vector.scalar_tensor_tensor(tab[:, j * C:(j + 1) * C], left, LOWEST, hn, ALU.is_equal, ALU.mult)\
                            .then_inc(sem("block_ev"), 1)
                blocks(dve, d1)
                nc.vector.memset(rows[:, :, C:C + 1], 1.0).then_inc(sem("ones_col"), 1)
                link(nc.vector.memset(acc[:, :], 0.0))
                sum_dve(dve, "e1", slots_d, KD, block_d, C + 1)
                dve.wait_ge(sem("tile_added"), tiles0["e1"] + T)
                a1 = acc[:, 0:NB * (C + 1)].rearrange("p (b w) -> p b w", w=C + 1)
                link(nc.vector.tensor_copy(deg.unsqueeze(2), a1[:, :, C:C + 1]))
                link(nc.vector.tensor_scalar(small[:, 160:160 + NB], deg, 1.0, None, ALU.max))
                link(nc.vector.reciprocal(small[:, 160:160 + NB], small[:, 160:160 + NB]))
                link(nc.vector.tensor_tensor(a1[:, :, 0:C], a1[:, :, 0:C], bc(small[:, 160:160 + NB].unsqueeze(2), [P, NB, C]), ALU.mult))
                link(nc.vector.tensor_tensor(x3, x3, a1[:, :, 0:C], ALU.add))
                for h in range(2):
                    dve.wait_ge(sem(f"gs_placed{h}"), SC_EDGES * 8 * NS)
                norm_dve(dve, "n1", x3, C, 1e-5, link)
                dve.sem_inc(sem("e1_done"), 1)

            def mean_add(a, dg):
                link(nc.vector.tensor_scalar(small[:, 160:160 + NB], dg, 1.0, None, ALU.max))
                link(nc.vector.reciprocal(small[:, 160:160 + NB], small[:, 160:160 + NB]))
                link(nc.vector.tensor_tensor(a, a, bc(small[:, 160:160 + NB].unsqueeze(2), [P, NB, C]), ALU.mult))
                link(nc.vector.tensor_tensor(x3, x3, a, ALU.add))

            if layers > 2:
                dve.wait_ge(sem("w2_loaded"), 16 * 3)

                def d2(it):
                    for j in range(5):
                        i = 5 * it + j
                        x_b = x_sb[:, bass.ds(i * C, C)]
                        after(dve, "block_out", first["d2"] + i + 1)
                        nc.vector.tensor_copy(xt_all[:, :, bass.ds(i * P, P)], xts[:, j, :].rearrange("p (k n) -> p k n", k=2))\
                            .then_inc(sem("d2_xt_all"), 1)
                        nc.vector.scalar_tensor_tensor(tab[:, j * C:(j + 1) * C], ps[:, 2 + j, 0:C], 2.0, bias[:, 0, :],
                                                       ALU.mult, ALU.add).then_inc(sem("d2_s"), 1)
                        after(dve, "d2_s", i + 1)
                        nc.vector.tensor_tensor(x_b, x_b, tab[:, j * C:(j + 1) * C], ALU.add).then_inc(sem("block_ev"), 1)
                blocks(dve, d2)
                dve.wait_ge(sem("d2_xt_all"), NB)
                dve.wait_ge(sem("block_ev"), first["d2"] + NB)
                dve.sem_inc(sem("d2_done"), 1)
                dve.wait_ge(sem("pf_bias"), 16)

                def pairs(q, s):
                    for m in range(NB):
                        g = m // 5
                        slot = (s * (NB // 5) + g) % 2
                        after(dve, "pf_mm", NB * q + m + 1)
                        if m % 5 == 0:
                            if isinstance(q, int):
                                after(dve, f"pf_stored{slot}", 32 * ((q * (NB // 5) + g) // 2))
                            else:
                                after(dve, f"pf_stored{slot}", (q - s) * (16 * (NB // 5)) + 32 * ((s * (NB // 5) + g) // 2))
                        nc.vector.tensor_tensor(
                            projtab[:, slot, m % 5, :].rearrange("p (r c) -> p r c", r=2),
                            ps[:, m % 5, :].rearrange("p (r c) -> p r c", r=2),
                            bc(bias[:, 1, :].unsqueeze(1), [P, 2, C]), ALU.add).then_inc(sem("pf_ev"), 1)
                pairs(0, 0)
                pairs(1, 1)
                with dve.Fori(2, PAIRS - 1, 2) as q0:
                    pairs(q0, 0)
                    pairs(q0 + 1, 1)
                dve.wait_ge(sem("pf_ev"), NB * PAIRS)
                for s in range(2):
                    dve.wait_ge(sem(f"pf_stored{s}"), 32 * PAIRS * (NB // 5) // 2)
                dve.sem_inc(sem("pf_done"), 1)
                link(nc.vector.memset(acc[:, :], 0.0))

                def pb_out(m, q):
                    after(dve, "pb_mm", m * PAIRS + q + 1)
                    after(dve, f"pb_stored{q % 4}", m * (16 * PAIRS // 4) + 16 * (q // 4))
                    nc.vector.tensor_tensor(
                        pb_ring[:, q % 4, :].rearrange("p (r c) -> p r c", r=2),
                        ps[:, 4 + q % 4, :].rearrange("p (r c) -> p r c", r=2),
                        bc(bias[:, 1, :].unsqueeze(1), [P, 2, C]), ALU.add).then_inc(sem("pb_ev"), 1)

                def pb_before(m, q):
                    if isinstance(m, int) and m == 0 and q == 0:
                        return
                    pb_out(*((m, q - 1) if q else (m - 1, PAIRS - 1)))
                sum_dve(dve, "e2f", slots_d, KD, block_d, C, lambda eng, body: groups_beside(eng, body, pb_before))
                pb_out(NB - 1, PAIRS - 1)
                dve.wait_ge(sem("tile_added"), tiles0["e2f"] + T)
                mean_add(acc[:, 0:NB * C].rearrange("p (b w) -> p b w", w=C), deg)
                link(nc.vector.memset(acc[:, :], 0.0))
                dve.wait_ge(sem("gs_slots"), 16)
                dve.sem_inc(sem("e2f_done"), 1)
                sum_dve(dve, "e2b", slots_s, KS, block_s, C + 1)
                dve.wait_ge(sem("tile_added"), tiles0["e2b"] + T)
                a2 = acc[:, 0:NB * (C + 1)].rearrange("p (b w) -> p b w", w=C + 1)
                link(nc.vector.tensor_copy(deg.unsqueeze(2), a2[:, :, C:C + 1]))
                mean_add(a2[:, :, 0:C], deg)
                norm_dve(dve, "n2", x3, C, 1e-5, link)
                dve.sem_inc(sem("e2_done"), 1)

            if layers > 3:
                emb3 = emb.rearrange("p (b d) -> p b d", d=D)
                dve.wait_ge(sem("w3_loaded"), 16 * 4)
                link(nc.vector.tensor_tensor(bias[:, 0, 0:D], bias[:, 0, 0:D], bias[:, 1, 0:D], ALU.add))

                def d3(it):
                    for j in range(5):
                        after(dve, "block_out", first["d3"] + 5 * it + j + 1)
                        nc.vector.tensor_tensor(emb[:, bass.ds((5 * it + j) * D, D)], ps[:, 2 + j, 0:D], bias[:, 0, 0:D],
                                                ALU.add).then_inc(sem("block_ev"), 1)
                blocks(dve, d3)
                dve.wait_ge(sem("block_ev"), first["d3"] + NB)
                dve.sem_inc(sem("d3_done"), 1)
                for s, e, nm in (("da", "e3a", "n3a"), ("db", "e3b", "n3b")):
                    dve.wait_ge(sem(s + "_loaded"), 16 * 5)

                    def qkv(it):
                        for j in range(5):
                            after(dve, "block_out", first[s] + 5 * it + j + 1)
                            nc.vector.tensor_copy(q_sb[:, bass.ds((5 * it + j) * D, D)], ps[:, 2 + j, 0:D])\
                                .then_inc(sem(s + "_q"), 1)
                            if j == 0:
                                after(dve, s + "_stored", 16 * it)
                            nc.vector.tensor_copy(tab[:, j * 2 * D:(j + 1) * 2 * D], ps[:, 2 + j, D:3 * D])\
                                .then_inc(sem("block_ev"), 1)
                    blocks(dve, qkv)
                    dve.wait_ge(sem(s + "_q"), NB)
                    link(nc.vector.memset(acc[:, 0:NB * W3], 0.0))
                    att_dve(dve, e)
                    dve.wait_ge(sem("tile_added"), tiles0[e] + T)
                    a3 = acc[:, 0:NB * W3].rearrange("p (b w) -> p b w", w=W3)
                    den3 = small[:, 104:104 + NB * H3].rearrange("p (b a) -> p b a", a=H3)
                    link(nc.vector.tensor_scalar(den3, a3[:, :, D:W3], 1e-8, None, ALU.add))
                    link(nc.vector.reciprocal(den3, den3))
                    agg = a3[:, :, 0:D].rearrange("p b (a d) -> p b a d", d=HD)
                    link(nc.vector.tensor_tensor(agg, agg, bc(den3.unsqueeze(3), [P, NB, H3, HD]), ALU.mult))
                    link(nc.vector.tensor_tensor(emb3, emb3, a3[:, :, 0:D], ALU.add))
                    norm_dve(dve, nm, emb3, D, 1e-6, link)
                    link(nc.vector.tensor_tensor(emb3, emb3, bc(bias[:, 0, 0:D].unsqueeze(1), [P, NB, D]), ALU.mult))
                    link(nc.vector.tensor_tensor(emb3, emb3, bc(bias[:, 1, 0:D].unsqueeze(1), [P, NB, D]), ALU.add))
                    dve.sem_inc(sem(e + "_done"), 1)
                dve.wait_ge(sem("w4_loaded"), 32)

                def d4(it):
                    for j in range(5):
                        i = 5 * it + j
                        x_b = x_sb[:, bass.ds(i * C, C)]
                        after(dve, "block_out", first["d4"] + i + 1)
                        nc.vector.tensor_tensor(tab[:, j * C:(j + 1) * C], ps[:, 2 + j, 0:C], bias[:, 0, :], ALU.add)\
                            .then_inc(sem("d4_s"), 1)
                        after(dve, "d4_s", i + 1)
                        nc.vector.tensor_tensor(x_b, x_b, tab[:, j * C:(j + 1) * C], ALU.add).then_inc(sem("block_ev"), 1)
                blocks(dve, d4)
                dve.wait_ge(sem("block_ev"), first["d4"] + NB)
                norm_dve(dve, "n4", x3, C, 1e-5, link)
            dve.sem_inc(sem("x_done"), 1)

        @block_.tensor
        def _(pe):
            pe.wait_ge(sem("consts"), 7)
            sort_pe(pe, "gd")
            pe.wait_ge(sem("w0_loaded"), 16 * 7)
            for d in range(2):
                for k in range(2):
                    last = nc.tensor.matmul(ps[:, 2, (2 * d + k) * HEADS:(2 * d + k + 1) * HEADS],
                                            wring[0:F0, 1, 0, d * C + k * P:d * C + (k + 1) * P],
                                            wring[0:F0, 1, 1, 0:HEADS], start=True, stop=True)
            last.then_inc(sem("w0_scores"), 1)
            pe.wait_ge(sem("w0_done"), 1)
            dense_pe(pe, "d0", wring[:, 0, :, :])
            sort_pe(pe, "gs")
            pe.wait_ge(sem("e0_max"), 1)
            nc.tensor.transpose(ps[0:HEADS, 6, 0:P], small[:, 0:HEADS], ident[:, :]).then_inc(sem("e0_maxT"), 1)
            pe.wait_ge(sem("e0_diag"), 1)
            nc.tensor.matmul(ps[:, 7, 0:HEADS], ones[0:HEADS, :], small[0:HEADS, 16:16 + HEADS], start=True, stop=True)\
                .then_inc(sem("e0_maxB"), 1)
            W0 = HEADS * F0 + HEADS

            def e0b(n, h):
                after(pe, "tile_onehot", groups0["e0b"] + n + 1)
                after(pe, "e0b_msg", n + 1)
                after(pe, "e0b_p", n + 1)
                for k in range(G):
                    sum_tile(pe, "e0b", n, h, k, G * (h % 2), 2 * G, W0, msgA[:, h, k, 0:W0])
            groups(pe, e0b)
            if layers > 1:
                pe.wait_ge(sem("w1_loaded"), 16 * 4)
                dense_pe(pe, "d1", wring[:, 0, :, :])
                pe.wait_ge(sem("ones_col"), 1)
                sum_pe(pe, "e1", C + 1)
            if layers > 2:
                pe.wait_ge(sem("w2_loaded"), 16 * 3)
                dense_pe(pe, "d2", wring[:, 0, :, :])
                pe.wait_ge(sem("d2_done"), 1)

                def pairs(q, s):
                    after(pe, f"pf_w{s}", 32 * (q - s) + 64)
                    for m in range(NB):
                        after(pe, "pf_ev", NB * q + m - 4)
                        for k in range(2):
                            last = nc.tensor.matmul(ps[:, m % 5, :], xt_all[:, k, m * P:(m + 1) * P],
                                                    wring[:, s, k, :], start=(k == 0), stop=(k == 1))
                        last.then_inc(sem("pf_mm"), 1)
                pairs(0, 0)
                pairs(1, 1)
                with pe.Fori(2, PAIRS - 1, 2) as q0:
                    pairs(q0, 0)
                    pairs(q0 + 1, 1)
                pe.wait_ge(sem("pf_ev"), NB * PAIRS)

                def pb(m, q):
                    if isinstance(m, int) and m == 0 and q == 0:
                        pe.wait_ge(sem("pb_loaded"), 16 * (1 + 2 * PAIRS))
                    if q == 0:
                        after(pe, "pb_xt", m + 1)
                    after(pe, "pb_ev", m * PAIRS + q - 3)
                    for k in range(2):
                        last = nc.tensor.matmul(ps[:, 4 + q % 4, :], xts[:, 0, k * P:(k + 1) * P], rel_res[2 * q + k],
                                                start=(k == 0), stop=(k == 1))
                    last.then_inc(sem("pb_mm"), 1)
                sum_pe(pe, "e2f", C, lambda eng, body: groups_beside(eng, body, pb))
                pe.wait_ge(sem("e2f_done"), 1)
                sum_pe(pe, "e2b", C + 1)
            if layers > 3:
                pe.wait_ge(sem("w3_loaded"), 16 * 4)
                dense_pe(pe, "d3", wring[:, 0, :, :])
                for s, e in (("da", "e3a"), ("db", "e3b")):
                    pe.wait_ge(sem(s + "_loaded"), 16 * 5)
                    dense_pe(pe, s, wring[:, 0, :, :])
                    pe.wait_ge(sem(s + "_q"), NB)
                    att_pe(pe, e)
                pe.wait_ge(sem("w4_loaded"), 32)
                dense_pe(pe, "d4", wring[:, 0, :, :])


def kernel(x, src, dst, edge_attr_2, edge_type_16, L0_gnn_W_forward, L0_gnn_W_reverse, L0_gnn_attn_forward,
           L1_gnn_W_self, L1_gnn_W_neigh, L2_gnn_Wf, L2_gnn_Wb, L2_gnn_loop_weight, L2_gnn_forward_bias,
           L2_gnn_backward_bias, L2_gnn_self_bias, L3_gnn_W_P_w, L3_gnn_W_P_b, L3_gnn_W_pos, L3_gnn_q1, L3_gnn_k1,
           L3_gnn_v1, L3_gnn_ln1_s, L3_gnn_ln1_b, L3_gnn_q2, L3_gnn_k2, L3_gnn_v2, L3_gnn_ln2_s, L3_gnn_ln2_b,
           L3_gnn_inv_w, L3_gnn_inv_b):
    import numpy as np
    import concourse.bacc as bacc
    from concourse import mybir
    from concourse.bass_utils import run_bass_kernel_spmd

    arrays = host_arrays(x, src, dst, edge_attr_2, edge_type_16, L0_gnn_W_forward, L0_gnn_W_reverse, L0_gnn_attn_forward,
                         L1_gnn_W_self, L1_gnn_W_neigh, L2_gnn_Wf, L2_gnn_Wb, L2_gnn_loop_weight, L2_gnn_forward_bias,
                         L2_gnn_backward_bias, L2_gnn_self_bias, L3_gnn_W_P_w, L3_gnn_W_P_b, L3_gnn_W_pos, L3_gnn_q1,
                         L3_gnn_k1, L3_gnn_v1, L3_gnn_ln1_s, L3_gnn_ln1_b, L3_gnn_q2, L3_gnn_k2, L3_gnn_v2, L3_gnn_ln2_s,
                         L3_gnn_ln2_b, L3_gnn_inv_w, L3_gnn_inv_b)
    nc = bacc.Bacc("TRN2", target_bir_lowering=False, num_devices=1)
    named = {f"in_{name}": a for name, a in arrays.items()}
    ins = {name: nc.dram_tensor(f"in_{name}", a.shape, mybir.dt.from_np(a.dtype), kind="ExternalInput").ap()
           for name, a in arrays.items()}
    out = nc.dram_tensor("out_0", (3125, 256), mybir.dt.float32, kind="ExternalOutput").ap()
    gnn_program(nc, **ins, out=out)
    r = run_bass_kernel_spmd(nc, [named], core_ids=[0])
    return r.results[0]["out_0"]


def host_arrays(x, src, dst, attr, etype, wf, wr, attn, w_self, w_neigh, rel_f, rel_b, loop_w, bias_f, bias_b, bias_self,
                wp, wp_b, w_pos, q1, k1, v1, ln1_s, ln1_b, q2, k2, v2, ln2_s, ln2_b, inv_w, inv_b):
    import numpy as np

    def tail(a, n, value):
        a = np.asarray(a)
        return np.concatenate([a, np.full((n,) + a.shape[1:], value, a.dtype)])

    nodes, edges = np.asarray(x).shape[0], np.asarray(src).shape[0]
    more_n, more_e = -nodes % 128, -edges % (128 * 26)
    padded = nodes + more_n
    arrays = dict(x=tail(x, more_n, 0), src=tail(src, more_e, padded), dst=tail(dst, more_e, padded),
                  etype=tail(etype, more_e, 0), attr=tail(attr, more_e, 0), wf=wf, wr=wr,
                  wft=np.transpose(np.asarray(wf)), wrt=np.transpose(np.asarray(wr)),
                  attnt=np.transpose(np.asarray(attn)[0]), w_self=w_self, w_neigh=w_neigh, rel_f=rel_f, rel_b=rel_b,
                  loop_w=loop_w, bias_f=bias_f, bias_b=bias_b, bias_self=bias_self, wp=wp, wp_b=wp_b,
                  w_pos=np.asarray(w_pos).reshape(-1), q1=q1, k1=k1, v1=v1, ln1_s=ln1_s, ln1_b=ln1_b, q2=q2, k2=k2, v2=v2,
                  ln2_s=ln2_s, ln2_b=ln2_b, inv_w=inv_w, inv_b=inv_b)
    return {name: np.ascontiguousarray(a) for name, a in arrays.items()}
```

```python
from contextlib import ExitStack

import concourse.bass as bass
from concourse import mybir


def gnn_program(nc, x, src, dst, src_real, etype, attr, wf, wr, wft, wrt, attnt, w_self, w_neigh, rel_f, rel_b, loop_w,
                bias_f, bias_b, bias_self, wp, wp_b, w_pos, q1, k1, v1, ln1_s, ln1_b, q2, k2, v2, ln2_s, ln2_b,
                inv_w, inv_b, out, layers=4):
    f32, i32 = mybir.dt.float32, mybir.dt.int32
    ALU, ACT, AX = mybir.AluOpType, mybir.ActivationFunctionType, mybir.AxisListType
    P = 128
    N, C = 3125, 256
    NP = x.shape[0]
    NB = NP // P
    EP = src.shape[0]
    EC = EP // P
    BINS = NB + 1
    G = 4
    R = 4
    T = -(-(EC + NB) // (G * R)) * G * R
    NG = T // G
    TP = T + 1
    HEADS, F0 = 4, 64
    HEADS_DVE = 2
    ROW0 = F0 + HEADS
    MAXK = 32
    RELS = rel_f.shape[0]
    D, H3 = 128, 8
    HD = D // H3
    W3 = D + H3
    FAR = 40.0
    SC_EDGES = 13
    KD, KS = 5, 3
    OFF = T * P
    LOWEST = -3.4028234663852886e38

    ctx = ExitStack()
    with ctx:
        def sb(name, shape, dt=f32):
            return ctx.enter_context(nc.sbuf_tensor(name, shape, dt))

        def dram(name, shape):
            return nc.dram_tensor(name, shape, f32).ap()

        sems = {}

        def sem(name):
            if name not in sems:
                sems[name] = ctx.enter_context(nc.semaphore(name))
            return sems[name]

        def after(eng, name, value):
            if not (isinstance(value, int) and value <= 0):
                eng.wait_ge(sem(name), value)

        def groups(eng, body):
            for n in range(R):
                body(n, n % R)
            with eng.Fori(R, NG - 2 * R + 1, R) as n0:
                for h in range(R):
                    body(n0 + h, h)
            for n in range(NG - R, NG):
                body(n, n % R)

        PAIRS = RELS // 2

        def groups_beside(eng, body, unit):
            assert NG == PAIRS * (NB + 1)
            for n in range(PAIRS):
                body(n, n % R)
            for j in range(PAIRS):
                body(PAIRS + j, j % R)
                unit(0, j)
            with eng.Fori(2, NB + 1) as i:
                for j in range(PAIRS):
                    body(i * PAIRS + j, j % R)
                    unit(i - 1, j)

        x_sb = sb("x_sb", [P, NB * C])
        slots_d = sb("slots_d", [P, TP * KD])
        slots_s = sb("slots_s", [P, TP * KS])
        block_d = sb("block_d", [1, T], i32)
        block_s = sb("block_s", [1, T], i32)
        gidx = sb("gidx", [P, R, G], i32)
        rows = sb("rows", [P, R * G, 264])
        onehot = sb("onehot", [P, R, G, P])
        msg = sb("msg", [P, R * G * 264])
        acc = sb("acc", [P, 6600])
        big1 = sb("big1", [P, NB * C])
        big2 = sb("big2", [P, NB * C])
        wring = sb("wring", [P, 2, 2, 512])
        xs = sb("xs", [P, 5, 256])
        xts = sb("xts", [P, 5, 256])
        bias = sb("bias", [P, 2, 256])
        iota_i = sb("iota_i", [P, P], i32)
        iota = sb("iota", [P, P])
        ident = sb("ident", [P, P])
        ones = sb("ones", [P, P])
        tri = sb("tri", [P, P])
        cnt = sb("cnt", [P, 32])
        base = sb("base", [P, 32])
        tiles_i = sb("tiles_i", [P, 32], i32)
        tiles_f = sb("tiles_f", [P, 32])
        incl = sb("incl", [P, 32])
        tend = sb("tend", [P, 4])
        tend_i = sb("tend_i", [P, 1], i32)
        stage = sb("stage", [P, 2, SC_EDGES * KD])
        stage_row = sb("stage_row", [P, 2, SC_EDGES], i32)
        small = sb("small", [P, 3 * 104])
        top8 = sb("top8", [P, 4, 8])
        unsorted = sb("unsorted", [1, 4], i32)
        in_order = sb("in_order", [1, 4])
        again = sb("again", [1, 4], i32)
        att = sb("att", [P, 3, G * H3])
        max0 = sb("max0", [P, R * G * HEADS])
        ps = ctx.enter_context(nc.psum_tensor("ps", [P, 8, 512], f32))

        recs_d = dram("recs_d", [OFF + P * TP, KD])
        slots_s_dram = dram("slots_s_dram", [P * TP, KS])
        table0 = dram("table0", [NP, 2 * ROW0])
        table1 = dram("table1", [NP, C])
        table2f = dram("table2f", [RELS * NP, C])
        table2b = dram("table2b", [RELS * NP, C])
        table3 = [dram("table3a", [NP, 2 * D]), dram("table3b", [NP, 2 * D])]

        x3 = x_sb[:, :].rearrange("p (b c) -> p b c", c=C)
        sd3 = slots_d[:, :].rearrange("p (t w) -> p t w", w=KD)
        ss3 = slots_s[:, :].rearrange("p (t w) -> p t w", w=KS)
        key_i = acc[:, 0:EC].bitcast(i32)
        kb_i = acc[:, EC:2 * EC].bitcast(i32)
        other_i = acc[:, 3 * EC:4 * EC].bitcast(i32)
        etype_i = acc[:, 4 * EC:5 * EC].bitcast(i32)
        prod = acc[:, 5 * EC:6 * EC]
        ms0 = big2[:, 0:R * G * ROW0].rearrange("p (r g w) -> p r g w", r=R, g=G)
        lin0 = big2[:, R * G * ROW0:2 * R * G * ROW0].rearrange("p (r g w) -> p r g w", r=R, g=G)
        MS0 = 2 * R * G * ROW0
        scratch = {"gd": [acc[:, i * EC:(i + 1) * EC] for i in (2, 3, 4, 6)],
                   "gs": [big2[:, MS0 + i * EC:MS0 + (i + 1) * EC] for i in range(4)]}
        attr_sb = rows[:, :, :].rearrange("p a b -> p (a b)")[:, 0:2 * EC]
        rec_d = big2[:, 0:EC * KD]
        row_d = big2[:, EC * KD:EC * (KD + 1)].bitcast(i32)
        rec_s = big1[:, 0:EC * KS]
        row_s = big1[:, EC * KS:EC * (KS + 1)].bitcast(i32)
        OWN = EC * (KS + 1)
        tile_block = big1[:, OWN:OWN + T]
        tile_first = big1[0:1, OWN + T:OWN + 2 * T].bitcast(i32)
        iota_t_i = big1[0:32, OWN + 2 * T:OWN + 3 * T].bitcast(i32)
        tile_ge = big1[0:32, OWN + 2 * T:OWN + 3 * T]
        node_sc = big1[:, OWN + 3 * T:OWN + 3 * T + NB * 2 * HEADS].rearrange("p (b w a) -> p b w a", w=2, a=HEADS)
        iota_t = slots_s[0:32, 0:T]
        rec_s2, row_s2 = msg[:, 0:EC * KS], msg[:, EC * KS:EC * (KS + 1)].bitcast(i32)
        sc0 = att[:, :, :].rearrange("p a b -> p (a b)")[:, 0:R * G * HEADS].rearrange("p (r w) -> p r w", r=R)
        low = small[:, 236:240]
        ranges = small[:, 240:244]
        shift = small[:, 244:248]
        under = small[:, 248:252]
        eps0 = small[:, 252:256]
        raw0 = small[:, 272:272 + G * HEADS]
        first_src = small[:, 296:297].bitcast(i32)
        first_attr = small[:, 297:299]
        next_i = small[0:P - 1, 300:301].bitcast(i32)
        next_f = small[0:P - 1, 301:302]
        falls = small[:, 302:304]
        msgA = msg[:, :].rearrange("p (r g w) -> p r g w", r=R, g=G)
        res3 = msg[:, 0:R * G * W3].rearrange("p (r g w) -> p r g w", r=R, g=G)
        oneT = msg[:, R * G * W3:R * G * (W3 + P)].rearrange("p (r g w) -> p r g w", r=R, g=G)
        qk3 = big1[:, 0:R * G * D].rearrange("p (r g w) -> p r g w", r=R, g=G)
        rows4 = rows[:, :, :].rearrange("p (r g) w -> p r g w", g=G)
        emb = big2[:, 0:NB * D]
        q_sb = acc[:, NB * W3:NB * (W3 + D)]
        tab1 = acc[:, 0:5 * 512]
        tab = big2[:, NB * D:NB * D + 5 * 512]
        tab0 = msg[:, 0:NB * 2 * ROW0]
        xt_all = big1[:, :].rearrange("p (k n) -> p k n", k=2)
        rel_res = [big2[:, i * 512:(i + 1) * 512] for i in range(12)] + [msg[:, i * 512:(i + 1) * 512] for i in range(4)]
        pb_ring = msg[:, 4 * 512:8 * 512].rearrange("p (s w) -> p s w", s=4)
        projtab = big2[:, 0:2 * 5 * 512].rearrange("p (s j w) -> p s j w", s=2, j=5)

        def bc(ap, shape):
            return ap.to_broadcast(shape)

        STAGES, AGAIN = ["e0", "e1", "e2f", "e2b", "e3a", "e3b"], "e0x"
        turn = {s: n for n, s in enumerate(STAGES)} | {AGAIN: 0}
        groups0 = {s: NG * n for s, n in turn.items()}
        tiles0 = {s: T * n for s, n in turn.items()}

        def of(s, name):
            return name + "_again" if s == AGAIN else name

        def gathered(s, n, h):
            return 16 * G * (NG // R) * turn[s] + (16 * G // R) * (n - h) + 16 * G

        def stage_index(act, s, slots, words, word):
            def body(n, h):
                after(act, "tile_sum", tiles0[s] + G * (n - R + 1))
                src_ap = slots[:, bass.ds(n * (G * words), G * words)].rearrange("p (t w) -> p t w", w=words)
                nc.scalar.activation(gidx[:, h, :], src_ap[:, :, word], ACT.Copy).then_inc(sem("row_numbers"), 1)
            return body

        def gather_loop(pool, s, table, width):
            def body(n, h):
                after(pool, of(s, "row_numbers"), groups0[s] + n + 1)
                pool.nop(nofuse=True)
                for k in range(G):
                    j = h * G + k
                    nc.gpsimd.indirect_dma_start(
                        out=rows[:, j, 0:width], out_offset=None, in_=table[:, :],
                        in_offset=bass.IndirectOffsetOnAxis(ap=gidx[:, h, k:k + 1], axis=0),
                    ).then_inc(sem(of(s, f"rows_ready{h}")), 16)
            groups(pool, body)

        def one_hot(dve, s, slots, words, n, h):
            loc = slots[:, bass.ds(n * (G * words), G * words)].rearrange("p (t w) -> p t w", w=words)[:, :, 2:3]
            nc.vector.tensor_tensor(onehot[:, h, :, :], bc(iota[:, :].unsqueeze(1), [P, G, P]),
                                    bc(loc, [P, G, P]), ALU.is_equal).then_inc(sem(of(s, "tile_onehot")), 1)

        def tile_blocks(block, n, engine):
            _, numbers = nc.values_load_multi_w_load_instructions(
                block[0:1, bass.ds(n * G, G)], engines=(engine,), min_val=0, max_val=NB - 1,
                skip_runtime_bounds_check_because="a count of blocks, cut off at NB - 1 when it was made")
            return numbers

        def adder(dve, s, block, n, bank, width, whole=False):
            of_tile = tile_blocks(block, n, mybir.EngineType.DVE)

            def add(k):
                b = of_tile[k]
                if not whole or k == 0:
                    after(dve, of(s, "tile_sum"), tiles0[s] + n * G + (G if whole else k + 1))
                after(dve, of(s, "tile_added"), tiles0[s] + n * G + k)
                nc.vector.tensor_tensor(acc[:, bass.ds(b * width, width)], acc[:, bass.ds(b * width, width)],
                                        ps[:, bank + k, 0:width], ALU.add).then_inc(sem(of(s, "tile_added")), 1)
            return add

        def add_tiles(dve, s, block, n, bank, width):
            add = adder(dve, s, block, n, bank, width)
            for k in range(G):
                add(k)

        def sum_tile(pe, s, n, h, k, bank, banks, width, rhs):
            after(pe, of(s, "tile_added"), tiles0[s] + n * G + k - banks + 1)
            nc.tensor.matmul(ps[:, bank + k, 0:width], onehot[:, h, k, :], rhs,
                             start=True, stop=True).then_inc(sem(of(s, "tile_sum")), 1)

        def sum_act(act, s, slots, words, word, loop=groups):
            loop(act, stage_index(act, s, slots, words, word))

        def sum_pe(pe, s, width, loop=groups):
            def body(n, h):
                after(pe, "tile_onehot", groups0[s] + n + 1)
                after(pe, f"rows_ready{h}", gathered(s, n, h))
                for k in range(G):
                    sum_tile(pe, s, n, h, k, 0, G, width, rows[:, h * G + k, 0:width])
            loop(pe, body)

        def sum_dve(dve, s, slots, words, block, width, loop=groups):
            def body(n, h):
                later = not isinstance(n, int) or n > 0
                if later:
                    add = adder(dve, s, block, n - 1, 0, width)
                    add(0)
                after(dve, "tile_sum", tiles0[s] + G * (n - R + 1))
                one_hot(dve, s, slots, words, n, h)
                if later:
                    for k in range(1, G):
                        add(k)
            loop(dve, body)
            add_tiles(dve, s, block, NG - 1, 0, width)

        DENSE = {"d0": (x_sb, 256, 2 * ROW0), "d1": (x_sb, 256, 512), "d2": (x_sb, 256, 256),
                 "d3": (x_sb, 256, D), "da": (emb, D, 3 * D), "db": (emb, D, 3 * D), "d4": (emb, D, C)}

        first = {s: NB * n for n, s in enumerate(DENSE)}

        def blocks(eng, body):
            body(0)
            with eng.Fori(1, NB // 5) as it:
                body(it)

        def dense_act(act, s):
            src_sb, width, _ = DENSE[s]

            def stage_block(it, j):
                nc.scalar.activation(xs[:, j, 0:width], src_sb[:, bass.ds((5 * it + j) * width, width)],
                                     ACT.Copy).then_inc(sem("block_xs"), 1)

            def body(it, more=True):
                for j in range(5):
                    after(act, "block_out", first[s] + 5 * it + j - 4)
                    if s == "d2":
                        after(act, "d2_xt_all", 5 * it + j - 4)
                    after(act, "block_tr", first[s] + 5 * it + j + 1)
                    nc.scalar.activation(xts[:, j, 0:width], ps[:, j % 2, 0:width], ACT.Copy)\
                        .then_inc(sem("block_xt"), 1)
                    if more:
                        stage_block(it + 1, j)
                if s == "d0":
                    for j in range(5):
                        after(act, "block_out", first[s] + 5 * it + j + 1)
                        nc.scalar.activation(
                            node_sc[:, bass.ds(5 * it + j, 1), :, :].rearrange("p b w a -> p (b w) a"),
                            ps[:, 2 + j, 0:2 * ROW0].rearrange("p (w c) -> p w c", w=2)[:, :, F0:ROW0], ACT.Copy)\
                            .then_inc(sem("d0_sc"), 1)
                        nc.scalar.activation(tab0[:, bass.ds((5 * it + j) * (2 * ROW0), 2 * ROW0)], ps[:, 2 + j, 0:2 * ROW0],
                                             ACT.Copy).then_inc(sem("block_ev"), 1)
            after(act, "block_tr", first[s])
            for j in range(5):
                stage_block(0, j)
            body(0)
            with act.Fori(1, NB // 5 - 1) as it:
                body(it)
            body(NB // 5 - 1, more=False)

        def dense_pe(pe, s, weights):
            _, width, wide = DENSE[s]
            kin = width // P

            def product(it, j):
                after(pe, "block_xt", first[s] + 5 * it + j + 1)
                after(pe, "block_ev", first[s] + 5 * it + j - 4)
                for k in range(kin):
                    last = nc.tensor.matmul(ps[:, 2 + j, 0:wide], xts[:, j, k * P:(k + 1) * P],
                                            weights[:, k, 0:wide], start=(k == 0), stop=(k == kin - 1))
                last.then_inc(sem("block_out"), 1)

            def body(it):
                for j in range(5):
                    after(pe, "block_xs", first[s] + 5 * it + j + 1)
                    after(pe, "block_xt", first[s] + 5 * it + j - (1 if j else 0))
                    for k in range(kin):
                        last = nc.tensor.transpose(ps[:, j % 2, k * P:(k + 1) * P], xs[:, j, k * P:(k + 1) * P],
                                                   ident[:, :])
                    last.then_inc(sem("block_tr"), 1)
                    if j:
                        product(it, j - 1)
                product(it, 4)
            blocks(pe, body)

        def table_store(sp, s, table, width, tab, whole):
            def body(it):
                after(sp, "block_ev", first[s] + 5 * it + 5)
                rows_of = tab[:, bass.ds(it * (5 * width), 5 * width)] if whole else tab[:, 0:5 * width]
                sp.dma_start(table[bass.ds(it * (5 * P), 5 * P), :].rearrange("(j p) w -> p j w", p=P),
                             rows_of.rearrange("p (j w) -> p j w", w=width)).then_inc(sem(s + "_stored"), 16)
            blocks(sp, body)

        TABLE_STORED = 16 * (NB // 5)

        ORDERS = {"gd": (dst, src_real, slots_d, KD, rec_d, row_d, block_d), "gs": (src, dst, slots_s, KS, rec_s, row_s, block_s)}

        def sort_keys(dve, o, link):
            _, _, slots, words, rec, rowno, block = ORDERS[o]
            r3 = rec.rearrange("p (f w) -> p f w", w=words)
            kbf, mask, scan, rank = scratch[o]
            dve.wait_ge(sem(o + "_loaded"), 16 * (5 if o == "gd" else 3))
            link(nc.vector.tensor_scalar(kb_i, key_i, 7, None, ALU.logical_shift_right))
            if o == "gd":
                nc.vector.tensor_copy(r3[:, :, 3:5], attr_sb.rearrange("p (f w) -> p f w", w=2))
            else:
                link(nc.vector.tensor_scalar(key_i, key_i, P - 1, None, ALU.bitwise_and))
            nc.vector.tensor_copy(r3[:, :, 2], key_i)
            nc.vector.tensor_copy(r3[:, :, 0], other_i)
            nc.vector.scalar_tensor_tensor(r3[:, :, 1], etype_i, float(NP), other_i, ALU.mult, ALU.add)\
                .then_inc(sem(o + "_records"), 1)
            link(nc.vector.memset(rank, 0.0))
            link(nc.vector.tensor_copy(kbf, kb_i))

        def count_bin(dve, o, b):
            kbf, mask, scan, rank = scratch[o]
            nc.vector.tensor_scalar(mask, kbf, iota[:, bass.ds(b, 1)], 0.0, ALU.is_equal, ALU.add,
                                    accum_out=cnt[:, bass.ds(b, 1)]).then_inc(sem(o + "_count"), 1)
            dve.wait_ge(sem(o + "_count"), b + 1)

        def rank_bin(dve, o, b, columns, steps):
            kbf, mask, scan, rank = [a[:, columns] for a in scratch[o]]
            nc.vector.tensor_scalar(mask, kbf, iota[:, bass.ds(b, 1)], 0.0, ALU.is_equal, ALU.add,
                                    accum_out=cnt[:, bass.ds(b, 1)]).then_inc(steps, 1)
            dve.wait_ge(steps, b * 4 + 1)
            nc.vector.tensor_tensor_scan(scan, mask, mask, 0.0, ALU.add, ALU.max).then_inc(steps, 1)
            dve.wait_ge(steps, b * 4 + 2)
            nc.vector.scalar_tensor_tensor(scan, scan, base[:, bass.ds(b, 1)], mask, ALU.add, ALU.mult).then_inc(steps, 1)
            dve.wait_ge(steps, b * 4 + 3)
            nc.vector.tensor_tensor(rank, rank, scan, ALU.add).then_inc(steps, 1)
            dve.wait_ge(steps, b * 4 + 4)

        def place_rows(dve, columns, rows_out, link):
            _, pos, pos_c, rank = [a[:, columns] for a in scratch["gs"]]
            pos, pos_c = pos.bitcast(i32), pos_c.bitcast(i32)
            link(nc.vector.tensor_copy(pos, rank))
            link(nc.vector.tensor_scalar(pos_c, pos, 7, None, ALU.logical_shift_right))
            link(nc.vector.tensor_scalar(pos, pos, P - 1, None, ALU.bitwise_and))
            link(nc.vector.scalar_tensor_tensor(rows_out[:, columns], pos, float(TP), pos_c, ALU.mult, ALU.add))
            dve.sem_inc(sem("gs_rows"), 1)

        TOTAL, BEFORE, COLUMN, FALLS = 0, 32, 64, 80

        def sort_tiles(dve, o, link):
            _, _, slots, words, rec, rowno, block = ORDERS[o]
            dve.sem_inc(sem(o + "_counted"), 1)
            dve.wait_ge(sem(o + "_totals"), 1)
            for tot, width, ti, tf in ((ps[0:BINS, 0, COLUMN:COLUMN + 1], 1, tend_i, tend),
                                       (ps[:, 0, TOTAL:TOTAL + BINS], BINS, tiles_i, tiles_f)):
                p = tot.shape[0]
                link(nc.vector.tensor_scalar(tf[0:p, 0:width], tot, float(P - 1), None, ALU.add))
                link(nc.vector.tensor_copy(ti[0:p, 0:width], tf[0:p, 0:width]))
                link(nc.vector.tensor_scalar(ti[0:p, 0:width], ti[0:p, 0:width], 7, None, ALU.logical_shift_right))
                link(nc.vector.tensor_copy(tf[0:p, 0:width], ti[0:p, 0:width]))
                if width == 1:
                    link(nc.vector.scalar_tensor_tensor(tend[0:NB, 2:3], tend[0:NB, 0:1], -float(P),
                                                        ps[0:NB, 0, COLUMN:COLUMN + 1], ALU.mult, ALU.add))
                    dve.sem_inc(sem(o + "_tiles"), 1)
            link(nc.vector.tensor_tensor_scan(incl[:, 0:NB], tiles_f[:, 0:NB], tiles_f[:, 0:NB], 0.0, ALU.add, ALU.max))
            link(nc.vector.tensor_tensor(base[:, 0:NB], incl[:, 0:NB], tiles_f[:, 0:NB], ALU.subtract))
            after_tiles = float(OFF) if o == "gd" else 0.0
            link(nc.vector.tensor_scalar(base[:, 0:NB], base[:, 0:NB], float(P), after_tiles - 1.0, ALU.mult, ALU.add))
            link(nc.vector.memset(base[:, NB:BINS], float(T * P) + after_tiles - 1.0))
            link(nc.vector.tensor_tensor(base[:, 0:BINS], base[:, 0:BINS], ps[:, 0, BEFORE:BEFORE + BINS], ALU.add))
            dve.wait_ge(sem(o + "_tends"), 1)
            link(nc.vector.tensor_tensor(tend[0:NB, 1:2], tend[0:NB, 0:1], ps[0:NB, 1, 0:1], ALU.add))
            nc.vector.tensor_scalar(tile_ge[0:NB - 1, :], iota_t[0:NB - 1, :], tend[0:NB - 1, 1:2], None, ALU.is_ge)\
                .then_inc(sem(o + "_ge"), 1)
            dve.wait_ge(sem(o + "_blocks"), 1)
            for half in range(2):
                part = slice(half * (T // 2), (half + 1) * (T // 2))
                link(nc.vector.tensor_copy(block[0:1, part], ps[0:1, 4 + half, 0:T // 2]))
                if o == "gd":
                    link(nc.vector.tensor_scalar(tile_block[:, part], ps[:, 4 + half, 0:T // 2], float(P), None, ALU.mult))

        def sort_pe(pe, o):
            pe.wait_ge(sem(o + "_counted"), 1)
            nc.tensor.matmul(ps[:, 0, TOTAL:TOTAL + BINS], ones[:, :], cnt[:, 0:BINS], start=True, stop=True)
            nc.tensor.matmul(ps[:, 0, BEFORE:BEFORE + BINS], tri[:, :], cnt[:, 0:BINS], start=True, stop=True)
            if o == "gd":
                nc.tensor.matmul(ps[0:1, 0, FALLS:FALLS + 1], falls[:, 0:1], ones[:, 0:1], start=True, stop=True)
            nc.tensor.matmul(ps[0:BINS, 0, COLUMN:COLUMN + 1], cnt[:, 0:BINS], ones[:, 0:1], start=True, stop=True)\
                .then_inc(sem(o + "_totals"), 1)
            pe.wait_ge(sem(o + "_tiles"), 1)
            nc.tensor.matmul(ps[0:NB, 1, 0:1], tri[0:NB, 0:NB], tend[0:NB, 0:1], start=True, stop=True)\
                .then_inc(sem(o + "_tends"), 1)
            pe.wait_ge(sem(o + "_ge"), 1)
            for half in range(2):
                ge = tile_ge[0:NB - 1, half * (T // 2):(half + 1) * (T // 2)]
                last = nc.tensor.matmul(ps[:, 4 + half, 0:T // 2], ones[0:NB - 1, :], ge, start=True, stop=True)
                if o == "gd":
                    last = nc.tensor.matmul(ps[0:1, 6 + half, 0:T // 2], tend[0:NB - 1, 2:3], ge, start=True, stop=True)
            last.then_inc(sem(o + "_blocks"), 1)

        NS = EC // SC_EDGES
        NS_EARLY = 16
        EARLY, LATE = slice(0, NS_EARLY * SC_EDGES), slice(NS_EARLY * SC_EDGES, EC)

        def scatter(pool, o, dram_slots, rec, rowno, first, end):
            words = ORDERS[o][3]

            def body(n, h):
                after(pool, f"{o}_placed{h}", SC_EDGES * 8 * (n - h))
                nc.gpsimd.tensor_copy(stage[:, h, 0:SC_EDGES * words],
                                      rec[:, bass.ds(n * (SC_EDGES * words), SC_EDGES * words)])\
                    .then_inc(sem(o + "_staged"), 1)
                nc.gpsimd.tensor_copy(stage_row[:, h, :], rowno[:, bass.ds(n * SC_EDGES, SC_EDGES)])\
                    .then_inc(sem(o + "_staged"), 1)
                pool.wait_ge(sem(o + "_staged"), 2 * n + 2)
                pool.nop(nofuse=True)
                for k in range(SC_EDGES):
                    nc.gpsimd.indirect_dma_start(
                        out=dram_slots[:, :], out_offset=bass.IndirectOffsetOnAxis(ap=stage_row[:, h, k:k + 1], axis=0),
                        in_=stage[:, h, k * words:(k + 1) * words], in_offset=None,
                    ).then_inc(sem(f"{o}_placed{h}"), 16)
            if first == 0:
                body(0, 0)
                body(1, 1)
            with pool.Fori(max(first, 2), end - 1, 2) as n0:
                body(n0, 0)
                body(n0 + 1, 1)

        def slots_load(sp, o, dram_slots):
            _, _, slots, words, _, _, _ = ORDERS[o]
            for h in range(2):
                sp.wait_ge(sem(f"{o}_placed{h}"), SC_EDGES * 8 * NS)
            sp.dma_start(slots[:, :], dram_slots.rearrange("(p t) w -> p (t w)", p=P)).then_inc(sem(o + "_slots"), 16)

        ALL_MAX = {"ranges": 1, "bound": 2, "top": 3}

        def all_max_dve(dve, name, out, link):
            dve.sem_inc(sem("all_max"), 1)
            dve.wait_ge(sem("all_max_rows"), ALL_MAX[name])
            link(nc.vector.tensor_reduce(small[0:HEADS, 8:9], ps[0:HEADS, 7, 0:P], AX.X, ALU.max))
            link(nc.vector.tensor_scalar(small[0:HEADS, 16:16 + HEADS], ident[0:HEADS, 0:HEADS], small[0:HEADS, 8:9], None, ALU.mult))
            dve.sem_inc(sem("all_max_diag"), 1)
            dve.wait_ge(sem("all_max_all"), ALL_MAX[name])
            link(nc.vector.tensor_copy(out, ps[:, 7, P:P + HEADS]))

        def all_max_pe(pe, name):
            pe.wait_ge(sem("all_max"), ALL_MAX[name])
            nc.tensor.transpose(ps[0:HEADS, 7, 0:P], small[:, 0:HEADS], ident[:, :]).then_inc(sem("all_max_rows"), 1)
            pe.wait_ge(sem("all_max_diag"), ALL_MAX[name])
            nc.tensor.matmul(ps[:, 7, P:P + HEADS], ones[0:HEADS, :], small[0:HEADS, 16:16 + HEADS], start=True, stop=True)\
                .then_inc(sem("all_max_all"), 1)

        W0 = HEADS * F0 + HEADS

        def e0_act(act, s):
            def index(n, h):
                after(act, of(s, "e0_ms"), n - R + 1)
                if s == "e0":
                    after(act, f"records_loaded{h}", (16 * G // R) * (n - h) + 16 * G)
                src_ap = slots_d[:, bass.ds(n * (G * KD), G * KD)].rearrange("p (t w) -> p t w", w=KD)
                nc.scalar.activation(gidx[:, h, :], src_ap[:, :, 0], ACT.Copy).then_inc(sem(of(s, "row_numbers")), 1)

            def reverse(n, h):
                after(act, of(s, "e0_ms"), n - R + 1)
                after(act, of(s, f"rows_ready{h}"), gathered(s, n, h))
                for k in range(G):
                    last = nc.scalar.activation(lin0[:, h, k, :], rows4[:, h, k, ROW0:2 * ROW0], ACT.Copy,
                                                scale=slots_d[:, bass.ds(n * (G * KD) + (k * KD + 4), 1)])
                last.then_inc(sem(of(s, "e0_reverse")), 1)

            def exponents(n, h):
                after(act, of(s, "e0_scores"), n + 1)
                after(act, of(s, "tile_sum"), G * (n - R + 1))
                nc.scalar.activation(msgA[:, h, :, HEADS * F0:W0], sc0[:, h, :].rearrange("p (g a) -> p g a", a=HEADS),
                                     ACT.Exp).then_inc(sem(of(s, "e0_p")), 1)
                after(act, of(s, "e0_p"), n + 1)
                for k in range(G):
                    for a in range(HEADS_DVE, HEADS):
                        last = nc.scalar.activation(msgA[:, h, k, a * F0:(a + 1) * F0], ms0[:, h, k, 0:F0], ACT.Copy,
                                                    scale=msgA[:, h, k, HEADS * F0 + a:HEADS * F0 + a + 1])
                last.then_inc(sem(of(s, "e0_weighted_act")), 1)

            def step(n, h, left):
                if left > 3:
                    index(n + 3, (h + 3) % R)
                if left > 1:
                    reverse(n + 1, (h + 1) % R)
                exponents(n, h)
            for n in range(3):
                index(n, n)
            reverse(0, 0)
            att_groups(act, step)

        def e0_sums(pe, s):
            def body(n, h):
                after(pe, of(s, "tile_onehot"), n + 1)
                after(pe, of(s, "e0_weighted"), n + 1)
                after(pe, of(s, "e0_weighted_act"), n + 1)
                for k in range(G):
                    sum_tile(pe, s, n, h, k, G * (h % 2), 2 * G, W0, msgA[:, h, k, 0:W0])
            return body

        def e0_dve(dve, s):
            def weighted(n, h):
                after(dve, of(s, "e0_p"), n + 1)
                nc.vector.tensor_tensor(
                    msgA[:, h, :, 0:HEADS_DVE * F0].rearrange("p g (a f) -> p g a f", f=F0),
                    bc(ms0[:, h, :, 0:F0].unsqueeze(2), [P, G, HEADS_DVE, F0]),
                    bc(msgA[:, h, :, HEADS * F0:HEADS * F0 + HEADS_DVE].unsqueeze(3), [P, G, HEADS_DVE, F0]),
                    ALU.mult).then_inc(sem(of(s, "e0_weighted")), 1)

            def step(n, h):
                older = not isinstance(n, int) or n > 1
                add = adder(dve, s, block_d, n - 2, G * (h % 2), W0, whole=True) if older else lambda k: None
                if not isinstance(n, int) or n > 0:
                    weighted(n - 1, (h - 1) % R)
                after(dve, of(s, f"rows_ready{h}"), gathered(s, n, h))
                after(dve, of(s, "e0_weighted_act"), n - R + 1)
                rec = slots_d[:, bass.ds(n * (G * KD), G * KD)].rearrange("p (t w) -> p t w", w=KD)
                nc.vector.tensor_tensor(ms0[:, h, :, :], rows4[:, h, :, 0:ROW0], bc(rec[:, :, 3:4], [P, G, ROW0]), ALU.mult)\
                    .then_inc(sem(of(s, "e0_forward")), 1)
                add(0)
                after(dve, of(s, "e0_forward"), n + 1)
                after(dve, of(s, "e0_reverse"), n + 1)
                nc.vector.tensor_tensor(ms0[:, h, :, :], ms0[:, h, :, :], lin0[:, h, :, :], ALU.add)\
                    .then_inc(sem(of(s, "e0_ms")), 1)
                if s == "e0":
                    nc.vector.tensor_tensor(rec[:, :, 2], rec[:, :, 2], tile_block[:, bass.ds(n * G, G)], ALU.subtract)
                after(dve, of(s, "e0_ms"), n + 1)
                own = ms0[:, h, :, F0:ROW0]
                raw = raw0.rearrange("p (g a) -> p g a", a=HEADS)
                nc.vector.scalar_tensor_tensor(raw, own, 0.2, own, ALU.mult, ALU.max).then_inc(sem(of(s, "e0_leaky")), 1)
                add(1)
                after(dve, of(s, "e0_leaky"), n + 1)
                nc.vector.tensor_tensor(sc0[:, h, :].rearrange("p (g a) -> p g a", a=HEADS), raw,
                                        bc(shift.unsqueeze(1), [P, G, HEADS]), ALU.subtract).then_inc(sem(of(s, "e0_scores")), 1)
                after(dve, of(s, "tile_sum"), G * (n - R + 1))
                places = bc(rec[:, :, 2:3], [P, G, P])
                heres = bc(iota[:, :].unsqueeze(1), [P, G, P])
                nc.vector.tensor_tensor(onehot[:, h, 0:G // 2, :], heres[:, 0:G // 2, :], places[:, 0:G // 2, :], ALU.is_equal)
                add(2)
                nc.vector.tensor_tensor(onehot[:, h, G // 2:G, :], heres[:, G // 2:G, :], places[:, G // 2:G, :], ALU.is_equal)\
                    .then_inc(sem(of(s, "tile_onehot")), 1)
                if h == R - 1:
                    after(dve, of(s, "e0_scores"), n + 1)
                    nc.vector.tensor_tensor(max0[:, :], max0[:, :], sc0.rearrange("p r w -> p (r w)"), ALU.max)\
                        .then_inc(sem(of(s, "e0_max")), 1)
                add(3)

            def finish():
                weighted(NG - 1, (NG - 1) % R)
                add_tiles(dve, s, block_d, NG - 2, 0, W0)
                add_tiles(dve, s, block_d, NG - 1, G, W0)
                dve.wait_ge(sem(of(s, "tile_added")), T)
                dve.wait_ge(sem(of(s, "e0_max")), NG // R)
            return step, finish

        NORMS = {s: n + 1 for n, s in enumerate(["n0", "n1", "n2", "n3a", "n3b", "n4"])}

        def norm_act(act, s):
            act.wait_ge(sem("norm_var"), NORMS[s])
            nc.scalar.activation(small[:, 32:32 + NB], small[:, 0:NB], ACT.Sqrt).then_inc(sem("norm_std"), 1)

        def norm_dve(dve, s, y, width, eps, link, scratch=big1):
            stats = scratch[:, 0:NB * 6].rearrange("p (b w) -> p b w", w=6)
            mean_var = scratch[:, NB * 6:NB * 8].rearrange("p (b w) -> p b w", w=2)
            for b in range(NB):
                last = nc.vector.bn_stats(stats[:, b, :], y[:, b, :])
            link(last)
            for b in range(NB):
                last = nc.vector.bn_aggr(mean_var[:, b, :], stats[:, b, :])
            link(last)
            nc.vector.tensor_scalar(small[:, 0:NB], mean_var[:, :, 1], eps, None, ALU.add).then_inc(sem("norm_var"), 1)
            dve.wait_ge(sem("norm_std"), NORMS[s])
            link(nc.vector.reciprocal(small[:, 96:96 + NB], small[:, 32:32 + NB]))
            for b in range(NB):
                last = nc.vector.tensor_scalar(y[:, b, :], y[:, b, :], mean_var[:, b, 0:1], small[:, 96 + b:97 + b],
                                               ALU.subtract, ALU.mult)
            link(last)

        ATTENTIONS = ["e3a", "e3b"]

        def att_groups(eng, step):
            for n in range(R):
                step(n, n, NG - n)
            with eng.Fori(R, NG - 2 * R + 1, R) as n0:
                for h in range(R):
                    step(n0 + h, h, NG)
            for n in range(NG - R, NG):
                step(n, n % R, NG - n)

        def att_act(act, s):
            start = NG * ATTENTIONS.index(s)

            def index(n, h):
                after(act, "att_res", start + n - R + 1)
                of = slots_s[:, bass.ds(n * (G * KS), G * KS)].rearrange("p (t w) -> p t w", w=KS)
                nc.scalar.activation(gidx[:, h, :], of[:, :, 0], ACT.Copy).then_inc(sem("row_numbers"), 1)

            def transposed(n, h):
                after(act, "att_tr", start + n + 1)
                nc.scalar.activation(oneT[:, h, :, :], ps[:, h % 2, :].rearrange("p (g e) -> p g e", g=G), ACT.Copy)\
                    .then_inc(sem("att_oneT"), 1)

            def exponents(n, h):
                after(act, "att_att", start + n + 1)
                after(act, "tile_sum", tiles0[s] + G * (n - R + 1))
                nc.scalar.activation(res3[:, h, :, D:W3], att[:, 1 + h % 2, :].rearrange("p (g a) -> p g a", a=H3),
                                     ACT.Exp).then_inc(sem("att_p"), 1)

            def step(n, h, left):
                if left > 3:
                    index(n + 3, (h + 3) % R)
                exponents(n, h)
                if left > 2:
                    transposed(n + 2, (h + 2) % R)
            for n in range(3):
                index(n, n)
            transposed(0, 0)
            transposed(1, 1)
            att_groups(act, step)

        def att_pe(pe, s):
            start = NG * ATTENTIONS.index(s)

            def transposes(n, h):
                after(pe, "tile_onehot", groups0[s] + n + 1)
                after(pe, "att_oneT", start + n - 1)
                for k in range(G):
                    last = nc.tensor.transpose(ps[:, h % 2, k * P:(k + 1) * P], onehot[:, h, k, :], ident[:, :])
                last.then_inc(sem("att_tr"), 1)

            def queries(n, h):
                after(pe, "att_oneT", start + n + 1)
                after(pe, "att_qk", start + n - 1)
                of_tile = tile_blocks(block_s, n, mybir.EngineType.PE)
                for k in range(G):
                    b = of_tile[k]
                    last = nc.tensor.matmul(ps[:, 2 + h % 2, k * D:(k + 1) * D], oneT[:, h, k, :],
                                            q_sb[:, bass.ds(b * D, D)], start=True, stop=True)
                last.then_inc(sem("att_q"), 1)

            def sums(n, h):
                after(pe, "att_res", start + n + 1)
                for k in range(G):
                    sum_tile(pe, s, n, h, k, 4, G, W3, res3[:, h, k, :])

            def step(n, h, left):
                if not isinstance(n, int) or n > 1:
                    sums(n - 2, (h - 2) % R)
                if left > 1:
                    queries(n + 1, (h + 1) % R)
                if left > 2:
                    transposes(n + 2, (h + 2) % R)
            transposes(0, 0)
            transposes(1, 1)
            queries(0, 0)
            att_groups(pe, step)
            sums(NG - 2, (NG - 2) % R)
            sums(NG - 1, (NG - 1) % R)

        def att_dve(dve, s):
            start = NG * ATTENTIONS.index(s)

            def step(n, h, left):
                older = not isinstance(n, int) or n > 1
                add = adder(dve, s, block_s, n - 2, 4, W3) if older else lambda k: None
                after(dve, "att_q", start + n + 1)
                after(dve, f"rows_ready{h}", gathered(s, n, h))
                nc.vector.tensor_tensor(qk3[:, h, :, :], ps[:, 2 + h % 2, :].rearrange("p (g d) -> p g d", d=D),
                                        rows4[:, h, :, 0:D], ALU.mult).then_inc(sem("att_qk"), 1)
                add(0)
                dve.wait_ge(sem("att_qk"), start + n + 1)
                nc.vector.tensor_reduce(att[:, 0, :], qk3[:, h, :, :].rearrange("p g (a d) -> p (g a) d", d=HD),
                                        AX.X, ALU.add).then_inc(sem("att_red"), 1)
                add(1)
                dve.wait_ge(sem("att_red"), start + n + 1)
                after(dve, "att_p", start + n - 1)
                nc.vector.tensor_scalar(att[:, 1 + h % 2, :], att[:, 0, :], 10.0, -10.0, ALU.min, ALU.max)\
                    .then_inc(sem("att_att"), 1)
                if left > 2:
                    after(dve, "tile_sum", tiles0[s] + G * (n - R + 3))
                    one_hot(dve, s, slots_s, KS, n + 2, (h + 2) % R)
                add(2)
                if not isinstance(n, int) or n > 0:
                    weighted(n - 1, (h - 1) % R)
                add(3)

            def weighted(n, h):
                after(dve, "att_p", start + n + 1)
                nc.vector.tensor_tensor(
                    res3[:, h, :, 0:D].rearrange("p g (a d) -> p g a d", d=HD),
                    rows4[:, h, :, D:2 * D].rearrange("p g (a d) -> p g a d", d=HD),
                    bc(res3[:, h, :, D:W3].unsqueeze(3), [P, G, H3, HD]), ALU.mult).then_inc(sem("att_res"), 1)
            one_hot(dve, s, slots_s, KS, 0, 0)
            one_hot(dve, s, slots_s, KS, 1, 1)
            att_groups(dve, step)
            weighted(NG - 1, (NG - 1) % R)
            add_tiles(dve, s, block_s, NG - 2, 4, W3)
            add_tiles(dve, s, block_s, NG - 1, 4, W3)

        block_ = ctx.enter_context(nc.Block())

        @block_.sync
        def _(sp):
            def edges(a):
                return a.rearrange("(p f) -> p f", p=P)

            def weight(dst_ap, src_ap, name):
                sp.dma_start(dst_ap, src_ap).then_inc(sem(name), 16)

            weight(key_i, edges(dst), "gd_loaded")
            with nc.allow_non_contiguous_dma(reason="one word a partition, once"):
                weight(next_i, edges(dst)[1:P, 0:1], "gd_loaded")
            weight(other_i, edges(src_real), "gd_loaded")
            weight(etype_i, edges(etype), "gd_loaded")
            weight(attr_sb, attr.rearrange("(p f) w -> p (f w)", p=P), "gd_loaded")
            weight(first_src, src_real.rearrange("(a n) -> a n", a=1)[0:1, 0:1].partition_broadcast(P), "first_edge")
            weight(first_attr, attr[0:1, :].partition_broadcast(P), "first_edge")
            weight(x3, x.rearrange("(b p) c -> p b c", p=P), "x_loaded")
            for k in range(2):
                weight(wring[:, 0, k, 0:F0], wft[k * P:(k + 1) * P, :], "w0_loaded")
                weight(wring[:, 0, k, ROW0:ROW0 + F0], wrt[k * P:(k + 1) * P, :], "w0_loaded")
            weight(wring[0:F0, 1, 0, 0:C], wf, "w0_loaded")
            weight(wring[0:F0, 1, 0, C:2 * C], wr, "w0_loaded")
            weight(wring[0:F0, 1, 1, 0:HEADS], attnt, "w0_loaded")
            sp.wait_ge(sem("fill"), 2)
            weight(slots_s_dram.rearrange("(p t) w -> p (t w)", p=P), slots_s[:, :], "gs_filled")
            sp.wait_ge(sem("fill_edge"), 1)
            weight(recs_d[OFF:OFF + P * TP, :].rearrange("(p t) w -> p (t w)", p=P), slots_d[:, :], "gd_filled")
            weight(recs_d[EP:OFF, :].rearrange("(p t) w -> p (t w)", p=P), slots_d[:, 0:(OFF - EP) // P * KD], "gd_filled")
            sp.wait_ge(sem("gd_records"), 1)
            weight(recs_d[0:EP, :].rearrange("(p f) w -> p (f w)", p=P), rec_d, "gd_recorded")
            table_store(sp, "d0", table0, 2 * ROW0, tab0, True)
            sp.wait_ge(sem("gd_done"), 1)
            weight(key_i, edges(src), "gs_loaded")
            weight(other_i, edges(dst), "gs_loaded")
            weight(etype_i, edges(etype), "gs_loaded")
            sp.wait_ge(sem("gd_filled"), 32)
            sp.wait_ge(sem("gd_recorded"), 16)
            sp.wait_ge(sem("gd_scattered"), 1)

            def records_load(n, h):
                after(sp, "row_numbers", groups0["e0"] + n - R + 1)
                _, starts = nc.values_load_multi_w_load_instructions(
                    tile_first[0:1, bass.ds(n * G, G)], engines=(mybir.EngineType.SP,), min_val=0, max_val=OFF + (T - 1) * P,
                    skip_runtime_bounds_check_because="128 * tile, less what blocks before fell short, or OFF more")
                for k in range(G):
                    sp.dma_start(slots_d[:, bass.ds((n * G + k) * KD, KD)], recs_d[bass.ds(starts[k], P), :])\
                        .then_inc(sem(f"records_loaded{h}"), 16)
            groups(sp, records_load)
            if layers > 1:
                sp.wait_ge(sem("e0_done"), 1)
                for k in range(2):
                    weight(wring[:, 0, k, 0:C], w_self[k * P:(k + 1) * P, :], "w1_loaded")
                    weight(wring[:, 0, k, C:2 * C], w_neigh[k * P:(k + 1) * P, :], "w1_loaded")
                table_store(sp, "d1", table1, C, tab1, False)
            if layers > 2:
                sp.wait_ge(sem("e1_done"), 1)
                for k in range(2):
                    weight(wring[:, 0, k, 0:C], loop_w[k * P:(k + 1) * P, :], "w2_loaded")
                weight(bias[:, 0, :], bias_self.rearrange("(a n) -> a n", a=1).partition_broadcast(P), "w2_loaded")
                sp.wait_ge(sem("d2_done"), 1)
                weight(bias[:, 1, :], bias_f.rearrange("(a n) -> a n", a=1).partition_broadcast(P), "pf_bias")
                rk = rel_f.rearrange("r (k p) c -> r k p c", p=P)

                def w_load(q, s):
                    for k in range(2):
                        for r in range(2):
                            sp.dma_start(wring[:, s, k, r * C:(r + 1) * C],
                                         rk[bass.ds(q * 2 + r, 1), k, :, :].rearrange("a p c -> p (a c)"))\
                                .then_inc(sem(f"pf_w{s}"), 16)

                w_load(0, 0)
                w_load(1, 1)

                def pairs(q, s, more):
                    for g in range(NB // 5):
                        after(sp, "pf_ev", NB * q + 5 * g + 5)
                        for r in range(2):
                            sp.dma_start(table2f[bass.ds((q * 2 + r) * NP + g * 5 * P, 5 * P), :]
                                         .rearrange("(j p) w -> p j w", p=P),
                                         projtab[:, (s * (NB // 5) + g) % 2, :, r * C:(r + 1) * C])\
                                .then_inc(sem(f"pf_stored{(s * (NB // 5) + g) % 2}"), 16)
                    if more:
                        after(sp, "pf_mm", NB * q + NB)
                        w_load(q + 2, s)
                with sp.Fori(0, RELS // 2 - 3, 2) as q0:
                    pairs(q0, 0, True)
                    pairs(q0 + 1, 1, True)
                pairs(RELS // 2 - 2, 0, False)
                pairs(RELS // 2 - 1, 1, False)
                sp.wait_ge(sem("pf_done"), 1)
                weight(bias[:, 1, :], bias_b.rearrange("(a n) -> a n", a=1).partition_broadcast(P), "pb_loaded")
                rk_b = rel_b.rearrange("r (k p) c -> k p r c", p=P)
                for q in range(PAIRS):
                    if q == 12 // 2:
                        slots_load(sp, "gs", slots_s_dram)
                    for k in range(2):
                        weight(rel_res[2 * q + k].rearrange("p (r c) -> p r c", r=2), rk_b[k, :, 2 * q:2 * q + 2, :], "pb_loaded")

                def pb_store(m, q):
                    after(sp, "pb_ev", m * PAIRS + q + 1)
                    sp.dma_start(table2b.rearrange("(r n) c -> n r c", n=NP)[bass.ds(m * P, P), 2 * q:2 * q + 2, :],
                                 pb_ring[:, q % 4, :].rearrange("p (r c) -> p r c", r=2)).then_inc(sem(f"pb_stored{q % 4}"), 16)
                for q in range(PAIRS):
                    pb_store(0, q)
                with sp.Fori(1, NB) as m:
                    for q in range(PAIRS):
                        pb_store(m, q)
            if layers > 3:
                sp.wait_ge(sem("e2_done"), 1)
                for k in range(2):
                    weight(wring[:, 0, k, 0:D], wp[k * P:(k + 1) * P, :], "w3_loaded")
                weight(bias[:, 0, 0:D], wp_b.rearrange("(a n) -> a n", a=1).partition_broadcast(P), "w3_loaded")
                weight(bias[:, 1, 0:D], w_pos.rearrange("(a n) -> a n", a=1).partition_broadcast(P), "w3_loaded")
                for s, e, qkv, table, sc, bi, before in (("da", "e3a", (q1, k1, v1), table3[0], ln1_s, ln1_b, "d3_done"),
                                                         ("db", "e3b", (q2, k2, v2), table3[1], ln2_s, ln2_b, "e3a_done")):
                    sp.wait_ge(sem(before), 1)
                    for i, w in enumerate(qkv):
                        weight(wring[:, 0, 0, i * D:(i + 1) * D], w, s + "_loaded")
                    weight(bias[:, 0, 0:D], sc.rearrange("(a n) -> a n", a=1).partition_broadcast(P), s + "_loaded")
                    weight(bias[:, 1, 0:D], bi.rearrange("(a n) -> a n", a=1).partition_broadcast(P), s + "_loaded")
                    table_store(sp, s, table, 2 * D, big1, True)
                sp.wait_ge(sem("e3b_done"), 1)
                weight(wring[:, 0, 0, 0:C], inv_w, "w4_loaded")
                weight(bias[:, 0, :], inv_b.rearrange("(a n) -> a n", a=1).partition_broadcast(P), "w4_loaded")
            sp.wait_ge(sem("x_done"), 1)
            full = N // P
            sp.dma_start(out[0:full * P, :].rearrange("(b p) c -> p b c", p=P), x3[:, 0:full, :]).then_inc(sem("out_stored"), 16)
            sp.dma_start(out[full * P:N, :], x_sb[0:N - full * P, full * C:(full + 1) * C]).then_inc(sem("out_stored"), 16)
            sp.wait_ge(sem("out_stored"), 32)

        @block_.gpsimd
        def _(pool):
            pool.iota(iota_i[:, :], [[1, P]], base=0, channel_multiplier=0).then_inc(sem("iota"), 1)
            pool.iota(iota_t_i, [[1, T]], base=0, channel_multiplier=0).then_inc(sem("iota"), 1)
            pool.memset(ident[:, :], 0.0).then_inc(sem("consts"), 1)
            pool.memset(tri[:, :], 1.0).then_inc(sem("consts"), 1)
            pool.memset(ones[:, :], 1.0).then_inc(sem("consts"), 1)
            pool.memset(slots_d[:, :], 0.0).then_inc(sem("consts"), 1)
            pool.memset(slots_s[:, :], 0.0).then_inc(sem("consts"), 1)
            pool.wait_ge(sem("consts"), 5)
            pool.affine_select(out=ident[:, :], in_=ident[:, :], compare_op=ALU.not_equal, fill=1.0, base=0,
                               pattern=[[-1, P]], channel_multiplier=1).then_inc(sem("consts"), 1)
            pool.affine_select(out=tri[:, :], in_=tri[:, :], compare_op=ALU.is_gt, fill=0.0, base=0,
                               pattern=[[1, P]], channel_multiplier=-1).then_inc(sem("consts"), 1)
            pool.memset(sd3[:, :, 2:3], -1.0).then_inc(sem("fill"), 1)
            pool.memset(ss3[:, :, 2:3], -1.0).then_inc(sem("fill"), 1)
            pool.wait_ge(sem("gd_known"), 1)
            scattering = nc.gpsimd.value_load(unsorted[0:1, 0:1])
            with pool.If(scattering != 0):
                pool.wait_ge(sem("gd_rows"), 1)
                pool.wait_ge(sem("gd_filled"), 32)
                scatter(pool, "gd", recs_d, rec_d, row_d, 0, NS)
                for h in range(2):
                    pool.wait_ge(sem(f"gd_placed{h}"), SC_EDGES * 8 * NS)
            pool.sem_inc(sem("gd_scattered"), 1)
            pool.wait_ge(sem("gs_keyed"), 1)
            pool.memset(acc[:, :], 0.0).then_inc(sem("acc_clear"), 1)
            pool.wait_ge(sem("d0_stored"), TABLE_STORED)
            gather_loop(pool, "e0", table0, 2 * ROW0)
            pool.wait_ge(sem("gs_rows"), 1)
            pool.wait_ge(sem("gs_filled"), 16)
            scatter(pool, "gs", slots_s_dram, rec_s, row_s, 0, NS_EARLY)
            pool.wait_ge(sem("e0_known"), 1)
            once_more = nc.gpsimd.value_load(again[0:1, 0:1])
            with pool.If(once_more != 0):
                gather_loop(pool, AGAIN, table0, 2 * ROW0)
            if layers > 1:
                pool.wait_ge(sem("d1_stored"), TABLE_STORED)
                gather_loop(pool, "e1", table1, C)
                pool.wait_ge(sem("gs_moved"), 1)
                pool.wait_ge(sem("gs_rows"), 2)
                scatter(pool, "gs", slots_s_dram, rec_s2, row_s2, NS_EARLY, NS)
            if layers > 2:
                for s in range(2):
                    pool.wait_ge(sem(f"pf_stored{s}"), 32 * PAIRS * (NB // 5) // 2)
                gather_loop(pool, "e2f", table2f, C)
                for s in range(4):
                    pool.wait_ge(sem(f"pb_stored{s}"), 16 * PAIRS * NB // 4)
                gather_loop(pool, "e2b", table2b, C)
            if layers > 3:
                for s, e, table in (("da", "e3a", table3[0]), ("db", "e3b", table3[1])):
                    pool.wait_ge(sem(s + "_stored"), TABLE_STORED)
                    gather_loop(pool, e, table, 2 * D)

        @block_.scalar
        def _(act):
            act.wait_ge(sem("w0_scores"), 1)
            for k in range(2):
                nc.scalar.activation(wring[:, 0, k, F0:ROW0], ps[:, 2, k * HEADS:(k + 1) * HEADS], ACT.Copy)
                last = nc.scalar.activation(wring[:, 0, k, ROW0 + F0:2 * ROW0], ps[:, 2, (2 + k) * HEADS:(3 + k) * HEADS], ACT.Copy)
            last.then_inc(sem("w0_done"), 1)
            act.wait_ge(sem("x_loaded"), 16)
            dense_act(act, "d0")
            e0_act(act, "e0")
            act.wait_ge(sem("e0_known"), 1)
            once_more = nc.scalar.value_load(again[0:1, 0:1])
            with act.If(once_more != 0):
                e0_act(act, AGAIN)
            act.wait_ge(sem("e0_under"), 1)
            nc.scalar.activation(eps0, under, ACT.Exp).then_inc(sem("e0_eps"), 1)
            norm_act(act, "n0")
            if layers > 1:
                act.wait_ge(sem("e0_done"), 1)
                dense_act(act, "d1")
                sum_act(act, "e1", slots_d, KD, 0)
                norm_act(act, "n1")
            if layers > 2:
                act.wait_ge(sem("e1_done"), 1)
                dense_act(act, "d2")

                def pb_xt(m, q):
                    if q == PAIRS // 2:
                        after(act, "pb_mm", m * PAIRS)
                        nc.scalar.activation(xts[:, 0, :].rearrange("p (k n) -> p k n", k=2), xt_all[:, :, bass.ds(m * P, P)],
                                             ACT.Copy).then_inc(sem("pb_xt"), 1)
                sum_act(act, "e2f", slots_d, KD, 1, lambda eng, body: groups_beside(eng, body, pb_xt))
                act.wait_ge(sem("gs_slots"), 16)
                sum_act(act, "e2b", slots_s, KS, 1)
                norm_act(act, "n2")
            if layers > 3:
                act.wait_ge(sem("e2_done"), 1)
                dense_act(act, "d3")
                for s, e, nm in (("da", "e3a", "n3a"), ("db", "e3b", "n3b")):
                    act.wait_ge(sem("d3_done" if s == "da" else "e3a_done"), 1)
                    dense_act(act, s)
                    att_act(act, e)
                    norm_act(act, nm)
                act.wait_ge(sem("e3b_done"), 1)
                dense_act(act, "d4")
                norm_act(act, "n4")

        @block_.vector
        def _(dve):
            chain = [0]

            def link(ins):
                chain[0] += 1
                ins.then_inc(sem("vector"), 1)
                dve.wait_ge(sem("vector"), chain[0])

            dve.wait_ge(sem("iota"), 2)
            link(nc.vector.tensor_copy(iota[:, :], iota_i[:, :]))
            dve.wait_ge(sem("consts"), 7)
            sort_keys(dve, "gd", link)
            dve.wait_ge(sem("fill"), 2)
            dve.wait_ge(sem("first_edge"), 32)
            link(nc.vector.tensor_copy(sd3[:, :, 0:1], bc(first_src.unsqueeze(1), [P, TP, 1])))
            link(nc.vector.tensor_copy(sd3[:, :, 3:5], bc(first_attr.unsqueeze(1), [P, TP, 2])))
            dve.sem_inc(sem("fill_edge"), 1)
            kbf = scratch["gd"][0]
            link(nc.vector.memset(falls[:, :], 0.0))
            link(nc.vector.tensor_scalar(next_i, next_i, 7, None, ALU.logical_shift_right))
            link(nc.vector.tensor_copy(next_f, next_i))
            link(nc.vector.tensor_tensor(falls[0:P - 1, 1:2], kbf[0:P - 1, EC - 1:EC], next_f, ALU.is_gt))
            link(nc.vector.tensor_tensor(prod[:, 0:EC - 1], kbf[:, 0:EC - 1], kbf[:, 1:EC], ALU.is_gt))
            link(nc.vector.tensor_reduce(falls[:, 0:1], prod[:, 0:EC - 1], AX.X, ALU.max))
            link(nc.vector.tensor_tensor(falls[:, 0:1], falls[:, 0:1], falls[:, 1:2], ALU.add))
            with dve.Fori(0, BINS) as b:
                count_bin(dve, "gd", b)
            dve.wait_ge(sem("gs_filled"), 16)
            link(nc.vector.tensor_copy(iota_t, iota_t_i))
            sort_tiles(dve, "gd", link)
            link(nc.vector.tensor_copy(unsorted[:, 0:1], ps[0:1, 0, FALLS:FALLS + 1]))
            link(nc.vector.tensor_scalar(in_order[:, 0:1], ps[0:1, 0, FALLS:FALLS + 1], 0.0, None, ALU.is_equal))
            first_f = tile_ge[0:1, :]
            for half in range(2):
                link(nc.vector.tensor_scalar(first_f[:, half * (T // 2):(half + 1) * (T // 2)], ps[0:1, 6 + half, 0:T // 2],
                                             float(-OFF), in_order[:, 0:1], ALU.add, ALU.mult))
            link(nc.vector.scalar_tensor_tensor(first_f, iota_t[0:1, :], float(P), first_f, ALU.mult, ALU.add))
            link(nc.vector.tensor_scalar(tile_first, first_f, float(OFF), None, ALU.add))
            dve.sem_inc(sem("gd_known"), 1)
            ranking = nc.vector.value_load(unsorted[0:1, 0:1])
            with dve.If(ranking != 0):
                with dve.Fori(0, BINS) as b:
                    rank_bin(dve, "gd", b, slice(0, EC), sem("gd_rank"))
                nc.vector.tensor_copy(row_d, scratch["gd"][3]).then_inc(sem("gd_rows"), 1)
                dve.wait_ge(sem("gd_rows"), 1)
            dve.sem_inc(sem("gd_done"), 1)
            both = attr_sb.rearrange("p (f w) -> p w f", w=2)
            link(nc.vector.tensor_reduce(small[:, 0:2], both, AX.X, ALU.max))
            link(nc.vector.tensor_reduce(small[:, 2:4], both, AX.X, ALU.min))
            link(nc.vector.tensor_scalar(small[:, 2:4], small[:, 2:4], -1.0, None, ALU.mult))
            all_max_dve(dve, "ranges", ranges, link)
            link(nc.vector.tensor_scalar(low, ranges, -1.0, None, ALU.mult))
            dve.wait_ge(sem("gd_recorded"), 16)
            dve.wait_ge(sem("gd_scattered"), 1)
            sort_keys(dve, "gs", link)
            dve.sem_inc(sem("gs_keyed"), 1)
            dve.wait_ge(sem("d0_sc"), NB)
            part = [small[:, 32 + 100 * w:32 + 100 * w + NB * HEADS].rearrange("p (b a) -> p b a", a=HEADS) for w in range(2)]
            for w in range(2):
                f_or_r = node_sc[:, :, w, :]
                link(nc.vector.tensor_scalar(part[w], f_or_r, ranges[:, w:w + 1], None, ALU.mult))
                link(nc.vector.scalar_tensor_tensor(part[w], f_or_r, low[:, 2 + w:3 + w], part[w], ALU.mult, ALU.max))
            link(nc.vector.tensor_tensor(part[0], part[0], part[1], ALU.add))
            link(nc.vector.tensor_reduce(small[:, 0:HEADS], part[0].rearrange("p b a -> p a b"), AX.X, ALU.max))
            link(nc.vector.scalar_tensor_tensor(small[:, 0:HEADS], small[:, 0:HEADS], 0.2, small[:, 0:HEADS], ALU.mult, ALU.max))
            all_max_dve(dve, "bound", shift, link)
            link(nc.vector.memset(max0[:, :], LOWEST))
            dve.wait_ge(sem("acc_clear"), 1)

            step, finish = e0_dve(dve, "e0")
            for n in range(R):
                step(n, n)
            with dve.Fori(0, NB) as b:
                for h in range(R):
                    step(b * R + (R + h), h)
                count_bin(dve, "gs", b)
            count_bin(dve, "gs", NB)
            sort_tiles(dve, "gs", link)
            with dve.Fori(0, NB) as b:
                for h in range(R):
                    step(b * R + ((NB + 1) * R + h), h)
                rank_bin(dve, "gs", b, EARLY, sem("gs_rank"))
            rank_bin(dve, "gs", NB, EARLY, sem("gs_rank"))
            link(nc.vector.tensor_tensor(base[:, 0:BINS], base[:, 0:BINS], cnt[:, 0:BINS], ALU.add))
            place_rows(dve, EARLY, row_s, link)
            for n in range((2 * NB + 1) * R, NG):
                step(n, n % R)
            finish()
            link(nc.vector.tensor_reduce(small[:, 0:HEADS], max0[:, :].rearrange("p (g a) -> p a g", a=HEADS), AX.X, ALU.max))
            all_max_dve(dve, "top", under, link)
            link(nc.vector.tensor_reduce(small[:, 8:9], under, AX.X, ALU.min))
            link(nc.vector.tensor_scalar(again[0:1, 0:1], small[0:1, 8:9], -FAR, None, ALU.is_lt))
            dve.sem_inc(sem("e0_known"), 1)
            once_more = nc.vector.value_load(again[0:1, 0:1])
            with dve.If(once_more != 0):
                nc.vector.memset(acc[:, :], 0.0).then_inc(sem("again_ready"), 1)
                nc.vector.tensor_tensor(shift, shift, under, ALU.add).then_inc(sem("again_ready"), 1)
                dve.wait_ge(sem("again_ready"), 2)
                nc.vector.memset(under, 0.0).then_inc(sem("again_ready"), 1)
                dve.wait_ge(sem("again_ready"), 3)
                step, finish = e0_dve(dve, AGAIN)
                groups(dve, step)
                finish()
            dve.sem_inc(sem("e0_under"), 1)
            a0 = acc[:, 0:NB * W0].rearrange("p (b w) -> p b w", w=W0)
            den = small[:, 128:128 + NB * HEADS].rearrange("p (b a) -> p b a", a=HEADS)
            dve.wait_ge(sem("e0_eps"), 1)
            link(nc.vector.tensor_scalar(eps0, eps0, 1e-10, None, ALU.mult))
            link(nc.vector.tensor_tensor(den, a0[:, :, HEADS * F0:W0], bc(eps0.unsqueeze(1), [P, NB, HEADS]), ALU.add))
            link(nc.vector.reciprocal(den, den))
            o0 = a0[:, :, 0:HEADS * F0]
            link(nc.vector.tensor_tensor(o0.rearrange("p b (a f) -> p b a f", f=F0), o0.rearrange("p b (a f) -> p b a f", f=F0),
                                         bc(den.unsqueeze(3), [P, NB, HEADS, F0]), ALU.mult))
            link(nc.vector.tensor_tensor(x3, x3, o0, ALU.add))
            norm_dve(dve, "n0", x3, C, 1e-5, link, big2)
            dve.sem_inc(sem("e0_done"), 1)
            deg = small[:, 128:128 + NB]

            if layers > 1:
                def d1(it):
                    for j in range(5):
                        i = 5 * it + j
                        hn = ps[:, 2 + j, C:2 * C]
                        x_b = x_sb[:, bass.ds(i * C, C)]
                        work = [msg[:, j * 512:j * 512 + C], msg[:, j * 512 + C:j * 512 + 2 * C]]
                        after(dve, "block_out", first["d1"] + i + 1)
                        nc.vector.tensor_tensor(x_b, x_b, ps[:, 2 + j, 0:C], ALU.add)
                        left = hn
                        for r in range(MAXK // 8):
                            nc.vector.max(top8[:, r, :], left).then_inc(sem("d1_top"), 1)
                            dve.wait_ge(sem("d1_top"), 8 * i + 2 * r + 1)
                            dve.nop(nofuse=True)
                            nc.vector.match_replace(work[r % 2], top8[:, r, :], left, LOWEST).then_inc(sem("d1_top"), 1)
                            dve.wait_ge(sem("d1_top"), 8 * i + 2 * r + 2)
                            dve.nop(nofuse=True)
                            left = work[r % 2]
                        if j == 0:
                            after(dve, "d1_stored", 16 * it)
                        nc.vector.scalar_tensor_tensor(tab1[:, j * C:(j + 1) * C], left, LOWEST, hn, ALU.is_equal, ALU.mult)\
                            .then_inc(sem("block_ev"), 1)
                blocks(dve, d1)
                dve.wait_ge(sem("block_ev"), first["d1"] + NB)
                nc.vector.tensor_copy(rec_s2, rec_s).then_inc(sem("gs_moved"), 1)
                nc.vector.memset(rows[:, :, C:C + 1], 1.0).then_inc(sem("ones_col"), 1)
                dve.wait_ge(sem("d1_stored"), TABLE_STORED)
                link(nc.vector.memset(acc[:, :], 0.0))

                def ranking(eng, body):
                    for n in range(R):
                        body(n, n)
                    with eng.Fori(0, NB) as b:
                        for h in range(R):
                            body(b * R + (R + h), h)
                        rank_bin(eng, "gs", b, LATE, sem("gs_rank_late"))
                    rank_bin(eng, "gs", NB, LATE, sem("gs_rank_late"))
                    place_rows(eng, LATE, row_s2, link)
                    with eng.Fori(NB + 1, 2 * NB + 1) as i:
                        for h in range(R):
                            body(i * R + h, h)
                    for n in range((2 * NB + 1) * R, NG):
                        body(n, n % R)
                sum_dve(dve, "e1", slots_d, KD, block_d, C + 1, ranking)
                dve.wait_ge(sem("tile_added"), tiles0["e1"] + T)
                a1 = acc[:, 0:NB * (C + 1)].rearrange("p (b w) -> p b w", w=C + 1)
                link(nc.vector.tensor_copy(deg.unsqueeze(2), a1[:, :, C:C + 1]))
                link(nc.vector.tensor_scalar(small[:, 160:160 + NB], deg, 1.0, None, ALU.max))
                link(nc.vector.reciprocal(small[:, 160:160 + NB], small[:, 160:160 + NB]))
                link(nc.vector.tensor_tensor(a1[:, :, 0:C], a1[:, :, 0:C], bc(small[:, 160:160 + NB].unsqueeze(2), [P, NB, C]), ALU.mult))
                link(nc.vector.tensor_tensor(x3, x3, a1[:, :, 0:C], ALU.add))
                dve.wait_ge(sem("gs_moved"), 1)
                for h in range(2):
                    dve.wait_ge(sem(f"gs_placed{h}"), SC_EDGES * 8 * NS_EARLY)
                norm_dve(dve, "n1", x3, C, 1e-5, link)
                dve.sem_inc(sem("e1_done"), 1)

            def mean_add(a, dg):
                link(nc.vector.tensor_scalar(small[:, 160:160 + NB], dg, 1.0, None, ALU.max))
                link(nc.vector.reciprocal(small[:, 160:160 + NB], small[:, 160:160 + NB]))
                link(nc.vector.tensor_tensor(a, a, bc(small[:, 160:160 + NB].unsqueeze(2), [P, NB, C]), ALU.mult))
                link(nc.vector.tensor_tensor(x3, x3, a, ALU.add))

            if layers > 2:
                dve.wait_ge(sem("w2_loaded"), 16 * 3)

                def d2(it):
                    for j in range(5):
                        i = 5 * it + j
                        x_b = x_sb[:, bass.ds(i * C, C)]
                        after(dve, "block_out", first["d2"] + i + 1)
                        nc.vector.tensor_copy(xt_all[:, :, bass.ds(i * P, P)], xts[:, j, :].rearrange("p (k n) -> p k n", k=2))\
                            .then_inc(sem("d2_xt_all"), 1)
                        nc.vector.scalar_tensor_tensor(tab[:, j * C:(j + 1) * C], ps[:, 2 + j, 0:C], 2.0, bias[:, 0, :],
                                                       ALU.mult, ALU.add).then_inc(sem("d2_s"), 1)
                        after(dve, "d2_s", i + 1)
                        nc.vector.tensor_tensor(x_b, x_b, tab[:, j * C:(j + 1) * C], ALU.add).then_inc(sem("block_ev"), 1)
                blocks(dve, d2)
                dve.wait_ge(sem("d2_xt_all"), NB)
                dve.wait_ge(sem("block_ev"), first["d2"] + NB)
                dve.sem_inc(sem("d2_done"), 1)
                dve.wait_ge(sem("pf_bias"), 16)

                def pairs(q, s):
                    for m in range(NB):
                        g = m // 5
                        slot = (s * (NB // 5) + g) % 2
                        after(dve, "pf_mm", NB * q + m + 1)
                        if m % 5 == 0:
                            if isinstance(q, int):
                                after(dve, f"pf_stored{slot}", 32 * ((q * (NB // 5) + g) // 2))
                            else:
                                after(dve, f"pf_stored{slot}", (q - s) * (16 * (NB // 5)) + 32 * ((s * (NB // 5) + g) // 2))
                        nc.vector.tensor_tensor(
                            projtab[:, slot, m % 5, :].rearrange("p (r c) -> p r c", r=2),
                            ps[:, m % 5, :].rearrange("p (r c) -> p r c", r=2),
                            bc(bias[:, 1, :].unsqueeze(1), [P, 2, C]), ALU.add).then_inc(sem("pf_ev"), 1)
                pairs(0, 0)
                pairs(1, 1)
                with dve.Fori(2, PAIRS - 1, 2) as q0:
                    pairs(q0, 0)
                    pairs(q0 + 1, 1)
                dve.wait_ge(sem("pf_ev"), NB * PAIRS)
                for s in range(2):
                    dve.wait_ge(sem(f"pf_stored{s}"), 32 * PAIRS * (NB // 5) // 2)
                dve.sem_inc(sem("pf_done"), 1)
                link(nc.vector.memset(acc[:, :], 0.0))

                def pb_out(m, q):
                    after(dve, "pb_mm", m * PAIRS + q + 1)
                    after(dve, f"pb_stored{q % 4}", m * (16 * PAIRS // 4) + 16 * (q // 4))
                    nc.vector.tensor_tensor(
                        pb_ring[:, q % 4, :].rearrange("p (r c) -> p r c", r=2),
                        ps[:, 4 + q % 4, :].rearrange("p (r c) -> p r c", r=2),
                        bc(bias[:, 1, :].unsqueeze(1), [P, 2, C]), ALU.add).then_inc(sem("pb_ev"), 1)

                def pb_before(m, q):
                    if isinstance(m, int) and m == 0 and q == 0:
                        return
                    pb_out(*((m, q - 1) if q else (m - 1, PAIRS - 1)))
                sum_dve(dve, "e2f", slots_d, KD, block_d, C, lambda eng, body: groups_beside(eng, body, pb_before))
                pb_out(NB - 1, PAIRS - 1)
                dve.wait_ge(sem("tile_added"), tiles0["e2f"] + T)
                mean_add(acc[:, 0:NB * C].rearrange("p (b w) -> p b w", w=C), deg)
                link(nc.vector.memset(acc[:, :], 0.0))
                dve.wait_ge(sem("gs_slots"), 16)
                dve.sem_inc(sem("e2f_done"), 1)
                sum_dve(dve, "e2b", slots_s, KS, block_s, C + 1)
                dve.wait_ge(sem("tile_added"), tiles0["e2b"] + T)
                a2 = acc[:, 0:NB * (C + 1)].rearrange("p (b w) -> p b w", w=C + 1)
                link(nc.vector.tensor_copy(deg.unsqueeze(2), a2[:, :, C:C + 1]))
                mean_add(a2[:, :, 0:C], deg)
                norm_dve(dve, "n2", x3, C, 1e-5, link)
                dve.sem_inc(sem("e2_done"), 1)

            if layers > 3:
                emb3 = emb.rearrange("p (b d) -> p b d", d=D)
                dve.wait_ge(sem("w3_loaded"), 16 * 4)
                link(nc.vector.tensor_tensor(bias[:, 0, 0:D], bias[:, 0, 0:D], bias[:, 1, 0:D], ALU.add))

                def d3(it):
                    for j in range(5):
                        after(dve, "block_out", first["d3"] + 5 * it + j + 1)
                        nc.vector.tensor_tensor(emb[:, bass.ds((5 * it + j) * D, D)], ps[:, 2 + j, 0:D], bias[:, 0, 0:D],
                                                ALU.add).then_inc(sem("block_ev"), 1)
                blocks(dve, d3)
                dve.wait_ge(sem("block_ev"), first["d3"] + NB)
                dve.sem_inc(sem("d3_done"), 1)
                for s, e, nm in (("da", "e3a", "n3a"), ("db", "e3b", "n3b")):
                    dve.wait_ge(sem(s + "_loaded"), 16 * 5)

                    def qkv(it):
                        for j in range(5):
                            after(dve, "block_out", first[s] + 5 * it + j + 1)
                            nc.vector.tensor_copy(q_sb[:, bass.ds((5 * it + j) * D, D)], ps[:, 2 + j, 0:D])\
                                .then_inc(sem(s + "_q"), 1)
                            nc.vector.tensor_copy(big1[:, bass.ds((5 * it + j) * (2 * D), 2 * D)], ps[:, 2 + j, D:3 * D])\
                                .then_inc(sem("block_ev"), 1)
                    blocks(dve, qkv)
                    dve.wait_ge(sem(s + "_q"), NB)
                    link(nc.vector.memset(acc[:, 0:NB * W3], 0.0))
                    att_dve(dve, e)
                    dve.wait_ge(sem("tile_added"), tiles0[e] + T)
                    a3 = acc[:, 0:NB * W3].rearrange("p (b w) -> p b w", w=W3)
                    den3 = small[:, 104:104 + NB * H3].rearrange("p (b a) -> p b a", a=H3)
                    link(nc.vector.tensor_scalar(den3, a3[:, :, D:W3], 1e-8, None, ALU.add))
                    link(nc.vector.reciprocal(den3, den3))
                    agg = a3[:, :, 0:D].rearrange("p b (a d) -> p b a d", d=HD)
                    link(nc.vector.tensor_tensor(agg, agg, bc(den3.unsqueeze(3), [P, NB, H3, HD]), ALU.mult))
                    link(nc.vector.tensor_tensor(emb3, emb3, a3[:, :, 0:D], ALU.add))
                    norm_dve(dve, nm, emb3, D, 1e-6, link)
                    link(nc.vector.tensor_tensor(emb3, emb3, bc(bias[:, 0, 0:D].unsqueeze(1), [P, NB, D]), ALU.mult))
                    link(nc.vector.tensor_tensor(emb3, emb3, bc(bias[:, 1, 0:D].unsqueeze(1), [P, NB, D]), ALU.add))
                    dve.sem_inc(sem(e + "_done"), 1)
                dve.wait_ge(sem("w4_loaded"), 32)

                def d4(it):
                    for j in range(5):
                        i = 5 * it + j
                        x_b = x_sb[:, bass.ds(i * C, C)]
                        after(dve, "block_out", first["d4"] + i + 1)
                        nc.vector.tensor_tensor(tab[:, j * C:(j + 1) * C], ps[:, 2 + j, 0:C], bias[:, 0, :], ALU.add)\
                            .then_inc(sem("d4_s"), 1)
                        after(dve, "d4_s", i + 1)
                        nc.vector.tensor_tensor(x_b, x_b, tab[:, j * C:(j + 1) * C], ALU.add).then_inc(sem("block_ev"), 1)
                blocks(dve, d4)
                dve.wait_ge(sem("block_ev"), first["d4"] + NB)
                norm_dve(dve, "n4", x3, C, 1e-5, link)
            dve.sem_inc(sem("x_done"), 1)

        @block_.tensor
        def _(pe):
            pe.wait_ge(sem("consts"), 7)
            pe.wait_ge(sem("w0_loaded"), 16 * 7)
            for d in range(2):
                for k in range(2):
                    last = nc.tensor.matmul(ps[:, 2, (2 * d + k) * HEADS:(2 * d + k + 1) * HEADS],
                                            wring[0:F0, 1, 0, d * C + k * P:d * C + (k + 1) * P],
                                            wring[0:F0, 1, 1, 0:HEADS], start=True, stop=True)
            last.then_inc(sem("w0_scores"), 1)
            pe.wait_ge(sem("w0_done"), 1)
            dense_pe(pe, "d0", wring[:, 0, :, :])
            pe.wait_ge(sem("block_ev"), first["d0"] + NB)
            sort_pe(pe, "gd")
            all_max_pe(pe, "ranges")
            all_max_pe(pe, "bound")
            body = e0_sums(pe, "e0")
            for n in range(R):
                body(n, n)
            with pe.Fori(1, NB) as i:
                for h in range(R):
                    body(i * R + h, h)
            half = NB * R
            body(half, 0)
            body(half + 1, 1)
            sort_pe(pe, "gs")
            body(half + 2, 2)
            body(half + 3, 3)
            with pe.Fori(NB + 1, 2 * NB + 1) as i:
                for h in range(R):
                    body(i * R + h, h)
            for n in range((2 * NB + 1) * R, NG):
                body(n, n % R)
            all_max_pe(pe, "top")
            pe.wait_ge(sem("e0_known"), 1)
            once_more = nc.tensor.value_load(again[0:1, 0:1])
            with pe.If(once_more != 0):
                groups(pe, e0_sums(pe, AGAIN))
            if layers > 1:
                pe.wait_ge(sem("w1_loaded"), 16 * 4)
                dense_pe(pe, "d1", wring[:, 0, :, :])
                pe.wait_ge(sem("ones_col"), 1)
                sum_pe(pe, "e1", C + 1)
            if layers > 2:
                pe.wait_ge(sem("w2_loaded"), 16 * 3)
                dense_pe(pe, "d2", wring[:, 0, :, :])
                pe.wait_ge(sem("d2_done"), 1)

                def pairs(q, s):
                    after(pe, f"pf_w{s}", 32 * (q - s) + 64)
                    for m in range(NB):
                        after(pe, "pf_ev", NB * q + m - 4)
                        for k in range(2):
                            last = nc.tensor.matmul(ps[:, m % 5, :], xt_all[:, k, m * P:(m + 1) * P],
                                                    wring[:, s, k, :], start=(k == 0), stop=(k == 1))
                        last.then_inc(sem("pf_mm"), 1)
                pairs(0, 0)
                pairs(1, 1)
                with pe.Fori(2, PAIRS - 1, 2) as q0:
                    pairs(q0, 0)
                    pairs(q0 + 1, 1)
                pe.wait_ge(sem("pf_ev"), NB * PAIRS)

                def pb(m, q):
                    if isinstance(m, int) and m == 0 and q == 0:
                        pe.wait_ge(sem("pb_loaded"), 16 * (1 + 2 * PAIRS))
                    if q == 0:
                        after(pe, "pb_xt", m + 1)
                    after(pe, "pb_ev", m * PAIRS + q - 3)
                    for k in range(2):
                        last = nc.tensor.matmul(ps[:, 4 + q % 4, :], xts[:, 0, k * P:(k + 1) * P], rel_res[2 * q + k],
                                                start=(k == 0), stop=(k == 1))
                    last.then_inc(sem("pb_mm"), 1)
                sum_pe(pe, "e2f", C, lambda eng, body: groups_beside(eng, body, pb))
                pe.wait_ge(sem("e2f_done"), 1)
                sum_pe(pe, "e2b", C + 1)
            if layers > 3:
                pe.wait_ge(sem("w3_loaded"), 16 * 4)
                dense_pe(pe, "d3", wring[:, 0, :, :])
                for s, e in (("da", "e3a"), ("db", "e3b")):
                    pe.wait_ge(sem(s + "_loaded"), 16 * 5)
                    dense_pe(pe, s, wring[:, 0, :, :])
                    pe.wait_ge(sem(s + "_q"), NB)
                    att_pe(pe, e)
                pe.wait_ge(sem("w4_loaded"), 32)
                dense_pe(pe, "d4", wring[:, 0, :, :])


def kernel(x, src, dst, edge_attr_2, edge_type_16, L0_gnn_W_forward, L0_gnn_W_reverse, L0_gnn_attn_forward,
           L1_gnn_W_self, L1_gnn_W_neigh, L2_gnn_Wf, L2_gnn_Wb, L2_gnn_loop_weight, L2_gnn_forward_bias,
           L2_gnn_backward_bias, L2_gnn_self_bias, L3_gnn_W_P_w, L3_gnn_W_P_b, L3_gnn_W_pos, L3_gnn_q1, L3_gnn_k1,
           L3_gnn_v1, L3_gnn_ln1_s, L3_gnn_ln1_b, L3_gnn_q2, L3_gnn_k2, L3_gnn_v2, L3_gnn_ln2_s, L3_gnn_ln2_b,
           L3_gnn_inv_w, L3_gnn_inv_b):
    import numpy as np
    import concourse.bacc as bacc
    from concourse import mybir
    from concourse.bass_utils import run_bass_kernel_spmd

    arrays = host_arrays(x, src, dst, edge_attr_2, edge_type_16, L0_gnn_W_forward, L0_gnn_W_reverse, L0_gnn_attn_forward,
                         L1_gnn_W_self, L1_gnn_W_neigh, L2_gnn_Wf, L2_gnn_Wb, L2_gnn_loop_weight, L2_gnn_forward_bias,
                         L2_gnn_backward_bias, L2_gnn_self_bias, L3_gnn_W_P_w, L3_gnn_W_P_b, L3_gnn_W_pos, L3_gnn_q1,
                         L3_gnn_k1, L3_gnn_v1, L3_gnn_ln1_s, L3_gnn_ln1_b, L3_gnn_q2, L3_gnn_k2, L3_gnn_v2, L3_gnn_ln2_s,
                         L3_gnn_ln2_b, L3_gnn_inv_w, L3_gnn_inv_b)
    nc = bacc.Bacc("TRN2", target_bir_lowering=False, num_devices=1)
    named = {f"in_{name}": a for name, a in arrays.items()}
    ins = {name: nc.dram_tensor(f"in_{name}", a.shape, mybir.dt.from_np(a.dtype), kind="ExternalInput").ap()
           for name, a in arrays.items()}
    out = nc.dram_tensor("out_0", (3125, 256), mybir.dt.float32, kind="ExternalOutput").ap()
    gnn_program(nc, **ins, out=out)
    r = run_bass_kernel_spmd(nc, [named], core_ids=[0])
    return r.results[0]["out_0"]


def host_arrays(x, src, dst, attr, etype, wf, wr, attn, w_self, w_neigh, rel_f, rel_b, loop_w, bias_f, bias_b, bias_self,
                wp, wp_b, w_pos, q1, k1, v1, ln1_s, ln1_b, q2, k2, v2, ln2_s, ln2_b, inv_w, inv_b):
    import numpy as np

    def tail(a, n, value):
        a = np.asarray(a)
        return np.concatenate([a, np.full((n,) + a.shape[1:], value, a.dtype)])

    nodes, edges = np.asarray(x).shape[0], np.asarray(src).shape[0]
    more_n, more_e = -nodes % 128, -edges % (128 * 26)
    padded = nodes + more_n
    arrays = dict(x=tail(x, more_n, 0), src=tail(src, more_e, padded), dst=tail(dst, more_e, padded),
                  src_real=tail(src, more_e, np.asarray(src)[-1]), etype=tail(etype, more_e, 0),
                  attr=tail(attr, more_e, np.asarray(attr)[-1]), wf=wf, wr=wr,
                  wft=np.transpose(np.asarray(wf)), wrt=np.transpose(np.asarray(wr)),
                  attnt=np.transpose(np.asarray(attn)[0]), w_self=w_self, w_neigh=w_neigh, rel_f=rel_f, rel_b=rel_b,
                  loop_w=loop_w, bias_f=bias_f, bias_b=bias_b, bias_self=bias_self, wp=wp, wp_b=wp_b,
                  w_pos=np.asarray(w_pos).reshape(-1), q1=q1, k1=k1, v1=v1, ln1_s=ln1_s, ln1_b=ln1_b, q2=q2, k2=k2, v2=v2,
                  ln2_s=ln2_s, ln2_b=ln2_b, inv_w=inv_w, inv_b=inv_b)
    return {name: np.ascontiguousarray(a) for name, a in arrays.items()}
```
